# Optimizing a Trainium2 kernel written in Bass

```python
import numpy as np
import jax
import jax.numpy as jnp

def _softmax(x, axis=-1):
    return jax.nn.softmax(x, axis=axis)

def _gelu(x):
    return jax.nn.gelu(x, approximate=True)

def _silu(x):
    return jax.nn.silu(x)

def _sigmoid(x):
    return jax.nn.sigmoid(x)

def _layernorm(x, axis=-1, eps=1e-05):
    m = jnp.mean(x, axis=axis, keepdims=True)
    v = jnp.var(x, axis=axis, keepdims=True)
    return (x - m) / jnp.sqrt(v + eps)

def _scatter_add(tgt, idx, src, axis=0):
    return tgt.at[idx].add(src)

def _segment_sum(src, seg, n):
    return jax.ops.segment_sum(src, seg, n)
kernel_name = 'mk_decoder_postln_d1_seqx_r8_eb2bc0'

def setup_inputs(seed: int=0):
    np.random.seed(seed)
    _w = jnp.asarray

    def _rec_inputs():
        import jax
        import jax.numpy as jnp
        _rk = jax.random.key(seed)
        x = -0.0005207 + 1.001 * jax.random.normal(jax.random.fold_in(_rk, 1), (2, 256, 512), jnp.float32)
        _lenS = 256 - jax.random.randint(jax.random.fold_in(_rk, 7), (2,), 0, max(1, 256 // 4) + 1, jnp.int32)
        _lenS2 = 512 - jax.random.randint(jax.random.fold_in(_rk, 8), (2,), 0, max(1, 512 // 4) + 1, jnp.int32)
        _ctx_4096P = jax.random.normal(jax.random.fold_in(_rk, 11), (2, 16, 512), jnp.float32)
        _ctx_4096c = jax.random.dirichlet(jax.random.fold_in(_rk, 511), 0.3 * jnp.ones((16,), jnp.float32), (2, 512))
        _ctx_4096t = jnp.einsum('bsk,bkd->bsd', _ctx_4096c, _ctx_4096P)
        _ctx_4096t = _ctx_4096t * jax.lax.rsqrt(jnp.mean(jnp.square(_ctx_4096t)) + 1e-12) * 0.953939
        ctx_4096 = -0.00010331 + 0.999899 * (_ctx_4096t + 0.3 * jax.random.normal(jax.random.fold_in(_rk, 611), (2, 512, 512), jnp.float32))
        return (x, ctx_4096)
    x, ctx_4096 = _rec_inputs()

    def _L0_attn_setup():
        import jax, jax.numpy as jnp
        import numpy as np
        import math
        HIDDEN = 512
        NUM_HEADS = 32
        HEAD_DIM = HIDDEN // NUM_HEADS
        SCALE = 1.0 / HEAD_DIM

        def _alibi_slopes(n_heads: int) -> np.ndarray:
            cp2 = 2 ** math.floor(math.log2(n_heads))
            base = 2 ** (-2 ** (-(math.log2(cp2) - 3)))
            slopes = base ** np.arange(1, cp2 + 1, dtype=np.float32)
            if cp2 != n_heads:
                extra_base = 2 ** (-2 ** (-(math.log2(2 * cp2) - 3)))
                n_rem = min(cp2, n_heads - cp2)
                extra = extra_base ** np.arange(1, 1 + 2 * n_rem, 2, dtype=np.float32)
                slopes = np.concatenate([slopes, extra])
            return slopes.astype(np.float32)
        key = jax.random.key(seed)
        k1, k2, k3, k4, k5 = jax.random.split(key, 5)
        B, S = (2, 256)
        return {'hidden_states': jax.random.normal(k1, (B, S, HIDDEN), dtype=jnp.float32), 'w_attn': jax.random.normal(k2, (HIDDEN, 3 * HIDDEN), dtype=jnp.float32) * 0.02, 'b_attn': jnp.zeros((3 * HIDDEN,), dtype=jnp.float32), 'w_proj': jax.random.normal(k3, (HIDDEN, HIDDEN), dtype=jnp.float32) * 0.02, 'b_proj': jnp.zeros((HIDDEN,), dtype=jnp.float32)}
    _L0_attn_all = _L0_attn_setup()
    _L0_attn_in = {k: v for k, v in _L0_attn_all.items() if k in ('w_attn', 'b_attn', 'w_proj', 'b_proj')}
    del _L0_attn_all

    def _L0_xattn_setup():
        import jax, jax.numpy as jnp
        import numpy as np
        HEADS = 32
        KV_HEADS = 8
        HEAD_DIM = 128
        EPS = 1e-06

        def rms_norm(x, w):
            var = jnp.mean(jnp.square(x.astype(jnp.float32)), axis=-1, keepdims=True)
            return (x.astype(jnp.float32) * jax.lax.rsqrt(var + EPS)).astype(x.dtype) * w
        key = jax.random.key(seed)
        ks = jax.random.split(key, 6)
        bsz, n_lat, seq, hidden = (8, 64, 512, 512)
        return {'latents': jax.random.normal(ks[0], (bsz, n_lat, hidden), jnp.float32), 'context': jax.random.normal(ks[1], (bsz, seq, hidden), jnp.float32), 'Wq': jax.random.normal(ks[2], (hidden, HEADS * HEAD_DIM), jnp.float32) * 0.02, 'Wk': jax.random.normal(ks[3], (hidden, KV_HEADS * HEAD_DIM), jnp.float32) * 0.02, 'Wv': jax.random.normal(ks[4], (hidden, KV_HEADS * HEAD_DIM), jnp.float32) * 0.02, 'Wo': jax.random.normal(ks[5], (HEADS * HEAD_DIM, hidden), jnp.float32) * 0.02, 'q_norm_w': jnp.ones((HEAD_DIM,), jnp.float32), 'k_norm_w': jnp.ones((HEAD_DIM,), jnp.float32)}
    _L0_xattn_all = _L0_xattn_setup()
    _L0_xattn_in = {k: v for k, v in _L0_xattn_all.items() if k in ('Wq', 'Wk', 'Wv', 'Wo', 'q_norm_w', 'k_norm_w')}
    del _L0_xattn_all

    def _L0_ffn_setup():
        import jax, jax.numpy as jnp
        import numpy as np
        B, L, H, Dh, M = (4, 256, 16, 32, 128)
        D = H * Dh
        key = jax.random.key(seed)
        kx, ku, kd, kp = jax.random.split(key, 4)
        x = jax.random.normal(kx, (B, L, D), dtype=jnp.float32)
        up = jax.random.normal(ku, (H, Dh, M), dtype=jnp.float32)
        down = jax.random.normal(kd, (H, M, Dh), dtype=jnp.float32)
        perm = jax.random.permutation(kp, D)
        return {'x': x, 'up': up, 'down': down, 'perm': perm}
    _L0_ffn_all = _L0_ffn_setup()
    _L0_ffn_in = {k: v for k, v in _L0_ffn_all.items() if k in ('up', 'down', 'perm')}
    del _L0_ffn_all
    return {'x': x, 'ctx_4096': ctx_4096, 'L0_attn_w_attn': _L0_attn_in['w_attn'], 'L0_attn_b_attn': _L0_attn_in['b_attn'], 'L0_attn_w_proj': _L0_attn_in['w_proj'], 'L0_attn_b_proj': _L0_attn_in['b_proj'], 'L0_xattn_Wq': _L0_xattn_in['Wq'], 'L0_xattn_Wk': _L0_xattn_in['Wk'], 'L0_xattn_Wv': _L0_xattn_in['Wv'], 'L0_xattn_Wo': _L0_xattn_in['Wo'], 'L0_xattn_q_norm_w': _L0_xattn_in['q_norm_w'], 'L0_xattn_k_norm_w': _L0_xattn_in['k_norm_w'], 'L0_ffn_up': _L0_ffn_in['up'], 'L0_ffn_down': _L0_ffn_in['down'], 'L0_ffn_perm': _L0_ffn_in['perm']}

def reference(x, ctx_4096, L0_attn_w_attn, L0_attn_b_attn, L0_attn_w_proj, L0_attn_b_proj, L0_xattn_Wq, L0_xattn_Wk, L0_xattn_Wv, L0_xattn_Wo, L0_xattn_q_norm_w, L0_xattn_k_norm_w, L0_ffn_up, L0_ffn_down, L0_ffn_perm):
    import jax
    import jax.numpy as jnp

    def _L0_attn_ref(hidden_states, w_attn, b_attn, w_proj, b_proj):
        import jax, jax.numpy as jnp
        import numpy as np
        import math
        HIDDEN = 512
        NUM_HEADS = 32
        HEAD_DIM = HIDDEN // NUM_HEADS
        SCALE = 1.0 / HEAD_DIM

        def _alibi_slopes(n_heads: int) -> np.ndarray:
            cp2 = 2 ** math.floor(math.log2(n_heads))
            base = 2 ** (-2 ** (-(math.log2(cp2) - 3)))
            slopes = base ** np.arange(1, cp2 + 1, dtype=np.float32)
            if cp2 != n_heads:
                extra_base = 2 ** (-2 ** (-(math.log2(2 * cp2) - 3)))
                n_rem = min(cp2, n_heads - cp2)
                extra = extra_base ** np.arange(1, 1 + 2 * n_rem, 2, dtype=np.float32)
                slopes = np.concatenate([slopes, extra])
            return slopes.astype(np.float32)
        B, S, _ = hidden_states.shape
        H, D = (NUM_HEADS, HEAD_DIM)
        qkv = hidden_states @ w_attn + b_attn
        q, k, v = jnp.split(qkv, 3, axis=-1)
        q = q.reshape(B, S, H, D)
        k = k.reshape(B, S, H, D)
        v = v.reshape(B, S, H, D)
        scores = jnp.einsum('bqhd,bkhd->bhqk', q, k) * SCALE
        slopes = jnp.asarray(_alibi_slopes(H))
        pos = jnp.arange(S)
        rel = pos[None, :] - pos[:, None]
        bias = slopes[:, None, None] * rel[None, :, :]
        causal = rel <= 0
        scores = jnp.where(causal[None, None], scores + bias[None], -jnp.inf)
        attn = jax.nn.softmax(scores, axis=-1)
        out = jnp.einsum('bhqk,bkhd->bqhd', attn, v).reshape(B, S, HIDDEN)
        return out @ w_proj + b_proj

    def _L0_xattn_ref(latents, context, Wq, Wk, Wv, Wo, q_norm_w, k_norm_w):
        import jax, jax.numpy as jnp
        import numpy as np
        HEADS = 32
        KV_HEADS = 8
        HEAD_DIM = 128
        EPS = 1e-06

        def rms_norm(x, w):
            var = jnp.mean(jnp.square(x.astype(jnp.float32)), axis=-1, keepdims=True)
            return (x.astype(jnp.float32) * jax.lax.rsqrt(var + EPS)).astype(x.dtype) * w
        bsz, q_len, hidden = latents.shape
        kv = jnp.concatenate([context, latents], axis=1)
        kv_len = kv.shape[1]
        groups = HEADS // KV_HEADS
        q = (latents @ Wq).reshape(bsz, q_len, HEADS, HEAD_DIM).transpose(0, 2, 1, 3)
        k = (kv @ Wk).reshape(bsz, kv_len, KV_HEADS, HEAD_DIM).transpose(0, 2, 1, 3)
        v = (kv @ Wv).reshape(bsz, kv_len, KV_HEADS, HEAD_DIM).transpose(0, 2, 1, 3)
        q = rms_norm(q, q_norm_w)
        k = rms_norm(k, k_norm_w)
        qg = q.reshape(bsz, KV_HEADS, groups, q_len, HEAD_DIM)
        scale = 1.0 / np.sqrt(HEAD_DIM)
        scores = jnp.einsum('bhgqd,bhkd->bhgqk', qg, k) * scale
        probs = jax.nn.softmax(scores.astype(jnp.float32), axis=-1).astype(q.dtype)
        out = jnp.einsum('bhgqk,bhkd->bhgqd', probs, v)
        out = out.reshape(bsz, HEADS, q_len, HEAD_DIM).transpose(0, 2, 1, 3)
        out = out.reshape(bsz, q_len, HEADS * HEAD_DIM)
        return out @ Wo

    def _L0_ffn_ref(x, up, down, perm):
        import jax, jax.numpy as jnp
        import numpy as np
        B, L, H, Dh, M = (4, 256, 16, 32, 128)
        D = H * Dh
        b, l, Dm = x.shape
        h, d = (up.shape[0], up.shape[1])
        unperm = jnp.argsort(perm)
        t = x.reshape(b * l, Dm)
        t = t[:, perm]
        t = t.reshape(b * l, h, d)
        t = jnp.einsum('bhd,hdm->bhm', t, up)
        t = jax.nn.gelu(t, approximate=False)
        t = jnp.einsum('bhm,hmd->bhd', t, down)
        t = t.reshape(b * l, h * d)
        t = t[:, unperm]
        out = t.reshape(b, l, Dm)
        return out
    x = _layernorm(x + _L0_attn_ref(x, L0_attn_w_attn, L0_attn_b_attn, L0_attn_w_proj, L0_attn_b_proj), axis=-1)
    x = _layernorm(x + _L0_xattn_ref(x, ctx_4096, L0_xattn_Wq, L0_xattn_Wk, L0_xattn_Wv, L0_xattn_Wo, L0_xattn_q_norm_w, L0_xattn_k_norm_w), axis=-1)
    x = _layernorm(x + _L0_ffn_ref(x, L0_ffn_up, L0_ffn_down, L0_ffn_perm), axis=-1)
    return x

_drawn_inputs = setup_inputs


def setup_inputs(seed=0):
    import zlib

    import numpy as np

    out = dict(_drawn_inputs(seed))
    spreads = {'L0_attn_b_attn': (0.0, 0.1),
     'L0_attn_b_proj': (0.0, 0.1),
     'L0_xattn_q_norm_w': (1.0, 0.6),
     'L0_xattn_k_norm_w': (1.0, 0.6)}
    factors = {}
    for name, (base, spread) in spreads.items():
        noise = np.random.default_rng([zlib.crc32(name.encode()), seed]).standard_normal(out[name].shape)
        drawn = base * np.exp(spread * noise) if base else spread * noise
        out[name] = jnp.asarray(drawn.astype(out[name].dtype))
    for name, factor in factors.items():
        out[name] = (out[name] * factor).astype(out[name].dtype)
    return out
```

```python
from contextlib import ExitStack

import concourse.bass as bass
from concourse import mybir

P = 128
ALU = mybir.AluOpType
ACT = mybir.ActivationFunctionType
AX = mybir.AxisListType
F32 = mybir.dt.float32
F32R = mybir.dt.float32r
I32 = mybir.dt.int32

B, S, D = 2, 256, 512
TOK = B * S
TT = TOK // P
KT = D // P
C = 512
CT = C // P
LN_EPS = 1e-5

SA_HEADS, SA_DIM = 32, 16
SA_SCALE = 1.0 / SA_DIM
SLOPES = [2.0 ** (-(h + 1) / 4) for h in range(SA_HEADS)]
MASKED = -1e36

XH, KVH, HD = 32, 8, 128
GRP = XH // KVH
KEYS = C + S
KTL = KEYS // P
HALF = KEYS // 2
X_SCALE = float(HD) ** -0.5
RMS_EPS = 1e-6

FH, FD, FM = 16, 32, 128
HPT = P // FD


def three_passes(nc, out, a_hi, a_lo, b_hi, b_lo, first, last):
    nc.tensor.matmul(out, a_hi, b_hi, start=first, stop=False)
    nc.tensor.matmul(out, a_hi, b_lo, start=False, stop=False)
    return nc.tensor.matmul(out, a_lo, b_hi, start=False, stop=last)


def f32(ap):
    return ap.bitcast(F32)


class Tensors:

    def __init__(self, nc, ctx):
        self.nc, self.ctx = nc, ctx

    def sb(self, name, shape, dt=F32):
        return self.ctx.enter_context(self.nc.sbuf_tensor(name, shape, dt))

    def sem(self, name):
        return self.ctx.enter_context(self.nc.semaphore(name))


def self_attention(nc, d, k):
    with ExitStack() as ctx:
        t = Tensors(nc, ctx)
        xT_hi = t.sb("xT_hi", [P, KT, TOK], F32R)
        xT_lo = t.sb("xT_lo", [P, KT, TOK], F32R)
        wa_raw = t.sb("wa_raw", [P, 2, 3 * D])
        wa_hi = t.sb("wa_hi", [P, KT, 3 * D], F32R)
        wa_lo = t.sb("wa_lo", [P, KT, 3 * D], F32R)
        wp_raw = t.sb("wp_raw", [P, KT, D])
        wp_hi = t.sb("wp_hi", [P, KT, D], F32R)
        wp_lo = t.sb("wp_lo", [P, KT, D], F32R)
        qT = t.sb("qT", [P, KT, TOK])
        kT_even = t.sb("kT_even", [P, KT, TOK])
        kT_odd = t.sb("kT_odd", [P, KT, TOK])
        v = t.sb("v_self", [P, TT, D])
        att = t.sb("att", [P, TT, D])
        qk_bias_rows = t.sb("qk_bias_rows", [2 * KT, P])
        qk_bias = t.sb("qk_bias", [P, 2 * KT])
        row_bias = t.sb("row_bias", [1, 2 * D])
        ones = t.sb("ones_row", [1, P])
        even = t.sb("even", [P, 1])
        odd = t.sb("odd", [P, 1])
        rel = t.sb("rel", [P, S])
        bias = t.sb("alibi", [P, 2, S])
        s_sb = t.sb("s_self", [P, 2, 3 * P])
        p_sb = t.sb("p_self", [P, 2, 3 * P])
        pT = t.sb("pT_self", [P, 2, 3 * P])
        mx = t.sb("mx_self", [P, 2, 2])
        nm = t.sb("nm_self", [P, 2, 2])
        rsum = t.sb("rsum_self", [P, TT, SA_HEADS])
        rinv = t.sb("rinv_self", [P, TT, SA_HEADS])
        stats = t.sb("stats1", [P, TT, 6])
        mv = t.sb("mv1", [P, TT, 2])
        std = t.sb("std1", [P, TT])
        rstd = t.sb("rstd1", [P, TT])
        x, bank, ident = k.x, k.bank, k.ident

        x_in, bias_in, wp_in = t.sem("x_in"), t.sem("bias_in"), t.sem("wp_in")
        wa_in = [t.sem("wa_in0"), t.sem("wa_in1")]
        const = t.sem("const_ready")
        mask = t.sem("mask_ready")
        xt_ps, xt_hi, xt_lo = t.sem("xt_ps"), t.sem("xt_hi"), t.sem("xt_lo")
        wa_his, wa_los = t.sem("wa_his"), t.sem("wa_los")
        wp_his, wp_los = t.sem("wp_his"), t.sem("wp_los")
        bt_ps, bt_out = t.sem("bt_ps"), t.sem("bt_out")
        qk_ps, q_out, k_out = t.sem("qk_ps"), t.sem("q_out"), t.sem("k_out")
        v_ps, v_out = t.sem("v_ps"), t.sem("v_out")
        bias_made = t.sem("alibi_made")
        s_ps, s_half, s_out = t.sem("s_ps_self"), t.sem("s_half_self"), t.sem("s_out_self")
        nm_made = t.sem("nm_made_self")
        p_made = t.sem("p_made_self")
        pt_ps, pt_out, o_ps = t.sem("pt_ps_self"), t.sem("pt_out_self"), t.sem("o_ps_self")
        rinv_made, att_out = t.sem("rinv_made_self"), t.sem("att_out")
        at_ps, at_hi, at_lo = t.sem("at_ps_self"), t.sem("at_hi_self"), t.sem("at_lo_self")
        y_ps, y_sum, y_stats, y_mv = t.sem("y_ps1"), t.sem("y_sum1"), t.sem("y_stats1"), t.sem("y_mv1")
        std_made, rstd_made, x1_made = t.sem("std_made1"), t.sem("rstd_made1"), t.sem("x1_made")
        x1t_ps, x1t_hi, x1t_lo = t.sem("x1t_ps"), t.sem("x1t_hi"), t.sem("x1t_lo")
        block = ctx.enter_context(nc.Block())

        heads = [(h, b) for h in range(SA_HEADS) for b in range(B)]
        N = len(heads)

        @block.sync
        def _(sp):
            for i in range(TT):
                sp.dma_start(x[:, i, :], d["x"].rearrange("b s d -> (b s) d")[i * P:(i + 1) * P, :])\
                    .then_inc(x_in, 16)
            sp.dma_start(qk_bias_rows[:], d["b_attn"][0:2 * D].rearrange("(m p) -> m p", p=P)).then_inc(bias_in, 16)
            sp.dma_start(row_bias[:, 0:D], d["b_attn"][2 * D:3 * D].rearrange("(a n) -> a n", a=1)).then_inc(bias_in, 16)
            sp.dma_start(row_bias[:, D:2 * D], d["b_proj"].rearrange("(a n) -> a n", a=1)).then_inc(bias_in, 16)
            for i in range(KT):
                if i >= 2:
                    sp.wait_ge(wa_los, i - 1)
                sp.dma_start(wa_raw[:, i % 2, :], d["w_attn"][i * P:(i + 1) * P, :]).then_inc(wa_in[i % 2], 16)
            sp.dma_start(wp_raw[:], d["w_proj"].rearrange("(k p) n -> p k n", p=P)).then_inc(wp_in, 16)

        @block.gpsimd
        def _(pool):
            nc.gpsimd.memset(ident[:], 0.0).then_inc(const, 1)
            nc.gpsimd.iota(rel[:], [[1, S]], base=-P, channel_multiplier=-1,
                           allow_small_or_imprecise_dtypes=True).then_inc(const, 1)
            nc.gpsimd.memset(ones[:], 1.0).then_inc(const, 1)
            pool.wait_ge(const, 3)
            nc.gpsimd.affine_select(out=ident[:], in_=ident[:], compare_op=ALU.not_equal, fill=1.0, base=0,
                                    pattern=[[-1, P]], channel_multiplier=1).then_inc(const, 1)
            nc.gpsimd.affine_select(out=rel[:], in_=rel[:], compare_op=ALU.is_ge, fill=MASKED, base=P,
                                    pattern=[[-1, S]], channel_multiplier=1).then_inc(const, 1)
            pool.wait_ge(const, 5)
            for h in range(SA_HEADS):
                if h >= 2:
                    pool.wait_ge(s_out, 2 * (h - 1))
                nc.gpsimd.tensor_scalar(bias[:, h % 2, :], rel[:], SLOPES[h] / SA_SCALE, 1.0, ALU.mult, ALU.mult)\
                    .then_inc(bias_made, 1)

        @block.scalar
        def _(act):
            act.wait_ge(bt_ps, 1)
            nc.scalar.activation(qk_bias[:], bank[:, 4, 0:2 * KT], ACT.Copy).then_inc(bt_out, 1)
            for i in range(KT):
                act.wait_ge(xt_ps, i + 1)
                nc.scalar.activation(xT_hi[:, i, :], bank[:, i, :], ACT.Copy).then_inc(xt_hi, 1)
            for i in range(KT):
                act.wait_ge(wa_in[i % 2], 16 * (i // 2 + 1))
                nc.scalar.activation(wa_hi[:, i, :], wa_raw[:, i % 2, :], ACT.Copy).then_inc(wa_his, 1)
            act.wait_ge(bt_out, 1)
            for m in range(KT):
                act.wait_ge(qk_ps, m + 1)
                nc.scalar.activation(qT[:, m, :], bank[:, 4 + m, :], ACT.Identity, bias=qk_bias[:, m:m + 1])\
                    .then_inc(q_out, 1)
            act.wait_ge(wp_in, 16)
            nc.scalar.activation(wp_hi[:], wp_raw[:], ACT.Copy).then_inc(wp_his, 1)
            for i in range(TT):
                act.wait_ge(v_ps, i + 1)
                nc.scalar.activation(v[:, i, :], bank[:, 4 + i, :], ACT.Copy).then_inc(v_out, 1)
            for n, (h, b) in enumerate(heads):
                act.wait_ge(nm_made, n + 1)
                if n >= 2:
                    act.wait_ge(pt_ps, n - 1)
                for qt, (a, e) in enumerate(((0, P), (P, 3 * P))):
                    nc.scalar.activation(p_sb[:, n % 2, a:e], s_sb[:, n % 2, a:e], ACT.Exp,
                                         bias=nm[:, n % 2, qt:qt + 1], scale=SA_SCALE,
                                         accum_out=rsum[:, 2 * b + qt, h:h + 1]).then_inc(p_made, 1)
            for i in range(KT):
                act.wait_ge(at_ps, i + 1)
                nc.scalar.activation(xT_hi[:, i, :], bank[:, i, :], ACT.Copy).then_inc(at_hi, 1)
            for i in range(TT):
                act.wait_ge(y_mv, i + 1)
                nc.scalar.activation(std[:, i:i + 1], mv[:, i, 1:2], ACT.Sqrt, bias=k.ln_eps[:]).then_inc(std_made, 1)
            for i in range(KT):
                act.wait_ge(x1t_ps, i + 1)
                nc.scalar.activation(k.x1_hi[:, i, :], bank[:, i, :], ACT.Copy).then_inc(x1t_hi, 1)

        @block.vector
        def _(dve):
            nc.vector.memset(even[:], 0.0).then_inc(mask, 1)
            nc.vector.memset(k.ln_eps[:], LN_EPS).then_inc(mask, 1)
            nc.vector.memset(k.rms_eps[:], RMS_EPS).then_inc(mask, 1)
            dve.wait_ge(mask, 3)
            for g in range(P // 32):
                nc.vector.memset(even[32 * g:32 * g + SA_DIM, :], 1.0).then_inc(mask, 1)
            dve.wait_ge(mask, 7)
            nc.vector.tensor_scalar(odd[:], even[:], -1.0, 1.0, ALU.mult, ALU.add).then_inc(mask, 1)
            for i in range(KT):
                dve.wait_ge(xt_hi, i + 1)
                nc.vector.tensor_tensor(xT_lo[:, i, :], bank[:, i, :], f32(xT_hi[:, i, :]), ALU.subtract)\
                    .then_inc(xt_lo, 1)
            for i in range(KT):
                dve.wait_ge(wa_his, i + 1)
                nc.vector.tensor_tensor(wa_lo[:, i, :], wa_raw[:, i % 2, :], f32(wa_hi[:, i, :]), ALU.subtract)\
                    .then_inc(wa_los, 1)
            dve.wait_ge(mask, 8)
            dve.wait_ge(bt_out, 1)
            for m in range(KT):
                dve.wait_ge(qk_ps, KT + m + 1)
                for dst, keep in ((kT_even, even), (kT_odd, odd)):
                    nc.vector.tensor_scalar(dst[:, m, :], bank[:, 4 + m, :], qk_bias[:, KT + m:KT + m + 1],
                                            keep[:], ALU.add, ALU.mult).then_inc(k_out, 1)
            dve.wait_ge(wp_his, 1)
            nc.vector.tensor_tensor(wp_lo[:], wp_raw[:], f32(wp_hi[:]), ALU.subtract).then_inc(wp_los, 1)

            def softmax_shift(n):
                h = heads[n][0]
                dve.wait_ge(s_ps, n + 1)
                dve.wait_ge(bias_made, h + 1)
                if n >= 2:
                    dve.wait_ge(p_made, 2 * (n - 1))
                for qt, (a, e, rel0) in enumerate(((0, P, P), (P, 3 * P, 0))):
                    nc.vector.tensor_tensor_reduce(out=s_sb[:, n % 2, a:e], in0=bank[:, n % 2, a:e],
                                                   in1=bias[:, h % 2, rel0:S], scale=1.0, scalar=-3e38,
                                                   op0=ALU.add, op1=ALU.max,
                                                   accum_out=mx[:, n % 2, qt:qt + 1])\
                        .then_inc(s_out if qt else s_half, 1)
                dve.wait_ge(s_half, n + 1)
                dve.wait_ge(s_out, n + 1)
                nc.vector.tensor_scalar(nm[:, n % 2, :], mx[:, n % 2, :], -SA_SCALE, None, ALU.mult)\
                    .then_inc(nm_made, 1)

            def take_transposed(n):
                dve.wait_ge(pt_ps, n + 1)
                if n >= 2:
                    dve.wait_ge(o_ps, n - 1)
                nc.vector.tensor_copy(pT[:, n % 2, :], bank[:, 2 + n % 2, 0:3 * P]).then_inc(pt_out, 1)

            softmax_shift(0)
            for n in range(N):
                if n + 1 < N:
                    softmax_shift(n + 1)
                take_transposed(n)
            dve.wait_ge(p_made, 2 * N)
            nc.vector.reciprocal(rinv[:], rsum[:]).then_inc(rinv_made, 1)
            dve.wait_ge(rinv_made, 1)
            dve.wait_ge(o_ps, N)
            for i in range(TT):
                nc.vector.tensor_tensor(att[:, i, :].rearrange("p (h e) -> p h e", h=SA_HEADS),
                                        bank[:, 4 + i, :].rearrange("p (h e) -> p h e", h=SA_HEADS),
                                        rinv[:, i, :].rearrange("p (h a) -> p h a", a=1)
                                        .to_broadcast([P, SA_HEADS, SA_DIM]), ALU.mult).then_inc(att_out, 1)
            for i in range(KT):
                dve.wait_ge(at_hi, i + 1)
                nc.vector.tensor_tensor(xT_lo[:, i, :], bank[:, i, :], f32(xT_hi[:, i, :]), ALU.subtract)\
                    .then_inc(at_lo, 1)
            for i in range(TT):
                dve.wait_ge(y_ps, i + 1)
                nc.vector.tensor_tensor(x[:, i, :], bank[:, 4 + i, :], x[:, i, :], ALU.add).then_inc(y_sum, 1)
                dve.wait_ge(y_sum, i + 1)
                nc.vector.bn_stats(stats[:, i, :], x[:, i, :]).then_inc(y_stats, 1)
                dve.wait_ge(y_stats, i + 1)
                nc.vector.bn_aggr(mv[:, i, :], stats[:, i, :]).then_inc(y_mv, 1)
            for i in range(TT):
                dve.wait_ge(std_made, i + 1)
                nc.vector.reciprocal(rstd[:, i:i + 1], std[:, i:i + 1]).then_inc(rstd_made, 1)
                dve.wait_ge(rstd_made, i + 1)
                nc.vector.tensor_scalar(x[:, i, :], x[:, i, :], mv[:, i, 0:1], rstd[:, i:i + 1],
                                        ALU.subtract, ALU.mult).then_inc(x1_made, 1)
            for i in range(KT):
                dve.wait_ge(x1t_hi, i + 1)
                nc.vector.tensor_tensor(k.x1_lo[:, i, :], bank[:, i, :], f32(k.x1_hi[:, i, :]), ALU.subtract)\
                    .then_inc(x1t_lo, 1)

        @block.tensor
        def _(pe):
            pe.wait_ge(const, 5)
            pe.wait_ge(bias_in, 48)
            nc.tensor.transpose(bank[:, 4, 0:2 * KT], qk_bias_rows[:], ident[0:2 * KT, 0:2 * KT]).then_inc(bt_ps, 1)
            pe.wait_ge(x_in, 16 * TT)
            for i in range(KT):
                for j in range(TT):
                    last = nc.tensor.transpose(bank[:, i, j * P:(j + 1) * P], x[:, j, i * P:(i + 1) * P], ident[:])
                last.then_inc(xt_ps, 1)
            pe.wait_ge(wa_los, KT)
            pe.wait_ge(xt_lo, KT)
            for m in range(2 * KT):
                if m == 0:
                    pe.wait_ge(bt_out, 1)
                if m >= KT:
                    pe.wait_ge(q_out, m - KT + 1)
                for i in range(KT):
                    w = slice(m * P, (m + 1) * P)
                    last = three_passes(nc, bank[:, 4 + m % KT, :], wa_hi[:, i, w], wa_lo[:, i, w],
                                        xT_hi[:, i, :], xT_lo[:, i, :], i == 0, i == KT - 1)
                last.then_inc(qk_ps, 1)
            for j in range(TT):
                pe.wait_ge(k_out, 2 * (j + 1))
                nc.tensor.matmul(bank[:, 4 + j, :], ones[:], row_bias[:, 0:D], start=True, stop=False)
                for i in range(KT):
                    w = slice(j * P, (j + 1) * P)
                    last = three_passes(nc, bank[:, 4 + j, :], xT_hi[:, i, w], xT_lo[:, i, w],
                                        wa_hi[:, i, 2 * D:3 * D], wa_lo[:, i, 2 * D:3 * D], False, i == KT - 1)
                last.then_inc(v_ps, 1)

            def scores(n):
                h, b = heads[n]
                m, r = h // 8, 32 * (h % 8 // 2)
                keys = kT_odd if h % 2 else kT_even
                if n >= 2:
                    pe.wait_ge(s_out, n - 1)
                nc.tensor.matmul(bank[:, n % 2, 0:P], qT[r:r + 32, m, b * S:b * S + P],
                                 keys[r:r + 32, m, b * S:b * S + P], start=True, stop=True)
                nc.tensor.matmul(bank[:, n % 2, P:3 * P], qT[r:r + 32, m, b * S + P:b * S + S],
                                 keys[r:r + 32, m, b * S:b * S + S], start=True, stop=True).then_inc(s_ps, 1)

            def transposes(n):
                pe.wait_ge(p_made, 2 * (n + 1))
                if n >= 2:
                    pe.wait_ge(pt_out, n - 1)
                for j in range(3):
                    last = nc.tensor.transpose(bank[:, 2 + n % 2, j * P:(j + 1) * P],
                                               p_sb[:, n % 2, j * P:(j + 1) * P], ident[:])
                last.then_inc(pt_ps, 1)

            def weigh_values(n):
                h, b = heads[n]
                w = slice(h * SA_DIM, (h + 1) * SA_DIM)
                pe.wait_ge(pt_out, n + 1)
                for qt, kt, start, stop in ((0, 0, True, True), (1, 0, True, False), (1, 1, False, True)):
                    last = nc.tensor.matmul(bank[:, 4 + 2 * b + qt, w], pT[:, n % 2, (qt + kt) * P:(qt + kt + 1) * P],
                                            v[:, 2 * b + kt, w], start=start, stop=stop)
                last.then_inc(o_ps, 1)

            pe.wait_ge(v_out, TT)
            scores(0)
            for n in range(N):
                if n + 1 < N:
                    scores(n + 1)
                if n >= 1:
                    weigh_values(n - 1)
                transposes(n)
            weigh_values(N - 1)
            pe.wait_ge(pt_out, N)
            for i in range(KT):
                pe.wait_ge(att_out, TT)
                for j in range(TT):
                    last = nc.tensor.transpose(bank[:, i, j * P:(j + 1) * P], att[:, j, i * P:(i + 1) * P], ident[:])
                last.then_inc(at_ps, 1)
            pe.wait_ge(wp_los, 1)
            pe.wait_ge(at_lo, KT)
            for j in range(TT):
                nc.tensor.matmul(bank[:, 4 + j, :], ones[:], row_bias[:, D:2 * D], start=True, stop=False)
                for i in range(KT):
                    w = slice(j * P, (j + 1) * P)
                    last = three_passes(nc, bank[:, 4 + j, :], xT_hi[:, i, w], xT_lo[:, i, w],
                                        wp_hi[:, i, :], wp_lo[:, i, :], False, i == KT - 1)
                last.then_inc(y_ps, 1)
            pe.wait_ge(x1_made, TT)
            for i in range(KT):
                for j in range(TT):
                    last = nc.tensor.transpose(bank[:, i, j * P:(j + 1) * P], x[:, j, i * P:(i + 1) * P], ident[:])
                last.then_inc(x1t_ps, 1)


def keys_values(nc, d, k):
    with ExitStack() as ctx:
        t = Tensors(nc, ctx)
        w_raw = t.sb("wkv_raw", [P, 2, KVH * HD])
        w_hi = t.sb("wkv_hi", [P, 2, KT, KVH * HD], F32R)
        w_lo = t.sb("wkv_lo", [P, 2, KT, KVH * HD], F32R)
        c_raw = t.sb("c_raw", [P, 2, D])
        cT_hi = t.sb("cT_hi", [P, 2, KT, P], F32R)
        cT_lo = t.sb("cT_lo", [P, 2, KT, P], F32R)
        k_raw = t.sb("k_raw", [P, KVH, HD])
        k_sq = t.sb("k_sq", [P, KVH, HD])
        k_ss = t.sb("k_ss", [P, KVH])
        k_std = t.sb("k_std", [P, KVH])
        k_inv = t.sb("k_inv", [P, KVH])
        k_nrm = t.sb("k_nrm", [P, KVH, HD])
        kT_st = t.sb("kT_st", [P, 2, KVH, P])
        v_st = t.sb("v_st", [P, 2, KVH, HD])
        nw_rows = t.sb("nw_rows", [2, HD])
        nw_cols = t.sb("nw_cols", [P, 2])
        nw = t.sb("nw", [P, 1])
        bank, ident = k.bank, k.ident

        nw_in = t.sem("nw_in")
        nw_ps, nw_out, nw_made = t.sem("nw_ps"), t.sem("nw_out"), t.sem("nw_made")
        w_in = [t.sem("wkv_in0"), t.sem("wkv_in1")]
        w_his, w_los = t.sem("wkv_his"), t.sem("wkv_los")
        c_in = [t.sem("c_in0"), t.sem("c_in1")]
        ct_ps, ct_hi, ct_lo = t.sem("ct_ps"), t.sem("ct_hi"), t.sem("ct_lo")
        k_ps, k_out, ksq_made, kss_made = t.sem("k_ps"), t.sem("k_out2"), t.sem("ksq_made"), t.sem("kss_made")
        kstd_made, kinv_made, knrm_made = t.sem("kstd_made"), t.sem("kinv_made"), t.sem("knrm_made")
        v_ps, v_out = t.sem("v_ps2"), t.sem("v_out2")
        kt_ps, kt_out = t.sem("kt_ps"), t.sem("kt_out")
        k_store = [t.sem("k_store0"), t.sem("k_store1")]
        v_store = [t.sem("v_store0"), t.sem("v_store1")]
        block = ctx.enter_context(nc.Block())

        LAT = S // P
        LAST = CT + LAT - 1

        def all_tiles(eng, step):
            for b in range(B):
                step(0, b, True, True, True)
            with eng.Fori(1, CT - 1) as c:
                for b in range(B):
                    step(c, b, False, True, True)
            for c in range(CT - 1, CT + LAT):
                for b in range(B):
                    step(c, b, False, c < CT, c < CT and b == 0)

        def context_rows(b, c):
            return d["ctx"].rearrange("b (c p) d -> b c p d", p=P)[b, c, :, :]

        @block.sync
        def _(sp):
            sp.dma_start(nw_rows[0:1, :], d["q_norm"].rearrange("(a n) -> a n", a=1)).then_inc(nw_in, 16)
            sp.dma_start(nw_rows[1:2, :], d["k_norm"].rearrange("(a n) -> a n", a=1)).then_inc(nw_in, 16)
            for b in range(B):
                sp.dma_start(c_raw[:, b, :], context_rows(b, 0)).then_inc(c_in[b], 16)
            for n in range(2 * KT):
                if n >= 2:
                    sp.wait_ge(w_los, n - 1)
                src = d["Wk"] if n < KT else d["Wv"]
                sp.dma_start(w_raw[:, n % 2, :], src[n % KT * P:(n % KT + 1) * P, :]).then_inc(w_in[n % 2], 16)

            v_view = k.v_dram.rearrange("h p (n e) -> p h n e", e=HD)
            k_view = k.kT_dram.rearrange("h p (n e) -> p h n e", e=P)

            def step(c, b, early, context, following):
                if context and not (isinstance(c, int) and c == CT - 1):
                    sp.wait_ge(ct_ps, 2 * c + b + 1)
                    sp.dma_start(c_raw[:, b, :], context_rows(b, c + 1)).then_inc(c_in[b], 16)
                sp.wait_ge(v_out, 2 * c + b + 1)
                sp.dma_start(v_view[:, :, b * KTL + c, :], v_st[:, b, :, :]).then_inc(v_store[b], 16)
                sp.wait_ge(kt_out, 2 * c + b + 1)
                sp.dma_start(k_view[:, :, b * KTL + c, :], kT_st[:, b, :, :]).then_inc(k_store[b], 16)

            all_tiles(sp, step)
            for b in range(B):
                sp.wait_ge(v_store[b], 16 * (LAST + 1))
                sp.wait_ge(k_store[b], 16 * (LAST + 1))

        @block.scalar
        def _(act):
            def context_hi(n, b, early):
                act.wait_ge(ct_ps, n + 1)
                if not early:
                    act.wait_ge(v_ps, n - 1)
                nc.scalar.activation(cT_hi[:, b, :, :], bank[:, 6, :].rearrange("p (k t) -> p k t", k=KT), ACT.Copy)\
                    .then_inc(ct_hi, 1)

            act.wait_ge(nw_ps, 1)
            nc.scalar.activation(nw_cols[:], bank[:, 0, 0:2], ACT.Copy).then_inc(nw_out, 1)
            for n in range(2 * KT):
                act.wait_ge(w_in[n % 2], 16 * (n // 2 + 1))
                nc.scalar.activation(w_hi[:, n // KT, n % KT, :], w_raw[:, n % 2, :], ACT.Copy).then_inc(w_his, 1)
                if n == 0:
                    context_hi(0, 0, True)
            act.wait_ge(nw_made, 1)

            def step(c, b, early, context, following):
                n = 2 * c + b
                act.wait_ge(k_ps, n + 1)
                nc.scalar.activation(k_raw[:].rearrange("p (a h) e -> p a (h e)", a=2), bank[:, 2 * b:2 * b + 2, :],
                                     ACT.Copy).then_inc(k_out, 1)
                act.wait_ge(k_out, n + 1)
                nc.scalar.activation(k_sq[:], k_raw[:], ACT.Square).then_inc(ksq_made, 1)
                act.wait_ge(kss_made, n + 1)
                nc.scalar.activation(k_std[:], k_ss[:], ACT.Sqrt, bias=k.rms_eps[:], scale=1.0 / HD)\
                    .then_inc(kstd_made, 1)
                if following:
                    context_hi(n + 1, 1 - b, early and b == 0)
                act.wait_ge(kt_ps, n + 1)
                if not early:
                    act.wait_ge(k_store[b], 16 * c)
                nc.scalar.activation(kT_st[:, b, :, :].rearrange("p (a h) e -> p a (h e)", a=2), bank[:, 6:8, :],
                                     ACT.Copy, scale=nw[:]).then_inc(kt_out, 1)

            all_tiles(act, step)

        @block.vector
        def _(dve):
            def context_lo(n, b):
                dve.wait_ge(ct_hi, n + 1)
                nc.vector.tensor_tensor(cT_lo[:, b, :, :], bank[:, 6, :].rearrange("p (k t) -> p k t", k=KT),
                                        f32(cT_hi[:, b, :, :]), ALU.subtract).then_inc(ct_lo, 1)

            dve.wait_ge(nw_out, 1)
            nc.vector.tensor_tensor(nw[:], nw_cols[:, 0:1], nw_cols[:, 1:2], ALU.mult).then_inc(nw_made, 1)
            for n in range(2 * KT):
                dve.wait_ge(w_his, n + 1)
                nc.vector.tensor_tensor(w_lo[:, n // KT, n % KT, :], w_raw[:, n % 2, :],
                                        f32(w_hi[:, n // KT, n % KT, :]), ALU.subtract).then_inc(w_los, 1)
                if n == 0:
                    context_lo(0, 0)

            def step(c, b, early, context, following):
                n = 2 * c + b
                dve.wait_ge(ksq_made, n + 1)
                nc.vector.tensor_reduce(k_ss[:], k_sq[:], AX.X, ALU.add).then_inc(kss_made, 1)
                dve.wait_ge(kstd_made, n + 1)
                nc.vector.reciprocal(k_inv[:], k_std[:]).then_inc(kinv_made, 1)
                dve.wait_ge(kinv_made, n + 1)
                nc.vector.tensor_tensor(k_nrm[:], k_raw[:], k_inv[:].rearrange("p (h a) -> p h a", a=1)
                                        .to_broadcast([P, KVH, HD]), ALU.mult).then_inc(knrm_made, 1)
                if following:
                    context_lo(n + 1, 1 - b)
                dve.wait_ge(v_ps, n + 1)
                if not early:
                    dve.wait_ge(v_store[b], 16 * c)
                nc.vector.tensor_copy(v_st[:, b, :, :].rearrange("p (a h) e -> p a (h e)", a=2), bank[:, 4:6, :])\
                    .then_inc(v_out, 1)

            all_tiles(dve, step)

        @block.tensor
        def _(pe):
            def context_transposes(b):
                for i in range(KT):
                    last = nc.tensor.transpose(bank[:, 6, i * P:(i + 1) * P], c_raw[:, b, i * P:(i + 1) * P], ident[:])
                last.then_inc(ct_ps, 1)

            def project(which, first_bank, rows_hi, rows_lo, done):
                for g in range(2):
                    w = slice(g * 512, (g + 1) * 512)
                    for i in range(KT):
                        last = three_passes(nc, bank[:, first_bank + g, :], rows_hi[:, i, :], rows_lo[:, i, :],
                                            w_hi[:, which, i, w], w_lo[:, which, i, w], i == 0, i == KT - 1)
                last.then_inc(done, 1)

            pe.wait_ge(nw_in, 32)
            nc.tensor.transpose(bank[:, 0, 0:2], nw_rows[:], ident[0:2, 0:2]).then_inc(nw_ps, 1)
            pe.wait_ge(c_in[0], 16)
            context_transposes(0)
            pe.wait_ge(nw_out, 1)
            pe.wait_ge(w_los, 2 * KT)

            def step(c, b, early, context, following):
                n = 2 * c + b
                if context:
                    pe.wait_ge(ct_lo, n + 1)
                    rows_hi, rows_lo = cT_hi[:, b, :, :], cT_lo[:, b, :, :]
                else:
                    row = (2 * b + c - CT) * P
                    rows_hi, rows_lo = k.x1_hi[:, :, row:row + P], k.x1_lo[:, :, row:row + P]
                if not early:
                    pe.wait_ge(k_out, n - 1)
                project(0, 2 * b, rows_hi, rows_lo, k_ps)
                if not (early and b == 0):
                    pe.wait_ge(kt_out, n)
                if following:
                    pe.wait_ge(c_in[1 - b], 16 * (c + b + 1))
                    context_transposes(1 - b)
                if not (early and b == 0):
                    pe.wait_ge(v_out, n)
                project(1, 4, rows_hi, rows_lo, v_ps)
                if following:
                    pe.wait_ge(ct_lo, n + 2)
                pe.wait_ge(knrm_made, n + 1)
                for h in range(KVH):
                    last = nc.tensor.transpose(bank[:, 6 + h // 4, h % 4 * P:(h % 4 + 1) * P], k_nrm[:, h, :], ident[:])
                last.then_inc(kt_ps, 1)

            all_tiles(pe, step)


UNITS = 2 * B
UT = 4
TILES = UNITS * UT
PIECE = 4
RING = 3
BEFORE = TT + GRP
STEP = [("S", 0), ("T", 0), ("T", 1), ("S", 1), ("T", 2), ("O", 0), ("T", 3), ("S", 2), ("O", 1), ("T", 4),
        ("O", 2), ("S", 3), ("T", 5), ("O", 3), ("O", 4), ("O", 5)]
SUM_AFTER = {1: 0, 3: 1, 4: 2, 5: 3}


class Turn:

    def __init__(self, i, last):
        self.i, self.last = i, last
        n = 0 if last else TT
        m = 0 if last else GRP
        base = BEFORE + (4 * KTL + TT + GRP + TT) * i
        t = [0, KTL, 2 * KTL + n, 3 * KTL + n + m + 2]
        self.weights = [base + a for a in t]
        self.queries = base + 2 * KTL
        self.queries_T = base + 3 * KTL + n
        self.output = [base + 3 * KTL + n + m, base + 4 * KTL + n + m + 2]
        self.begin = base
        self.slot0 = (BEFORE, t, 2 * KTL, 3 * KTL + n, [3 * KTL + n + m, 4 * KTL + n + m + 2])

    def bank(self, kind, k, at=0):
        before, t, q, qt, w = self.slot0
        if kind == "T":
            offset = t[k] + at
        elif kind == "W":
            offset = w[k] + at
        else:
            offset = (q if kind == "Q" else qt) + at
        return 4 + (before + offset) % RING


assert (4 * KTL + TT + GRP + TT) % RING == 0


def cross_attention(nc, d, k):
    with ExitStack() as ctx:
        t = Tensors(nc, ctx)
        k_raw = t.sb("xk_raw", [P, B, KEYS])
        v_raw = t.sb("xv_raw", [P, B, KEYS])
        k_hi = t.sb("xk_hi", [P, B, KEYS], F32R)
        k_lo = t.sb("xk_lo", [P, B, KEYS], F32R)
        v_hi = t.sb("xv_hi", [P, B, KEYS], F32R)
        v_lo = t.sb("xv_lo", [P, B, KEYS], F32R)
        wq_raw = t.sb("wq_raw", [P, KT, D])
        wq_hi = t.sb("wq_hi", [P, KT, D], F32R)
        wq_lo = t.sb("wq_lo", [P, KT, D], F32R)
        wo_raw = t.sb("wo_raw", [P, GRP, D])
        wo_hi = t.sb("wo_hi", [P, GRP, D], F32R)
        wo_lo = t.sb("wo_lo", [P, GRP, D], F32R)
        q = t.sb("q_rows", [P, TT, D])
        q_sq = t.sb("q_sq", [P, TT, D])
        q_ss = t.sb("q_ss", [P, TT * GRP])
        q_ms = t.sb("q_ms", [P, TT * GRP])
        q_inv = t.sb("q_inv", [P, TT * GRP])
        minus_half = t.sb("minus_half", [P, TT * GRP])
        q_rms = t.sb("q_rms", [P, TT * GRP])
        qT_hi = t.sb("qT_hi", [P, GRP, TOK], F32R)
        qT_lo = t.sb("qT_lo", [P, GRP, TOK], F32R)
        prob = t.sb("prob", [P, 2 * UT, KEYS])
        mx = t.sb("x_mx", [P, 2 * UT])
        nm = t.sb("x_nm", [P, 2 * UT])
        rsum = t.sb("x_rsum", [P, 2 * UT])
        rinv = t.sb("x_rinv", [P, 2 * UT])
        pT_hi = t.sb("pT_hi", [P, KTL, UT * P], F32R)
        pT_lo = t.sb("pT_lo", [P, KTL, UT * P], F32R)
        oT_hi = t.sb("oT_hi", [P, GRP, TOK], F32R)
        oT_lo = t.sb("oT_lo", [P, GRP, TOK], F32R)
        x, bank, ident = k.x, k.bank, k.ident

        k_in = [t.sem("xk_in0"), t.sem("xk_in1")]
        v_in = [t.sem("xv_in0"), t.sem("xv_in1")]
        wq_in, wo_in = t.sem("wq_in"), t.sem("wo_in")
        piece_hi = t.sem("piece_hi")
        k_split, v_split, wq_split, wo_split = t.sem("xk_split"), t.sem("xv_split"), t.sem("wq_split"), t.sem("wo_split")
        ring_full = t.sem("ring_full")
        ring_out = t.sem("ring_out")
        q_out, qt_his = t.sem("xq_out"), t.sem("qt_his")
        half_set, ss_part, ms_made = t.sem("half_set"), t.sem("ss_part"), t.sem("ms_made")
        inv_made, rms_made = t.sem("inv_made"), t.sem("rms_made")
        s_full, mx_made, nm_made = t.sem("s_full"), t.sem("x_mx_made"), t.sem("x_nm_made")
        exp_made, rinv_made, prob_made = t.sem("exp_made"), t.sem("x_rinv_made"), t.sem("prob_made")
        pt_his = t.sem("pt_his")
        o_full, o_his, o_out = t.sem("o_full"), t.sem("o_his"), t.sem("o_out")
        block = ctx.enter_context(nc.Block())

        def turns(eng, body):
            with eng.Fori(0, KVH - 1) as i:
                body(Turn(i, False))
            body(Turn(KVH - 1, True))

        def tile_of(u, j):
            return 2 * (u % 2) + j // 2, 2 * (u // 2) + j % 2

        def column(u, j):
            g, tt = tile_of(u, j)
            return slice(tt * GRP + g, tt * GRP + g + 1)

        @block.sync
        def _(sp):
            wq_view = d["Wq"].rearrange("(k p) (h n) -> h p k n", p=P, n=D)
            wo_view = d["Wo"].rearrange("(h g p) n -> h p g n", p=HD, g=GRP)

            def load_keys(b, i):
                sp.dma_start(k_raw[:, b, :], k.kT_dram[i, :, b * KEYS:(b + 1) * KEYS]).then_inc(k_in[b], 16)

            def load_values(b, i):
                sp.dma_start(v_raw[:, b, :], k.v_dram[i, :, b * KEYS:(b + 1) * KEYS]).then_inc(v_in[b], 16)

            def load_wq(i):
                sp.dma_start(wq_raw[:], wq_view[i, :, :, :]).then_inc(wq_in, 16)

            def load_wo(i):
                sp.dma_start(wo_raw[:], wo_view[i, :, :, :]).then_inc(wo_in, 16)

            load_wq(0)
            for b in range(B):
                load_keys(b, 0)
            for b in range(B):
                load_values(b, 0)
            load_wo(0)
            sp.wait_ge(wq_split, PIECE)
            load_wq(1)
            sp.wait_ge(k_split, PIECE)
            for b in range(B):
                load_keys(b, 1)
            sp.wait_ge(v_split, PIECE // 2)
            load_values(0, 1)
            with sp.Fori(0, KVH - 2) as i:
                sp.wait_ge(v_split, PIECE * i + PIECE)
                load_values(1, i + 1)
                sp.wait_ge(wq_split, PIECE * i + 2 * PIECE)
                load_wq(i + 2)
                sp.wait_ge(wo_split, PIECE * i + PIECE)
                load_wo(i + 1)
                sp.wait_ge(k_split, PIECE * i + PIECE + PIECE // 2)
                load_keys(0, i + 2)
                sp.wait_ge(v_split, PIECE * i + PIECE + PIECE // 2)
                load_values(0, i + 2)
                sp.wait_ge(k_split, PIECE * i + 2 * PIECE)
                load_keys(1, i + 2)
            sp.wait_ge(v_split, PIECE * (KVH - 1))
            load_values(1, KVH - 1)
            sp.wait_ge(wo_split, PIECE * (KVH - 1))
            load_wo(KVH - 1)

        @block.gpsimd
        def _(pool):
            awaited = pool.alloc_register("awaited")

            def wait_alone(sem, value):
                if not isinstance(value, int):
                    pool.reg_mov(awaited, value)
                    value = awaited
                pool.wait_ge(half_set, 1)
                pool.wait_ge(sem, value)

            def split(hi, lo, raw, count, done):
                nc.gpsimd.tensor_scalar(hi, raw, 1.0, 1.0, ALU.mult, ALU.mult).then_inc(piece_hi, 1)
                pool.wait_ge(piece_hi, count + 1)
                nc.gpsimd.tensor_tensor(lo, raw, f32(hi), ALU.subtract).then_inc(done, 1)

            def keys(b, piece, i, count):
                w = slice(piece * HALF, (piece + 1) * HALF)
                wait_alone(k_in[b], 16 * i + 16)
                split(k_hi[:, b, w], k_lo[:, b, w], k_raw[:, b, w], count, k_split)

            def values(b, piece, i, count):
                w = slice(piece * HALF, (piece + 1) * HALF)
                wait_alone(v_in[b], 16 * i + 16)
                split(v_hi[:, b, w], v_lo[:, b, w], v_raw[:, b, w], count, v_split)

            def query_weights(piece, i, count):
                wait_alone(wq_in, 16 * i + 16)
                split(wq_hi[:, piece, :], wq_lo[:, piece, :], wq_raw[:, piece, :], count, wq_split)

            def output_weights(piece, i, count):
                wait_alone(wo_in, 16 * i + 16)
                split(wo_hi[:, piece, :], wo_lo[:, piece, :], wo_raw[:, piece, :], count, wo_split)

            def inverse_rms(i):
                pool.wait_ge(ms_made, i + 1)
                nc.gpsimd.tensor_tensor(q_inv[:], q_ms[:], minus_half[:], ALU.pow).then_inc(inv_made, 1)

            def norm(n, s):
                wait_alone(rinv_made, n + 1)
                nc.gpsimd.tensor_scalar(prob[:, s, :], prob[:, s, :], rinv[:, s:s + 1], 1.0, ALU.mult, ALU.mult)\
                    .then_inc(prob_made, 1)

            for p in range(PIECE):
                query_weights(p, 0, p)
            for b in range(B):
                for p in range(2):
                    keys(b, p, 0, PIECE + 2 * b + p)
            for p in range(2):
                values(0, p, 0, 2 * PIECE + p)
            pool.wait_ge(half_set, 1)
            inverse_rms(0)
            for j in range(UT):
                norm(j, j)
            FIRST = 2 * PIECE + 2

            def body(turn):
                i = turn.i
                c = FIRST + 4 * PIECE * i
                more = not turn.last
                o = 0 if turn.last else PIECE
                for s in range(UNITS):
                    if s == UNITS - 1 and turn.last:
                        break
                    for j in range(UT):
                        norm(TILES * i + UT * (s + 1) + j, UT * ((s + 1) % 2) + j)
                        if s == 0 and j == 0:
                            wait_alone(ring_full, turn.begin - 1)
                            values(1, 0, i, c)
                        elif s == 0 and j == 1:
                            values(1, 1, i, c + 1)
                            if more:
                                query_weights(0, i + 1, c + 2)
                        elif s == 0 and more:
                            query_weights(j - 1, i + 1, c + 1 + j)
                        elif s == 1 and j == 0 and more:
                            query_weights(3, i + 1, c + 5)
                        elif s == 1 and j > 0:
                            if j == 1:
                                wait_alone(ring_full, turn.begin)
                            output_weights(j - 1, i, c + 1 + o + j)
                        elif s == 2 and j == 0:
                            output_weights(3, i, c + 5 + o)
                            if more:
                                inverse_rms(i + 1)
                        elif s == 2 and j < 3 and more:
                            if j == 1:
                                wait_alone(s_full, TILES * i + 2 * UT)
                            keys(0, j - 1, i + 1, c + 9 + j)
                        elif s == 2 and more:
                            wait_alone(o_full, UNITS * i + 2)
                            values(0, 0, i + 1, c + 12)
                        elif s == 3 and j == 0:
                            values(0, 1, i + 1, c + 13)
                        elif s == 3 and j < 3:
                            if j == 1:
                                wait_alone(s_full, TILES * (i + 1))
                            keys(1, j - 1, i + 1, c + 13 + j)

            turns(pool, body)

        @block.scalar
        def _(act):
            def take_queries(first, bank_of, i):
                for tt in range(TT):
                    act.wait_ge(ring_full, first + tt + 1)
                    nc.scalar.activation(q[:, tt, :], bank[:, bank_of(tt), :], ACT.Copy).then_inc(q_out, 1)

            def split_queries(first, bank_of):
                for g in range(GRP):
                    act.wait_ge(ring_full, first + g + 1)
                    nc.scalar.activation(qT_hi[:, g, :], bank[:, bank_of(g), :], ACT.Copy).then_inc(qt_his, 1)

            def exponentials(n, u, j):
                s = UT * (u % 2) + j
                act.wait_ge(nm_made, n + 1)
                nc.scalar.activation(prob[:, s, :].rearrange("p (a e) -> p a e", a=2),
                                     bank[:, 2 * (j % 2):2 * (j % 2) + 2, 0:HALF], ACT.Exp, bias=nm[:, s:s + 1],
                                     scale=q_rms[:, column(u, j)], accum_out=rsum[:, s:s + 1]).then_inc(exp_made, 1)

            take_queries(0, lambda a: 4 + a % RING, 0)
            split_queries(TT, lambda a: 4 + (TT + a) % RING)
            for j in range(UT):
                exponentials(j, 0, j)

            def body(turn):
                i = turn.i
                for s in range(UNITS):
                    u = (s + 1) % UNITS
                    for what, a in STEP:
                        if what == "S" and not (turn.last and s == UNITS - 1):
                            exponentials(TILES * i + UT * (s + 1) + a, u, a)
                        elif what == "T":
                            act.wait_ge(ring_full, turn.weights[s] + a + 1)
                            nc.scalar.activation(pT_hi[:, a, :], bank[:, turn.bank("T", s, a), :], ACT.Copy)\
                                .then_inc(pt_his, 1)
                    act.wait_ge(o_full, UNITS * i + s + 1)
                    g, rows = 2 * (s % 2), slice(s // 2 * S, (s // 2 + 1) * S)
                    nc.scalar.activation(oT_hi[:, g:g + 2, rows], bank[:, 7, :].rearrange("p (g t) -> p g t", g=2),
                                         ACT.Copy).then_inc(o_his, 1)
                    if s == 1 and not turn.last:
                        take_queries(turn.queries, lambda a: turn.bank("Q", 0, a), i + 1)
                    if s == 2 and not turn.last:
                        split_queries(turn.queries_T, lambda a: turn.bank("QT", 0, a))

            turns(act, body)

        @block.vector
        def _(dve):
            nc.vector.memset(minus_half[:], -0.5).then_inc(half_set, 1)

            def mean_squares(first, bank_of, i):
                for tt in range(TT):
                    dve.wait_ge(q_out, TT * i + tt + 1)
                    for g in range(GRP):
                        w = slice(g * HD, (g + 1) * HD)
                        nc.vector.tensor_tensor_reduce(out=q_sq[:, tt, w], in0=bank[:, bank_of(tt), w], in1=q[:, tt, w],
                                                       scale=1.0, scalar=0.0, op0=ALU.mult, op1=ALU.add,
                                                       accum_out=q_ss[:, tt * GRP + g:tt * GRP + g + 1])\
                            .then_inc(ring_out if g == GRP - 1 else ss_part, 1)
                dve.wait_ge(ss_part, (GRP - 1) * TT * (i + 1))
                dve.wait_ge(ring_out, first + TT)
                nc.vector.tensor_scalar(q_ms[:], q_ss[:], 1.0 / HD, RMS_EPS, ALU.mult, ALU.add).then_inc(ms_made, 1)

            def query_scales(i):
                dve.wait_ge(inv_made, i + 1)
                nc.vector.tensor_scalar(q_rms[:], q_inv[:], X_SCALE, None, ALU.mult).then_inc(rms_made, 1)
                dve.wait_ge(rms_made, i + 1)

            def split_queries(first, bank_of, i):
                for g in range(GRP):
                    dve.wait_ge(qt_his, GRP * i + g + 1)
                    nc.vector.tensor_tensor(qT_lo[:, g, :], bank[:, bank_of(g), :], f32(qT_hi[:, g, :]), ALU.subtract)\
                        .then_inc(ring_out, 1)

            def shift(n, u, j):
                s = UT * (u % 2) + j
                dve.wait_ge(s_full, n + 1)
                nc.vector.reduce_max(mx[:, s:s + 1], bank[:, 2 * (j % 2):2 * (j % 2) + 2, 0:HALF], AX.XY)\
                    .then_inc(mx_made, 1)
                dve.wait_ge(mx_made, n + 1)
                nc.vector.tensor_scalar(nm[:, s:s + 1], mx[:, s:s + 1], q_rms[:, column(u, j)], -1.0,
                                        ALU.mult, ALU.mult).then_inc(nm_made, 1)

            def invert_sum(n, u, j):
                s = UT * (u % 2) + j
                dve.wait_ge(exp_made, n + 1)
                nc.vector.reciprocal(rinv[:, s:s + 1], rsum[:, s:s + 1]).then_inc(rinv_made, 1)

            mean_squares(0, lambda a: 4 + a % RING, 0)
            split_queries(TT, lambda a: 4 + (TT + a) % RING, 0)
            query_scales(0)
            for j in range(UT):
                shift(j, 0, j)
                invert_sum(j, 0, j)

            def add_output(turn, b):
                for r in range(2):
                    tt = 2 * b + r
                    dve.wait_ge(ring_full, turn.output[b] + r + 1)
                    nc.vector.tensor_tensor(x[:, tt, :], bank[:, turn.bank("W", b, r), :], x[:, tt, :], ALU.add)\
                        .then_inc(ring_out, 1)

            def body(turn):
                i = turn.i
                for s in range(UNITS):
                    u = (s + 1) % UNITS
                    n = TILES * i + UT * (s + 1)
                    scores = not (turn.last and s == UNITS - 1)
                    for what, a in STEP:
                        if what == "S" and scores:
                            shift(n + a, u, a)
                        elif what == "T":
                            dve.wait_ge(pt_his, KTL * (UNITS * i + s) + a + 1)
                            nc.vector.tensor_tensor(pT_lo[:, a, :], bank[:, turn.bank("T", s, a), :],
                                                    f32(pT_hi[:, a, :]), ALU.subtract).then_inc(ring_out, 1)
                            if a in SUM_AFTER and scores:
                                invert_sum(n + SUM_AFTER[a], u, SUM_AFTER[a])
                    dve.wait_ge(o_his, UNITS * i + s + 1)
                    g, rows = 2 * (s % 2), slice(s // 2 * S, (s // 2 + 1) * S)
                    nc.vector.tensor_tensor(oT_lo[:, g:g + 2, rows], bank[:, 7, :].rearrange("p (g t) -> p g t", g=2),
                                            f32(oT_hi[:, g:g + 2, rows]), ALU.subtract).then_inc(o_out, 1)
                    if s == 1 and not turn.last:
                        mean_squares(turn.queries, lambda a: turn.bank("Q", 0, a), i + 1)
                    if s == 2:
                        if not turn.last:
                            dve.wait_ge(exp_made, TILES * (i + 1))
                            query_scales(i + 1)
                            split_queries(turn.queries_T, lambda a: turn.bank("QT", 0, a), i + 1)
                        add_output(turn, 0)
                    if s == 3:
                        add_output(turn, 1)

            turns(dve, body)

        @block.tensor
        def _(pe):
            def ring_free(use):
                pe.wait_ge(ring_out, use - RING + 1)

            def queries(first, bank_of, i, early):
                pe.wait_ge(wq_split, PIECE * (i + 1))
                for tt in range(TT):
                    if not (early and tt < RING):
                        ring_free(first + tt)
                    for m in range(KT):
                        w = slice(tt * P, (tt + 1) * P)
                        last = three_passes(nc, bank[:, bank_of(tt), :], k.x1_hi[:, m, w], k.x1_lo[:, m, w],
                                            wq_hi[:, m, :], wq_lo[:, m, :], m == 0, m == KT - 1)
                    last.then_inc(ring_full, 1)

            def transposed_queries(first, bank_of, i):
                pe.wait_ge(q_out, TT * (i + 1))
                for g in range(GRP):
                    ring_free(first + g)
                    for tt in range(TT):
                        last = nc.tensor.transpose(bank[:, bank_of(g), tt * P:(tt + 1) * P],
                                                   q[:, tt, g * HD:(g + 1) * HD], ident[:])
                    last.then_inc(ring_full, 1)

            def scores(n, u, j, early):
                g, tt = tile_of(u, j)
                b, w = u // 2, slice(tt * P, (tt + 1) * P)
                if not early:
                    pe.wait_ge(exp_made, n - 1)
                for a_hi, k_part, start, stop in ((qT_hi, k_hi, True, False), (qT_hi, k_lo, False, False),
                                                  (qT_lo, k_hi, False, True)):
                    for c in range(2):
                        last = nc.tensor.matmul(bank[:, 2 * (j % 2) + c, 0:HALF], a_hi[:, g, w],
                                                k_part[:, b, c * HALF:(c + 1) * HALF], start=start, stop=stop)
                last.then_inc(s_full, 1)

            queries(0, lambda a: 4 + a % RING, 0, True)
            transposed_queries(TT, lambda a: 4 + (TT + a) % RING, 0)
            pe.wait_ge(ring_out, BEFORE)
            pe.wait_ge(k_split, PIECE)
            for j in range(UT):
                scores(j, 0, j, j < 2)

            def output(turn, b):
                pe.wait_ge(o_out, UNITS * turn.i + 2 * b + 2)
                for r in range(2):
                    w = slice((2 * b + r) * P, (2 * b + r + 1) * P)
                    ring_free(turn.output[b] + r)
                    for g in range(GRP):
                        last = three_passes(nc, bank[:, turn.bank("W", b, r), :], oT_hi[:, g, w], oT_lo[:, g, w],
                                            wo_hi[:, g, :], wo_lo[:, g, :], g == 0, g == GRP - 1)
                    last.then_inc(ring_full, 1)

            def body(turn):
                i = turn.i
                for s in range(UNITS):
                    u = (s + 1) % UNITS
                    b = s // 2
                    for what, a in STEP:
                        if what == "S" and not (turn.last and s == UNITS - 1):
                            if a == 0 and s == 1:
                                pe.wait_ge(k_split, PIECE * (i + 1))
                            if a == 0 and s == 3:
                                pe.wait_ge(k_split, PIECE * (i + 1) + PIECE // 2)
                                pe.wait_ge(ring_out, turn.queries_T + GRP)
                            scores(TILES * i + UT * (s + 1) + a, u, a, False)
                        elif what == "T":
                            if a == 0:
                                pe.wait_ge(prob_made, TILES * i + UT * (s + 1))
                            ring_free(turn.weights[s] + a)
                            for j in range(UT):
                                last = nc.tensor.transpose(bank[:, turn.bank("T", s, a), j * P:(j + 1) * P],
                                                           prob[:, UT * (s % 2) + j, a * P:(a + 1) * P], ident[:])
                            last.then_inc(ring_full, 1)
                        elif what == "O":
                            if a == 0:
                                if s > 0:
                                    pe.wait_ge(o_out, UNITS * i + s)
                                pe.wait_ge(v_split, PIECE * i + 2 * b + 2)
                            pe.wait_ge(ring_out, turn.weights[s] + a + 1)
                            w = slice(a * HD, (a + 1) * HD)
                            last = three_passes(nc, bank[:, 7, :], v_hi[:, b, w], v_lo[:, b, w],
                                                pT_hi[:, a, :], pT_lo[:, a, :], a == 0, a == KTL - 1)
                    last.then_inc(o_full, 1)
                    if s == 1 and not turn.last:
                        queries(turn.queries, lambda a: turn.bank("Q", 0, a), i + 1, False)
                    if s == 2:
                        if not turn.last:
                            transposed_queries(turn.queries_T, lambda a: turn.bank("QT", 0, a), i + 1)
                        pe.wait_ge(wo_split, PIECE * (i + 1))
                        output(turn, 0)
                    if s == 3:
                        output(turn, 1)

            turns(pe, body)


def feed_forward(nc, d, k):
    with ExitStack() as ctx:
        t = Tensors(nc, ctx)
        up = t.sb("up_w", [P, FH // HPT, FM])
        down = t.sb("down_w", [P, FH, FD])
        perm_i = t.sb("perm_i", [1, D], I32)
        perm_f = t.sb("perm_f", [1, D])
        perm_rows_i = t.sb("perm_rows_i", [KT, P], I32)
        perm_rows = t.sb("perm_rows", [KT, P])
        perm_cols = t.sb("perm_cols", [P, KT])
        index_row = t.sb("index_row", [P, D])
        index_col = t.sb("index_col", [P, KT])
        ones = t.sb("ones_row2", [1, P])
        gather = t.sb("gather", [P, KT, D], F32R)
        scatter = t.sb("scatter", [P, KT, D], F32R)
        xT_hi = t.sb("x2T_hi", [P, KT, TOK], F32R)
        xT_lo = t.sb("x2T_lo", [P, KT, TOK], F32R)
        tT = t.sb("tT", [P, KT, TOK])
        hid = t.sb("hid", [P, HPT, TOK])
        yT_hi = t.sb("yT_hi", [P, KT, TOK], F32R)
        yT_lo = t.sb("yT_lo", [P, KT, TOK], F32R)
        stats = t.sb("stats2", [P, TT, 6])
        mv = t.sb("mv2", [P, 2, TT, 2])
        std = t.sb("std2", [P, 2 * TT])
        rstd = t.sb("rstd2", [P, 2 * TT])
        x, bank, ident = k.x, k.bank, k.ident

        perm_in, up_in, down_in, out_stored = t.sem("perm_in"), t.sem("up_in"), t.sem("down_in"), t.sem("out_stored")
        index_made, perm_made, perm_ps, cols_out = t.sem("index_made"), t.sem("perm_made"), t.sem("perm_ps"), t.sem("cols_out")
        gather_made, scatter_made = t.sem("gather_made"), t.sem("scatter_made")
        y_sum, y_stats, y_mv = t.sem("y_sum2"), t.sem("y_stats2"), t.sem("y_mv2")
        std_made, rstd_made, ln_made = t.sem("std_made2"), t.sem("rstd_made2"), t.sem("ln_made2")
        xt_ps, xt_hi, xt_lo = t.sem("x2t_ps"), t.sem("x2t_hi"), t.sem("x2t_lo")
        t_ps, t_out = t.sem("t_ps"), t.sem("t_out")
        h_ps, h_out = t.sem("h_ps"), t.sem("h_out")
        y_ps, y_hi, y_lo, z_ps = t.sem("y_ps2"), t.sem("y_hi2"), t.sem("y_lo2"), t.sem("z_ps")
        block = ctx.enter_context(nc.Block())

        @block.sync
        def _(sp):
            sp.dma_start(perm_i[:], d["perm"].rearrange("(a n) -> a n", a=1)).then_inc(perm_in, 16)
            sp.dma_start(perm_rows_i[:], d["perm"].rearrange("(k p) -> k p", p=P)).then_inc(perm_in, 16)
            sp.dma_start(up[:], d["up"].rearrange("(t q) e m -> (q e) t m", q=HPT)).then_inc(up_in, 16)
            sp.dma_start(down[:], d["down"].rearrange("h m e -> m h e")).then_inc(down_in, 16)
            for i in range(TT):
                sp.wait_ge(ln_made, TT + i + 1)
                sp.dma_start(d["out"].rearrange("b s d -> (b s) d")[i * P:(i + 1) * P, :], x[:, i, :])\
                    .then_inc(out_stored, 16)
            sp.wait_ge(out_stored, 16 * TT)

        @block.gpsimd
        def _(pool):
            nc.gpsimd.memset(ones[:], 1.0).then_inc(index_made, 1)
            nc.gpsimd.iota(index_row[:], [[1, D]], base=0, channel_multiplier=0,
                           allow_small_or_imprecise_dtypes=True).then_inc(index_made, 1)
            nc.gpsimd.iota(index_col[:], [[P, KT]], base=0, channel_multiplier=1,
                           allow_small_or_imprecise_dtypes=True).then_inc(index_made, 1)

        @block.scalar
        def _(act):
            act.wait_ge(perm_ps, 1)
            nc.scalar.activation(perm_cols[:], bank[:, 7, 0:KT], ACT.Copy).then_inc(cols_out, 1)
            for i in range(TT):
                act.wait_ge(y_mv, i + 1)
                nc.scalar.activation(std[:, i:i + 1], mv[:, 0, i, 1:2], ACT.Sqrt, bias=k.ln_eps[:]).then_inc(std_made, 1)
            for i in range(KT):
                act.wait_ge(xt_ps, i + 1)
                nc.scalar.activation(xT_hi[:, i, :], bank[:, i, :], ACT.Copy).then_inc(xt_hi, 1)
            for i in range(KT):
                act.wait_ge(t_ps, i + 1)
                nc.scalar.activation(tT[:, i, :], bank[:, 4 + i, :], ACT.Copy).then_inc(t_out, 1)
            for h in range(FH):
                act.wait_ge(h_ps, h + 1)
                nc.scalar.activation(hid[:, h % HPT, :], bank[:, h % HPT, :], ACT.Gelu).then_inc(h_out, 1)
            for i in range(KT):
                act.wait_ge(y_ps, HPT * (i + 1))
                nc.scalar.activation(yT_hi[:, i, :], bank[:, 4 + i, :], ACT.Copy).then_inc(y_hi, 1)
            for i in range(TT):
                act.wait_ge(y_mv, TT + i + 1)
                nc.scalar.activation(std[:, TT + i:TT + i + 1], mv[:, 1, i, 1:2], ACT.Sqrt, bias=k.ln_eps[:])\
                    .then_inc(std_made, 1)

        @block.vector
        def _(dve):
            def statistics(r, i):
                nc.vector.bn_stats(stats[:, i, :], x[:, i, :]).then_inc(y_stats, 1)
                dve.wait_ge(y_stats, TT * r + i + 1)
                nc.vector.bn_aggr(mv[:, r, i, :], stats[:, i, :]).then_inc(y_mv, 1)

            def normalise(r, i):
                n = TT * r + i
                dve.wait_ge(std_made, n + 1)
                nc.vector.reciprocal(rstd[:, n:n + 1], std[:, n:n + 1]).then_inc(rstd_made, 1)
                dve.wait_ge(rstd_made, n + 1)
                nc.vector.tensor_scalar(x[:, i, :], x[:, i, :], mv[:, r, i, 0:1], rstd[:, n:n + 1],
                                        ALU.subtract, ALU.mult).then_inc(ln_made, 1)

            dve.wait_ge(perm_in, 32)
            nc.vector.tensor_copy(perm_f[:], perm_i[:]).then_inc(perm_made, 1)
            nc.vector.tensor_copy(perm_rows[:], perm_rows_i[:]).then_inc(perm_made, 1)
            for i in range(TT):
                statistics(0, i)
            for i in range(TT):
                normalise(0, i)
            dve.wait_ge(index_made, 3)
            dve.wait_ge(cols_out, 1)
            for i in range(KT):
                nc.vector.tensor_scalar(gather[:, i, :], bank[:, 6, :], index_col[:, i:i + 1], None, ALU.is_equal)\
                    .then_inc(gather_made, 1)
            for i in range(KT):
                dve.wait_ge(xt_hi, i + 1)
                nc.vector.tensor_tensor(xT_lo[:, i, :], bank[:, i, :], f32(xT_hi[:, i, :]), ALU.subtract)\
                    .then_inc(xt_lo, 1)
            for i in range(KT):
                nc.vector.tensor_scalar(scatter[:, i, :], index_row[:], perm_cols[:, i:i + 1], None, ALU.is_equal)\
                    .then_inc(scatter_made, 1)
            for i in range(KT):
                dve.wait_ge(y_hi, i + 1)
                nc.vector.tensor_tensor(yT_lo[:, i, :], bank[:, 4 + i, :], f32(yT_hi[:, i, :]), ALU.subtract)\
                    .then_inc(y_lo, 1)
            for i in range(TT):
                dve.wait_ge(z_ps, i + 1)
                nc.vector.tensor_tensor(x[:, i, :], bank[:, i, :], x[:, i, :], ALU.add).then_inc(y_sum, 1)
                dve.wait_ge(y_sum, i + 1)
                statistics(1, i)
            for i in range(TT):
                normalise(1, i)

        @block.tensor
        def _(pe):
            pe.wait_ge(perm_made, 2)
            pe.wait_ge(index_made, 1)
            nc.tensor.matmul(bank[:, 6, :], ones[:], perm_f[:], start=True, stop=True)
            nc.tensor.transpose(bank[:, 7, 0:KT], perm_rows[:], ident[0:KT, 0:KT]).then_inc(perm_ps, 1)
            pe.wait_ge(ln_made, TT)
            for i in range(KT):
                for j in range(TT):
                    last = nc.tensor.transpose(bank[:, i, j * P:(j + 1) * P], x[:, j, i * P:(i + 1) * P], ident[:])
                last.then_inc(xt_ps, 1)
            pe.wait_ge(gather_made, KT)
            pe.wait_ge(xt_lo, KT)
            for i in range(KT):
                for j in range(KT):
                    w = slice(i * P, (i + 1) * P)
                    nc.tensor.matmul(bank[:, 4 + i, :], gather[:, j, w], xT_hi[:, j, :], start=j == 0, stop=False)
                    last = nc.tensor.matmul(bank[:, 4 + i, :], gather[:, j, w], xT_lo[:, j, :], start=False,
                                            stop=j == KT - 1)
                last.then_inc(t_ps, 1)
            pe.wait_ge(up_in, 16)
            pe.wait_ge(down_in, 16)
            pe.wait_ge(t_out, KT)

            def up_product(h):
                r = FD * (h % HPT)
                if h >= HPT:
                    pe.wait_ge(h_out, h - HPT + 1)
                nc.tensor.matmul(bank[:, h % HPT, :], up[r:r + FD, h // HPT, :], tT[r:r + FD, h // HPT, :],
                                 start=True, stop=True).then_inc(h_ps, 1)

            def down_product(h):
                r = FD * (h % HPT)
                pe.wait_ge(h_out, h + 1)
                nc.tensor.matmul(bank[r:r + FD, 4 + h // HPT, :], down[:, h, :], hid[:, h % HPT, :],
                                 start=True, stop=True).then_inc(y_ps, 1)

            up_product(0)
            up_product(1)
            for h in range(FH):
                if h + 2 < FH:
                    up_product(h + 2)
                down_product(h)
            pe.wait_ge(y_lo, KT)
            pe.wait_ge(scatter_made, KT)
            for j in range(TT):
                w = slice(j * P, (j + 1) * P)
                for i in range(KT):
                    nc.tensor.matmul(bank[:, j, :], yT_hi[:, i, w], scatter[:, i, :], start=i == 0, stop=False)
                    last = nc.tensor.matmul(bank[:, j, :], yT_lo[:, i, w], scatter[:, i, :], start=False,
                                            stop=i == KT - 1)
                last.then_inc(z_ps, 1)


class Kept:
    pass


def build(nc, d):
    with ExitStack() as ctx:
        t = Tensors(nc, ctx)
        k = Kept()
        k.x = t.sb("x_rows", [P, TT, D])
        k.x1_hi = t.sb("x1_hi", [P, KT, TOK], F32R)
        k.x1_lo = t.sb("x1_lo", [P, KT, TOK], F32R)
        k.ident = t.sb("ident", [P, P])
        k.ln_eps = t.sb("ln_eps", [P, 1])
        k.rms_eps = t.sb("rms_eps", [P, 1])
        k.bank = ctx.enter_context(nc.psum_tensor("bank", [P, 8, 512], F32))
        k.kT_dram = nc.dram_tensor("kT_by_head", [KVH, HD, B * KEYS], F32, kind="Internal").ap()
        k.v_dram = nc.dram_tensor("v_by_head", [KVH, P, B * KEYS], F32, kind="Internal").ap()
        self_attention(nc, d, k)
        keys_values(nc, d, k)
        cross_attention(nc, d, k)
        feed_forward(nc, d, k)


_INS = {"x": "x", "ctx": "ctx_4096", "w_attn": "L0_attn_w_attn", "b_attn": "L0_attn_b_attn",
        "w_proj": "L0_attn_w_proj", "b_proj": "L0_attn_b_proj", "Wq": "L0_xattn_Wq", "Wk": "L0_xattn_Wk",
        "Wv": "L0_xattn_Wv", "Wo": "L0_xattn_Wo", "q_norm": "L0_xattn_q_norm_w", "k_norm": "L0_xattn_k_norm_w",
        "up": "L0_ffn_up", "down": "L0_ffn_down", "perm": "L0_ffn_perm"}


def kernel(**inputs):
    import numpy as np
    import concourse.bacc as bacc
    from concourse.bass_utils import run_bass_kernel_spmd

    nc = bacc.Bacc("TRN2", target_bir_lowering=False, num_devices=1)
    arrays, d = {}, {}
    for name, given in _INS.items():
        a = np.ascontiguousarray(inputs[given])
        arrays[f"in_{name}"] = a
        d[name] = nc.dram_tensor(f"in_{name}", a.shape, mybir.dt.from_np(a.dtype), kind="ExternalInput").ap()
    d["out"] = nc.dram_tensor("out", (B, S, D), F32, kind="ExternalOutput").ap()
    build(nc, d)
    return run_bass_kernel_spmd(nc, [arrays], core_ids=[0]).results[0]["out"]
```

```python
from contextlib import ExitStack

import concourse.bass as bass
from concourse import mybir

P = 128
ALU = mybir.AluOpType
ACT = mybir.ActivationFunctionType
AX = mybir.AxisListType
F32 = mybir.dt.float32
F32R = mybir.dt.float32r
I32 = mybir.dt.int32

B, S, D = 2, 256, 512
TOK = B * S
TT = TOK // P
KT = D // P
C = 512
CT = C // P
LN_EPS = 1e-5

SA_HEADS, SA_DIM = 32, 16
SA_SCALE = 1.0 / SA_DIM
SLOPES = [2.0 ** (-(h + 1) / 4) for h in range(SA_HEADS)]
MASKED = -1e36

XH, KVH, HD = 32, 8, 128
GRP = XH // KVH
KEYS = C + S
KTL = KEYS // P
HALF = KEYS // 2
X_SCALE = float(HD) ** -0.5
RMS_EPS = 1e-6

FH, FD, FM = 16, 32, 128
HPT = P // FD


def three_passes(nc, out, a_hi, a_lo, b_hi, b_lo, first, last):
    nc.tensor.matmul(out, a_hi, b_hi, start=first, stop=False)
    nc.tensor.matmul(out, a_hi, b_lo, start=False, stop=False)
    return nc.tensor.matmul(out, a_lo, b_hi, start=False, stop=last)


def f32(ap):
    return ap.bitcast(F32)


class Tensors:

    def __init__(self, nc, ctx):
        self.nc, self.ctx = nc, ctx

    def sb(self, name, shape, dt=F32):
        return self.ctx.enter_context(self.nc.sbuf_tensor(name, shape, dt))

    def sem(self, name):
        return self.ctx.enter_context(self.nc.semaphore(name))


def self_attention(nc, d, k):
    with ExitStack() as ctx:
        t = Tensors(nc, ctx)
        xT_hi = t.sb("xT_hi", [P, KT, TOK], F32R)
        xT_lo = t.sb("xT_lo", [P, KT, TOK], F32R)
        wa_raw = t.sb("wa_raw", [P, 2, 3 * D])
        wa_hi = t.sb("wa_hi", [P, KT, 3 * D], F32R)
        wa_lo = t.sb("wa_lo", [P, KT, 3 * D], F32R)
        wp_raw = t.sb("wp_raw", [P, KT, D])
        wp_hi = t.sb("wp_hi", [P, KT, D], F32R)
        wp_lo = t.sb("wp_lo", [P, KT, D], F32R)
        qT = t.sb("qT", [P, KT, TOK])
        kT_even = t.sb("kT_even", [P, KT, TOK])
        kT_odd = t.sb("kT_odd", [P, KT, TOK])
        v = t.sb("v_self", [P, TT, D])
        att = t.sb("att", [P, TT, D])
        qk_bias_rows = t.sb("qk_bias_rows", [2 * KT, P])
        qk_bias = t.sb("qk_bias", [P, 2 * KT])
        row_bias = t.sb("row_bias", [1, 2 * D])
        ones = t.sb("ones_row", [1, P])
        even = t.sb("even", [P, 1])
        odd = t.sb("odd", [P, 1])
        rel = t.sb("rel", [P, S])
        bias = t.sb("alibi", [P, 2, S])
        s_sb = t.sb("s_self", [P, 2, 3 * P])
        p_sb = t.sb("p_self", [P, 2, 3 * P])
        pT = t.sb("pT_self", [P, 2, 3 * P])
        mx = t.sb("mx_self", [P, 2, 2])
        nm = t.sb("nm_self", [P, 2, 2])
        rsum = t.sb("rsum_self", [P, TT, SA_HEADS])
        rinv = t.sb("rinv_self", [P, TT, SA_HEADS])
        stats = t.sb("stats1", [P, TT, 6])
        mv = t.sb("mv1", [P, TT, 2])
        std = t.sb("std1", [P, TT])
        rstd = t.sb("rstd1", [P, TT])
        x, bank, ident = k.x, k.bank, k.ident

        x_in, bias_in, wp_in = t.sem("x_in"), t.sem("bias_in"), t.sem("wp_in")
        wa_in = [t.sem("wa_in0"), t.sem("wa_in1")]
        const = t.sem("const_ready")
        mask = t.sem("mask_ready")
        xt_ps, xt_hi, xt_lo = t.sem("xt_ps"), t.sem("xt_hi"), t.sem("xt_lo")
        wa_his, wa_los = t.sem("wa_his"), t.sem("wa_los")
        wp_his, wp_los = t.sem("wp_his"), t.sem("wp_los")
        bt_ps, bt_out = t.sem("bt_ps"), t.sem("bt_out")
        qk_ps, q_out, k_out = t.sem("qk_ps"), t.sem("q_out"), t.sem("k_out")
        v_ps, v_out = t.sem("v_ps"), t.sem("v_out")
        bias_made = t.sem("alibi_made")
        s_ps, s_half, s_out = t.sem("s_ps_self"), t.sem("s_half_self"), t.sem("s_out_self")
        nm_made = t.sem("nm_made_self")
        p_made = t.sem("p_made_self")
        pt_ps, pt_out, o_ps = t.sem("pt_ps_self"), t.sem("pt_out_self"), t.sem("o_ps_self")
        rinv_made, att_out = t.sem("rinv_made_self"), t.sem("att_out")
        at_ps, at_hi, at_lo = t.sem("at_ps_self"), t.sem("at_hi_self"), t.sem("at_lo_self")
        y_ps, y_sum, y_stats, y_mv = t.sem("y_ps1"), t.sem("y_sum1"), t.sem("y_stats1"), t.sem("y_mv1")
        std_made, rstd_made, x1_made = t.sem("std_made1"), t.sem("rstd_made1"), t.sem("x1_made")
        x1t_ps, x1t_hi, x1t_lo = t.sem("x1t_ps"), t.sem("x1t_hi"), t.sem("x1t_lo")
        block = ctx.enter_context(nc.Block())

        heads = [(h, b) for h in range(SA_HEADS) for b in range(B)]
        N = len(heads)

        @block.sync
        def _(sp):
            for i in range(TT):
                sp.dma_start(x[:, i, :], d["x"].rearrange("b s d -> (b s) d")[i * P:(i + 1) * P, :])\
                    .then_inc(x_in, 16)
            sp.dma_start(qk_bias_rows[:], d["b_attn"][0:2 * D].rearrange("(m p) -> m p", p=P)).then_inc(bias_in, 16)
            sp.dma_start(row_bias[:, 0:D], d["b_attn"][2 * D:3 * D].rearrange("(a n) -> a n", a=1)).then_inc(bias_in, 16)
            sp.dma_start(row_bias[:, D:2 * D], d["b_proj"].rearrange("(a n) -> a n", a=1)).then_inc(bias_in, 16)
            for i in range(KT):
                if i >= 2:
                    sp.wait_ge(wa_los, i - 1)
                sp.dma_start(wa_raw[:, i % 2, :], d["w_attn"][i * P:(i + 1) * P, :]).then_inc(wa_in[i % 2], 16)
            sp.dma_start(wp_raw[:], d["w_proj"].rearrange("(k p) n -> p k n", p=P)).then_inc(wp_in, 16)

        @block.gpsimd
        def _(pool):
            nc.gpsimd.memset(ident[:], 0.0).then_inc(const, 1)
            nc.gpsimd.iota(rel[:], [[1, S]], base=-P, channel_multiplier=-1,
                           allow_small_or_imprecise_dtypes=True).then_inc(const, 1)
            nc.gpsimd.memset(ones[:], 1.0).then_inc(const, 1)
            pool.wait_ge(const, 3)
            nc.gpsimd.affine_select(out=ident[:], in_=ident[:], compare_op=ALU.not_equal, fill=1.0, base=0,
                                    pattern=[[-1, P]], channel_multiplier=1).then_inc(const, 1)
            nc.gpsimd.affine_select(out=rel[:], in_=rel[:], compare_op=ALU.is_ge, fill=MASKED, base=P,
                                    pattern=[[-1, S]], channel_multiplier=1).then_inc(const, 1)
            pool.wait_ge(const, 5)
            for h in range(SA_HEADS):
                if h >= 2:
                    pool.wait_ge(s_out, 2 * (h - 1))
                nc.gpsimd.tensor_scalar(bias[:, h % 2, :], rel[:], SLOPES[h] / SA_SCALE, 1.0, ALU.mult, ALU.mult)\
                    .then_inc(bias_made, 1)

        @block.scalar
        def _(act):
            act.wait_ge(bt_ps, 1)
            nc.scalar.activation(qk_bias[:], bank[:, 4, 0:2 * KT], ACT.Copy).then_inc(bt_out, 1)
            for i in range(KT):
                act.wait_ge(xt_ps, i + 1)
                nc.scalar.activation(xT_hi[:, i, :], bank[:, i, :], ACT.Copy).then_inc(xt_hi, 1)
            for i in range(KT):
                act.wait_ge(wa_in[i % 2], 16 * (i // 2 + 1))
                nc.scalar.activation(wa_hi[:, i, :], wa_raw[:, i % 2, :], ACT.Copy).then_inc(wa_his, 1)
            act.wait_ge(bt_out, 1)
            for m in range(KT):
                act.wait_ge(qk_ps, m + 1)
                nc.scalar.activation(qT[:, m, :], bank[:, 4 + m, :], ACT.Identity, bias=qk_bias[:, m:m + 1])\
                    .then_inc(q_out, 1)
            act.wait_ge(wp_in, 16)
            nc.scalar.activation(wp_hi[:], wp_raw[:], ACT.Copy).then_inc(wp_his, 1)
            for i in range(TT):
                act.wait_ge(v_ps, i + 1)
                nc.scalar.activation(v[:, i, :], bank[:, 4 + i, :], ACT.Copy).then_inc(v_out, 1)
            for n, (h, b) in enumerate(heads):
                act.wait_ge(nm_made, n + 1)
                if n >= 2:
                    act.wait_ge(pt_ps, n - 1)
                for qt, (a, e) in enumerate(((0, P), (P, 3 * P))):
                    nc.scalar.activation(p_sb[:, n % 2, a:e], s_sb[:, n % 2, a:e], ACT.Exp,
                                         bias=nm[:, n % 2, qt:qt + 1], scale=SA_SCALE,
                                         accum_out=rsum[:, 2 * b + qt, h:h + 1]).then_inc(p_made, 1)
            for i in range(KT):
                act.wait_ge(at_ps, i + 1)
                nc.scalar.activation(xT_hi[:, i, :], bank[:, i, :], ACT.Copy).then_inc(at_hi, 1)
            for i in range(TT):
                act.wait_ge(y_mv, i + 1)
                nc.scalar.activation(std[:, i:i + 1], mv[:, i, 1:2], ACT.Sqrt, bias=k.ln_eps[:]).then_inc(std_made, 1)
            for i in range(KT):
                act.wait_ge(x1t_ps, i + 1)
                nc.scalar.activation(k.x1_hi[:, i, :], bank[:, i, :], ACT.Copy).then_inc(x1t_hi, 1)

        @block.vector
        def _(dve):
            nc.vector.memset(even[:], 0.0).then_inc(mask, 1)
            nc.vector.memset(k.ln_eps[:], LN_EPS).then_inc(mask, 1)
            nc.vector.memset(k.rms_eps[:], RMS_EPS).then_inc(mask, 1)
            dve.wait_ge(mask, 3)
            for g in range(P // 32):
                nc.vector.memset(even[32 * g:32 * g + SA_DIM, :], 1.0).then_inc(mask, 1)
            dve.wait_ge(mask, 7)
            nc.vector.tensor_scalar(odd[:], even[:], -1.0, 1.0, ALU.mult, ALU.add).then_inc(mask, 1)
            for i in range(KT):
                dve.wait_ge(xt_hi, i + 1)
                nc.vector.tensor_tensor(xT_lo[:, i, :], bank[:, i, :], f32(xT_hi[:, i, :]), ALU.subtract)\
                    .then_inc(xt_lo, 1)
            for i in range(KT):
                dve.wait_ge(wa_his, i + 1)
                nc.vector.tensor_tensor(wa_lo[:, i, :], wa_raw[:, i % 2, :], f32(wa_hi[:, i, :]), ALU.subtract)\
                    .then_inc(wa_los, 1)
            dve.wait_ge(mask, 8)
            dve.wait_ge(bt_out, 1)
            for m in range(KT):
                dve.wait_ge(qk_ps, KT + m + 1)
                for dst, keep in ((kT_even, even), (kT_odd, odd)):
                    nc.vector.tensor_scalar(dst[:, m, :], bank[:, 4 + m, :], qk_bias[:, KT + m:KT + m + 1],
                                            keep[:], ALU.add, ALU.mult).then_inc(k_out, 1)
            dve.wait_ge(wp_his, 1)
            nc.vector.tensor_tensor(wp_lo[:], wp_raw[:], f32(wp_hi[:]), ALU.subtract).then_inc(wp_los, 1)

            def softmax_shift(n):
                h = heads[n][0]
                dve.wait_ge(s_ps, n + 1)
                dve.wait_ge(bias_made, h + 1)
                if n >= 2:
                    dve.wait_ge(p_made, 2 * (n - 1))
                for qt, (a, e, rel0) in enumerate(((0, P, P), (P, 3 * P, 0))):
                    nc.vector.tensor_tensor_reduce(out=s_sb[:, n % 2, a:e], in0=bank[:, n % 2, a:e],
                                                   in1=bias[:, h % 2, rel0:S], scale=1.0, scalar=-3e38,
                                                   op0=ALU.add, op1=ALU.max,
                                                   accum_out=mx[:, n % 2, qt:qt + 1])\
                        .then_inc(s_out if qt else s_half, 1)
                dve.wait_ge(s_half, n + 1)
                dve.wait_ge(s_out, n + 1)
                nc.vector.tensor_scalar(nm[:, n % 2, :], mx[:, n % 2, :], -SA_SCALE, None, ALU.mult)\
                    .then_inc(nm_made, 1)

            def take_transposed(n):
                dve.wait_ge(pt_ps, n + 1)
                if n >= 2:
                    dve.wait_ge(o_ps, n - 1)
                nc.vector.tensor_copy(pT[:, n % 2, :], bank[:, 2 + n % 2, 0:3 * P]).then_inc(pt_out, 1)

            softmax_shift(0)
            for n in range(N):
                if n + 1 < N:
                    softmax_shift(n + 1)
                take_transposed(n)
            dve.wait_ge(p_made, 2 * N)
            nc.vector.reciprocal(rinv[:], rsum[:]).then_inc(rinv_made, 1)
            dve.wait_ge(rinv_made, 1)
            dve.wait_ge(o_ps, N)
            for i in range(TT):
                nc.vector.tensor_tensor(att[:, i, :].rearrange("p (h e) -> p h e", h=SA_HEADS),
                                        bank[:, 4 + i, :].rearrange("p (h e) -> p h e", h=SA_HEADS),
                                        rinv[:, i, :].rearrange("p (h a) -> p h a", a=1)
                                        .to_broadcast([P, SA_HEADS, SA_DIM]), ALU.mult).then_inc(att_out, 1)
            for i in range(KT):
                dve.wait_ge(at_hi, i + 1)
                nc.vector.tensor_tensor(xT_lo[:, i, :], bank[:, i, :], f32(xT_hi[:, i, :]), ALU.subtract)\
                    .then_inc(at_lo, 1)
            for i in range(TT):
                dve.wait_ge(y_ps, i + 1)
                nc.vector.tensor_tensor(x[:, i, :], bank[:, 4 + i, :], x[:, i, :], ALU.add).then_inc(y_sum, 1)
                dve.wait_ge(y_sum, i + 1)
                nc.vector.bn_stats(stats[:, i, :], x[:, i, :]).then_inc(y_stats, 1)
                dve.wait_ge(y_stats, i + 1)
                nc.vector.bn_aggr(mv[:, i, :], stats[:, i, :]).then_inc(y_mv, 1)
            for i in range(TT):
                dve.wait_ge(std_made, i + 1)
                nc.vector.reciprocal(rstd[:, i:i + 1], std[:, i:i + 1]).then_inc(rstd_made, 1)
                dve.wait_ge(rstd_made, i + 1)
                nc.vector.tensor_scalar(x[:, i, :], x[:, i, :], mv[:, i, 0:1], rstd[:, i:i + 1],
                                        ALU.subtract, ALU.mult).then_inc(x1_made, 1)
            for i in range(KT):
                dve.wait_ge(x1t_hi, i + 1)
                nc.vector.tensor_tensor(k.x1_lo[:, i, :], bank[:, i, :], f32(k.x1_hi[:, i, :]), ALU.subtract)\
                    .then_inc(x1t_lo, 1)

        @block.tensor
        def _(pe):
            pe.wait_ge(const, 5)
            pe.wait_ge(bias_in, 48)
            nc.tensor.transpose(bank[:, 4, 0:2 * KT], qk_bias_rows[:], ident[0:2 * KT, 0:2 * KT]).then_inc(bt_ps, 1)
            pe.wait_ge(x_in, 16 * TT)
            for i in range(KT):
                for j in range(TT):
                    last = nc.tensor.transpose(bank[:, i, j * P:(j + 1) * P], x[:, j, i * P:(i + 1) * P], ident[:])
                last.then_inc(xt_ps, 1)
            pe.wait_ge(wa_los, KT)
            pe.wait_ge(xt_lo, KT)
            for m in range(2 * KT):
                if m == 0:
                    pe.wait_ge(bt_out, 1)
                if m >= KT:
                    pe.wait_ge(q_out, m - KT + 1)
                for i in range(KT):
                    w = slice(m * P, (m + 1) * P)
                    last = three_passes(nc, bank[:, 4 + m % KT, :], wa_hi[:, i, w], wa_lo[:, i, w],
                                        xT_hi[:, i, :], xT_lo[:, i, :], i == 0, i == KT - 1)
                last.then_inc(qk_ps, 1)
            for j in range(TT):
                pe.wait_ge(k_out, 2 * (j + 1))
                nc.tensor.matmul(bank[:, 4 + j, :], ones[:], row_bias[:, 0:D], start=True, stop=False)
                for i in range(KT):
                    w = slice(j * P, (j + 1) * P)
                    last = three_passes(nc, bank[:, 4 + j, :], xT_hi[:, i, w], xT_lo[:, i, w],
                                        wa_hi[:, i, 2 * D:3 * D], wa_lo[:, i, 2 * D:3 * D], False, i == KT - 1)
                last.then_inc(v_ps, 1)

            def scores(n):
                h, b = heads[n]
                m, r = h // 8, 32 * (h % 8 // 2)
                keys = kT_odd if h % 2 else kT_even
                if n >= 2:
                    pe.wait_ge(s_out, n - 1)
                nc.tensor.matmul(bank[:, n % 2, 0:P], qT[r:r + 32, m, b * S:b * S + P],
                                 keys[r:r + 32, m, b * S:b * S + P], start=True, stop=True)
                nc.tensor.matmul(bank[:, n % 2, P:3 * P], qT[r:r + 32, m, b * S + P:b * S + S],
                                 keys[r:r + 32, m, b * S:b * S + S], start=True, stop=True).then_inc(s_ps, 1)

            def transposes(n):
                pe.wait_ge(p_made, 2 * (n + 1))
                if n >= 2:
                    pe.wait_ge(pt_out, n - 1)
                for j in range(3):
                    last = nc.tensor.transpose(bank[:, 2 + n % 2, j * P:(j + 1) * P],
                                               p_sb[:, n % 2, j * P:(j + 1) * P], ident[:])
                last.then_inc(pt_ps, 1)

            def weigh_values(n):
                h, b = heads[n]
                w = slice(h * SA_DIM, (h + 1) * SA_DIM)
                pe.wait_ge(pt_out, n + 1)
                for qt, kt, start, stop in ((0, 0, True, True), (1, 0, True, False), (1, 1, False, True)):
                    last = nc.tensor.matmul(bank[:, 4 + 2 * b + qt, w], pT[:, n % 2, (qt + kt) * P:(qt + kt + 1) * P],
                                            v[:, 2 * b + kt, w], start=start, stop=stop)
                last.then_inc(o_ps, 1)

            pe.wait_ge(v_out, TT)
            scores(0)
            for n in range(N):
                if n + 1 < N:
                    scores(n + 1)
                if n >= 1:
                    weigh_values(n - 1)
                transposes(n)
            weigh_values(N - 1)
            pe.wait_ge(pt_out, N)
            for i in range(KT):
                pe.wait_ge(att_out, TT)
                for j in range(TT):
                    last = nc.tensor.transpose(bank[:, i, j * P:(j + 1) * P], att[:, j, i * P:(i + 1) * P], ident[:])
                last.then_inc(at_ps, 1)
            pe.wait_ge(wp_los, 1)
            pe.wait_ge(at_lo, KT)
            for j in range(TT):
                nc.tensor.matmul(bank[:, 4 + j, :], ones[:], row_bias[:, D:2 * D], start=True, stop=False)
                for i in range(KT):
                    w = slice(j * P, (j + 1) * P)
                    last = three_passes(nc, bank[:, 4 + j, :], xT_hi[:, i, w], xT_lo[:, i, w],
                                        wp_hi[:, i, :], wp_lo[:, i, :], False, i == KT - 1)
                last.then_inc(y_ps, 1)
            pe.wait_ge(x1_made, TT)
            for i in range(KT):
                for j in range(TT):
                    last = nc.tensor.transpose(bank[:, i, j * P:(j + 1) * P], x[:, j, i * P:(i + 1) * P], ident[:])
                last.then_inc(x1t_ps, 1)


def keys_values(nc, d, k):
    with ExitStack() as ctx:
        t = Tensors(nc, ctx)
        w_raw = t.sb("wkv_raw", [P, 2, KVH * HD])
        w_hi = t.sb("wkv_hi", [P, 2, KT, KVH * HD], F32R)
        w_lo = t.sb("wkv_lo", [P, 2, KT, KVH * HD], F32R)
        c_raw = t.sb("c_raw", [P, 2, D])
        cT_hi = t.sb("cT_hi", [P, 2, KT, P], F32R)
        cT_lo = t.sb("cT_lo", [P, 2, KT, P], F32R)
        k_raw = t.sb("k_raw", [P, KVH, HD])
        k_sq = t.sb("k_sq", [P, KVH, HD])
        k_ss = t.sb("k_ss", [P, KVH])
        k_std = t.sb("k_std", [P, KVH])
        k_inv = t.sb("k_inv", [P, KVH])
        k_nrm = t.sb("k_nrm", [P, KVH, HD])
        kT_st = t.sb("kT_st", [P, 2, KVH, P])
        v_st = t.sb("v_st", [P, 2, KVH, HD])
        nw_rows = t.sb("nw_rows", [2, HD])
        nw_cols = t.sb("nw_cols", [P, 2])
        nw = t.sb("nw", [P, 1])
        bank, ident = k.bank, k.ident

        nw_in = t.sem("nw_in")
        nw_ps, nw_out, nw_made = t.sem("nw_ps"), t.sem("nw_out"), t.sem("nw_made")
        w_in = [t.sem("wkv_in0"), t.sem("wkv_in1")]
        w_his, w_los = t.sem("wkv_his"), t.sem("wkv_los")
        c_in = [t.sem("c_in0"), t.sem("c_in1")]
        ct_ps, ct_hi, ct_lo = t.sem("ct_ps"), t.sem("ct_hi"), t.sem("ct_lo")
        k_ps, k_out, ksq_made, kss_made = t.sem("k_ps"), t.sem("k_out2"), t.sem("ksq_made"), t.sem("kss_made")
        kstd_made, kinv_made, knrm_made = t.sem("kstd_made"), t.sem("kinv_made"), t.sem("knrm_made")
        v_ps, v_out = t.sem("v_ps2"), t.sem("v_out2")
        kt_ps, kt_out = t.sem("kt_ps"), t.sem("kt_out")
        k_store = [t.sem("k_store0"), t.sem("k_store1")]
        v_store = [t.sem("v_store0"), t.sem("v_store1")]
        block = ctx.enter_context(nc.Block())

        LAT = S // P
        LAST = CT + LAT - 1

        def all_tiles(eng, step):
            for b in range(B):
                step(0, b, True, True, True)
            with eng.Fori(1, CT - 1) as c:
                for b in range(B):
                    step(c, b, False, True, True)
            for c in range(CT - 1, CT + LAT):
                for b in range(B):
                    step(c, b, False, c < CT, c < CT and b == 0)

        def context_rows(b, c):
            return d["ctx"].rearrange("b (c p) d -> b c p d", p=P)[b, c, :, :]

        @block.sync
        def _(sp):
            sp.dma_start(nw_rows[0:1, :], d["q_norm"].rearrange("(a n) -> a n", a=1)).then_inc(nw_in, 16)
            sp.dma_start(nw_rows[1:2, :], d["k_norm"].rearrange("(a n) -> a n", a=1)).then_inc(nw_in, 16)
            for b in range(B):
                sp.dma_start(c_raw[:, b, :], context_rows(b, 0)).then_inc(c_in[b], 16)
            for n in range(2 * KT):
                if n >= 2:
                    sp.wait_ge(w_los, n - 1)
                src = d["Wk"] if n < KT else d["Wv"]
                sp.dma_start(w_raw[:, n % 2, :], src[n % KT * P:(n % KT + 1) * P, :]).then_inc(w_in[n % 2], 16)

            v_view = k.v_dram.rearrange("h p (n e) -> p h n e", e=HD)
            k_view = k.kT_dram.rearrange("h p (n e) -> p h n e", e=P)

            def step(c, b, early, context, following):
                if context and not (isinstance(c, int) and c == CT - 1):
                    sp.wait_ge(ct_ps, 2 * c + b + 1)
                    sp.dma_start(c_raw[:, b, :], context_rows(b, c + 1)).then_inc(c_in[b], 16)
                sp.wait_ge(v_out, 2 * c + b + 1)
                sp.dma_start(v_view[:, :, b * KTL + c, :], v_st[:, b, :, :]).then_inc(v_store[b], 16)
                sp.wait_ge(kt_out, 2 * c + b + 1)
                sp.dma_start(k_view[:, :, b * KTL + c, :], kT_st[:, b, :, :]).then_inc(k_store[b], 16)

            all_tiles(sp, step)
            for b in range(B):
                sp.wait_ge(v_store[b], 16 * (LAST + 1))
                sp.wait_ge(k_store[b], 16 * (LAST + 1))

        @block.scalar
        def _(act):
            def context_hi(n, b, early):
                act.wait_ge(ct_ps, n + 1)
                if not early:
                    act.wait_ge(v_ps, n - 1)
                nc.scalar.activation(cT_hi[:, b, :, :], bank[:, 6, :].rearrange("p (k t) -> p k t", k=KT), ACT.Copy)\
                    .then_inc(ct_hi, 1)

            act.wait_ge(nw_ps, 1)
            nc.scalar.activation(nw_cols[:], bank[:, 0, 0:2], ACT.Copy).then_inc(nw_out, 1)
            for n in range(2 * KT):
                act.wait_ge(w_in[n % 2], 16 * (n // 2 + 1))
                nc.scalar.activation(w_hi[:, n // KT, n % KT, :], w_raw[:, n % 2, :], ACT.Copy).then_inc(w_his, 1)
                if n == 0:
                    context_hi(0, 0, True)
            act.wait_ge(nw_made, 1)

            def step(c, b, early, context, following):
                n = 2 * c + b
                act.wait_ge(k_ps, n + 1)
                nc.scalar.activation(k_raw[:].rearrange("p (a h) e -> p a (h e)", a=2), bank[:, 2 * b:2 * b + 2, :],
                                     ACT.Copy).then_inc(k_out, 1)
                act.wait_ge(k_out, n + 1)
                nc.scalar.activation(k_sq[:], k_raw[:], ACT.Square).then_inc(ksq_made, 1)
                act.wait_ge(kss_made, n + 1)
                nc.scalar.activation(k_std[:], k_ss[:], ACT.Sqrt, bias=k.rms_eps[:], scale=1.0 / HD)\
                    .then_inc(kstd_made, 1)
                if following:
                    context_hi(n + 1, 1 - b, early and b == 0)
                act.wait_ge(kt_ps, n + 1)
                if not early:
                    act.wait_ge(k_store[b], 16 * c)
                nc.scalar.activation(kT_st[:, b, :, :].rearrange("p (a h) e -> p a (h e)", a=2), bank[:, 6:8, :],
                                     ACT.Copy, scale=nw[:]).then_inc(kt_out, 1)

            all_tiles(act, step)

        @block.vector
        def _(dve):
            def context_lo(n, b):
                dve.wait_ge(ct_hi, n + 1)
                nc.vector.tensor_tensor(cT_lo[:, b, :, :], bank[:, 6, :].rearrange("p (k t) -> p k t", k=KT),
                                        f32(cT_hi[:, b, :, :]), ALU.subtract).then_inc(ct_lo, 1)

            dve.wait_ge(nw_out, 1)
            nc.vector.tensor_tensor(nw[:], nw_cols[:, 0:1], nw_cols[:, 1:2], ALU.mult).then_inc(nw_made, 1)
            for n in range(2 * KT):
                dve.wait_ge(w_his, n + 1)
                nc.vector.tensor_tensor(w_lo[:, n // KT, n % KT, :], w_raw[:, n % 2, :],
                                        f32(w_hi[:, n // KT, n % KT, :]), ALU.subtract).then_inc(w_los, 1)
                if n == 0:
                    context_lo(0, 0)

            def step(c, b, early, context, following):
                n = 2 * c + b
                dve.wait_ge(ksq_made, n + 1)
                nc.vector.tensor_reduce(k_ss[:], k_sq[:], AX.X, ALU.add).then_inc(kss_made, 1)
                dve.wait_ge(kstd_made, n + 1)
                nc.vector.reciprocal(k_inv[:], k_std[:]).then_inc(kinv_made, 1)
                dve.wait_ge(kinv_made, n + 1)
                nc.vector.tensor_tensor(k_nrm[:], k_raw[:], k_inv[:].rearrange("p (h a) -> p h a", a=1)
                                        .to_broadcast([P, KVH, HD]), ALU.mult).then_inc(knrm_made, 1)
                if following:
                    context_lo(n + 1, 1 - b)
                dve.wait_ge(v_ps, n + 1)
                if not early:
                    dve.wait_ge(v_store[b], 16 * c)
                nc.vector.tensor_copy(v_st[:, b, :, :].rearrange("p (a h) e -> p a (h e)", a=2), bank[:, 4:6, :])\
                    .then_inc(v_out, 1)

            all_tiles(dve, step)

        @block.tensor
        def _(pe):
            def context_transposes(b):
                for i in range(KT):
                    last = nc.tensor.transpose(bank[:, 6, i * P:(i + 1) * P], c_raw[:, b, i * P:(i + 1) * P], ident[:])
                last.then_inc(ct_ps, 1)

            def project(which, first_bank, rows_hi, rows_lo, done):
                for g in range(2):
                    w = slice(g * 512, (g + 1) * 512)
                    for i in range(KT):
                        last = three_passes(nc, bank[:, first_bank + g, :], rows_hi[:, i, :], rows_lo[:, i, :],
                                            w_hi[:, which, i, w], w_lo[:, which, i, w], i == 0, i == KT - 1)
                last.then_inc(done, 1)

            pe.wait_ge(nw_in, 32)
            nc.tensor.transpose(bank[:, 0, 0:2], nw_rows[:], ident[0:2, 0:2]).then_inc(nw_ps, 1)
            pe.wait_ge(c_in[0], 16)
            context_transposes(0)
            pe.wait_ge(nw_out, 1)
            pe.wait_ge(w_los, 2 * KT)

            def step(c, b, early, context, following):
                n = 2 * c + b
                if context:
                    pe.wait_ge(ct_lo, n + 1)
                    rows_hi, rows_lo = cT_hi[:, b, :, :], cT_lo[:, b, :, :]
                else:
                    row = (2 * b + c - CT) * P
                    rows_hi, rows_lo = k.x1_hi[:, :, row:row + P], k.x1_lo[:, :, row:row + P]
                if not early:
                    pe.wait_ge(k_out, n - 1)
                project(0, 2 * b, rows_hi, rows_lo, k_ps)
                if not (early and b == 0):
                    pe.wait_ge(kt_out, n)
                if following:
                    pe.wait_ge(c_in[1 - b], 16 * (c + b + 1))
                    context_transposes(1 - b)
                if not (early and b == 0):
                    pe.wait_ge(v_out, n)
                project(1, 4, rows_hi, rows_lo, v_ps)
                if following:
                    pe.wait_ge(ct_lo, n + 2)
                pe.wait_ge(knrm_made, n + 1)
                for h in range(KVH):
                    last = nc.tensor.transpose(bank[:, 6 + h // 4, h % 4 * P:(h % 4 + 1) * P], k_nrm[:, h, :], ident[:])
                last.then_inc(kt_ps, 1)

            all_tiles(pe, step)


UNITS = 2 * B
UT = 4
TILES = UNITS * UT
PIECE = 4
RING = 3

FILLERS = ((("W", 2), ("QT", 2), ("QT", 3), ("W", 3)),
           (("Q", 0), None, None, ("Q", 1)),
           (("Q", 2), ("QT", 0), ("QT", 1), ("W", 0)),
           (("Q", 3), None, None, ("W", 1)))


class Turn:

    BEFORE = TT + 2
    EACH = UNITS * KTL + 2 * TT + TT

    def __init__(self, i, first=False, more=True, ahead=True):
        self.i, self.first, self.more, self.ahead = i, first, more, ahead
        begin, shift = (self.BEFORE, 0) if first else (self.BEFORE - 2 + self.EACH * i, self.BEFORE - 2)
        shift = self.BEFORE if first else shift
        self.use, self.bank = {}, {}
        n = 0
        for s in range(UNITS):
            for what, a in self.tensor_order(s):
                if what in ("T", "Q", "QT", "W"):
                    self.use[s, what, a] = begin + n
                    self.bank[s, what, a] = 4 + (shift + n) % RING
                    n += 1
        self.end = begin + n
        self.pieces = 3 * PIECE + 2 + 4 * PIECE * i - (0 if more else PIECE)

    def fillers(self, s):
        kept = []
        for f in FILLERS[s]:
            from_before = s == 0 and f is not None and f[0] == "W"
            of_next = f is not None and (f[0] == "Q" or s == 2 and f[0] == "QT")
            kept.append(None if from_before and self.first or of_next and not self.more else f)
        return kept

    def scored(self, s):
        return self.more or s < UNITS - 1

    def tensor_order(self, s):
        f = self.fillers(s)
        order = [("T", 0), ("S", 0), ("T", 1), f[0], f[1], ("T", 2), ("O", 0), ("S", 1), ("T", 3), ("O", 1),
                 ("S", 2), ("T", 4), ("O", 2), ("S", 3), ("T", 5), ("O", 3), f[2], f[3], ("O", 4), ("O", 5)]
        return [e for e in order if e is not None and (e[0] != "S" or self.scored(s))]

    def scalar_order(self, s):
        f = self.fillers(s)
        order = [("T", 0), ("T", 1), ("E", 0), f[0], f[1], ("T", 2), ("T", 3), ("E", 1), ("T", 4), ("E", 2),
                 ("T", 5), ("E", 3), f[2], f[3], ("O", 0)]
        return [e for e in order if e is not None and (e[0] != "E" or self.scored(s))]

    def vector_order(self, s):
        f = self.fillers(s)
        order = [("T", 0), ("M", 0), ("T", 1), ("I", 0), f[0], f[1], ("T", 2), ("M", 1), ("T", 3), ("M", 2), ("I", 1),
                 ("T", 4), ("M", 3), ("I", 2), ("T", 5), ("I", 3), f[2], f[3], ("O", 0)]
        return [e for e in order if e is not None and (e[0] not in "MI" or self.scored(s))]


assert Turn.EACH % RING == 0


def cross_attention(nc, d, k):
    with ExitStack() as ctx:
        t = Tensors(nc, ctx)
        k_raw = t.sb("xk_raw", [P, B, KEYS])
        v_raw = t.sb("xv_raw", [P, B, KEYS])
        k_hi = t.sb("xk_hi", [P, B, KEYS], F32R)
        k_lo = t.sb("xk_lo", [P, B, KEYS], F32R)
        v_hi = t.sb("xv_hi", [P, B, KEYS], F32R)
        v_lo = t.sb("xv_lo", [P, B, KEYS], F32R)
        wq_raw = t.sb("wq_raw", [P, KT, D])
        wq_hi = t.sb("wq_hi", [P, KT, D], F32R)
        wq_lo = t.sb("wq_lo", [P, KT, D], F32R)
        wo_raw = t.sb("wo_raw", [P, GRP, D])
        wo_hi = t.sb("wo_hi", [P, GRP, D], F32R)
        wo_lo = t.sb("wo_lo", [P, GRP, D], F32R)
        q = t.sb("q_rows", [P, TT, D])
        q_sq = t.sb("q_sq", [P, TT, D])
        q_ss = t.sb("q_ss", [P, TT * GRP])
        q_ms = t.sb("q_ms", [P, TT * GRP])
        q_inv = t.sb("q_inv", [P, TT * GRP])
        minus_half = t.sb("minus_half", [P, TT * GRP])
        q_rms = t.sb("q_rms", [P, TT * GRP])
        qT_hi = t.sb("qT_hi", [P, GRP, TOK], F32R)
        qT_lo = t.sb("qT_lo", [P, GRP, TOK], F32R)
        prob = t.sb("prob", [P, 2 * UT, KEYS])
        mx = t.sb("x_mx", [P, 2 * UT])
        nm = t.sb("x_nm", [P, 2 * UT])
        rsum = t.sb("x_rsum", [P, 2 * UT])
        rinv = t.sb("x_rinv", [P, 2 * UT])
        pT_hi = t.sb("pT_hi", [P, KTL, UT * P], F32R)
        pT_lo = t.sb("pT_lo", [P, KTL, UT * P], F32R)
        oT_hi = t.sb("oT_hi", [P, GRP, TOK], F32R)
        oT_lo = t.sb("oT_lo", [P, GRP, TOK], F32R)
        x, bank, ident = k.x, k.bank, k.ident

        k_in = [t.sem("xk_in0"), t.sem("xk_in1")]
        v_in = [t.sem("xv_in0"), t.sem("xv_in1")]
        wq_in, wo_in = t.sem("wq_in"), t.sem("wo_in")
        piece_hi = t.sem("piece_hi")
        k_split, v_split, wq_split, wo_split = t.sem("xk_split"), t.sem("xv_split"), t.sem("wq_split"), t.sem("wo_split")
        ring_full = t.sem("ring_full")
        ring_out = t.sem("ring_out")
        q_out, qt_his = t.sem("xq_out"), t.sem("qt_his")
        half_set, ss_part, ms_made = t.sem("half_set"), t.sem("ss_part"), t.sem("ms_made")
        inv_made, rms_made = t.sem("inv_made"), t.sem("rms_made")
        s_full, mx_made, nm_made = t.sem("s_full"), t.sem("x_mx_made"), t.sem("x_nm_made")
        exp_made, rinv_made, prob_made = t.sem("exp_made"), t.sem("x_rinv_made"), t.sem("prob_made")
        pt_his = t.sem("pt_his")
        o_full, o_his, o_out = t.sem("o_full"), t.sem("o_his"), t.sem("o_out")
        block = ctx.enter_context(nc.Block())

        def turns(eng, body):
            body(Turn(0, first=True))
            with eng.Fori(1, KVH - 2) as i:
                body(Turn(i))
            body(Turn(KVH - 2, ahead=False))
            body(Turn(KVH - 1, more=False, ahead=False))

        def first_bank(use):
            return 4 + use % RING

        last_use = Turn(KVH - 1, more=False, ahead=False).end
        last_banks = [4 + (last_use + r) % RING for r in range(2)]

        def tile_of(u, j):
            return 2 * (u % 2) + j // 2, 2 * (u // 2) + j % 2

        def column(u, j):
            g, tt = tile_of(u, j)
            return slice(tt * GRP + g, tt * GRP + g + 1)

        def columns(b):
            return slice(2 * b * GRP, 2 * (b + 1) * GRP)

        @block.sync
        def _(sp):
            wq_view = d["Wq"].rearrange("(k p) (h n) -> h p k n", p=P, n=D)
            wo_view = d["Wo"].rearrange("(h g p) n -> h p g n", p=HD, g=GRP)

            def load_keys(b, i):
                sp.dma_start(k_raw[:, b, :], k.kT_dram[i, :, b * KEYS:(b + 1) * KEYS]).then_inc(k_in[b], 16)

            def load_values(b, i):
                sp.dma_start(v_raw[:, b, :], k.v_dram[i, :, b * KEYS:(b + 1) * KEYS]).then_inc(v_in[b], 16)

            def load_wq(i):
                sp.dma_start(wq_raw[:], wq_view[i, :, :, :]).then_inc(wq_in, 16)

            def load_wo(i):
                sp.dma_start(wo_raw[:], wo_view[i, :, :, :]).then_inc(wo_in, 16)

            load_wq(0)
            for b in range(B):
                load_keys(b, 0)
            for b in range(B):
                load_values(b, 0)
            load_wo(0)
            sp.wait_ge(wq_split, PIECE)
            load_wq(1)
            for b in range(B):
                sp.wait_ge(k_split, 2 * b + 2)
                load_keys(b, 1)
            sp.wait_ge(v_split, 2)
            load_values(0, 1)
            sp.wait_ge(wq_split, 2 * PIECE)
            load_wq(2)

            def this_head(i):
                sp.wait_ge(v_split, PIECE * i + 4)
                load_values(1, i + 1)
                sp.wait_ge(wo_split, PIECE * i + PIECE)
                load_wo(i + 1)

            def next_head(i):
                sp.wait_ge(k_split, PIECE * i + 6)
                load_keys(0, i + 2)
                sp.wait_ge(v_split, PIECE * i + 6)
                load_values(0, i + 2)
                sp.wait_ge(k_split, PIECE * i + 8)
                load_keys(1, i + 2)

            with sp.Fori(0, KVH - 3) as i:
                this_head(i)
                next_head(i)
                sp.wait_ge(wq_split, PIECE * i + 3 * PIECE)
                load_wq(i + 3)
            this_head(KVH - 3)
            next_head(KVH - 3)
            this_head(KVH - 2)

        @block.gpsimd
        def _(pool):
            awaited = pool.alloc_register("awaited")

            def wait_alone(sem, value):
                if not isinstance(value, int):
                    pool.reg_mov(awaited, value)
                    value = awaited
                pool.wait_ge(half_set, 1)
                pool.wait_ge(sem, value)

            def split(hi, lo, raw, count, done):
                nc.gpsimd.tensor_scalar(hi, raw, 1.0, 1.0, ALU.mult, ALU.mult).then_inc(piece_hi, 1)
                pool.wait_ge(piece_hi, count + 1)
                nc.gpsimd.tensor_tensor(lo, raw, f32(hi), ALU.subtract).then_inc(done, 1)

            def keys(b, piece, i, count):
                w = slice(piece * HALF, (piece + 1) * HALF)
                wait_alone(k_in[b], 16 * i + 16)
                split(k_hi[:, b, w], k_lo[:, b, w], k_raw[:, b, w], count, k_split)

            def values(b, piece, i, count):
                w = slice(piece * HALF, (piece + 1) * HALF)
                wait_alone(v_in[b], 16 * i + 16)
                split(v_hi[:, b, w], v_lo[:, b, w], v_raw[:, b, w], count, v_split)

            def query_weights(piece, i, count):
                wait_alone(wq_in, 16 * i + 16)
                split(wq_hi[:, piece, :], wq_lo[:, piece, :], wq_raw[:, piece, :], count, wq_split)

            def output_weights(piece, i, count):
                wait_alone(wo_in, 16 * i + 16)
                split(wo_hi[:, piece, :], wo_lo[:, piece, :], wo_raw[:, piece, :], count, wo_split)

            def inverse_rms(b, i):
                pool.wait_ge(ms_made, 2 * i + b + 1)
                nc.gpsimd.tensor_tensor(q_inv[:, columns(b)], q_ms[:, columns(b)], minus_half[:, columns(b)], ALU.pow)\
                    .then_inc(inv_made, 1)

            def norm(n, s):
                wait_alone(rinv_made, n + 1)
                nc.gpsimd.tensor_scalar(prob[:, s, :], prob[:, s, :], rinv[:, s:s + 1], 1.0, ALU.mult, ALU.mult)\
                    .then_inc(prob_made, 1)

            for p in range(PIECE):
                query_weights(p, 0, p)
            for b in range(B):
                for p in range(2):
                    keys(b, p, 0, PIECE + 2 * b + p)
                pool.wait_ge(half_set, 1)
                inverse_rms(b, 0)
            for j in range(UT):
                norm(j, j)
                if j < 2:
                    values(0, j, 0, 2 * PIECE + j)
            pool.wait_ge(ring_full, TT)
            for p in range(PIECE):
                query_weights(p, 1, 2 * PIECE + 2 + p)

            def body(turn):
                i, c = turn.i, turn.pieces

                def norms(s, tiles):
                    for j in tiles:
                        norm(TILES * i + UT * (s + 1) + j, UT * ((s + 1) % 2) + j)

                norms(0, (0,))
                if not turn.first:
                    wait_alone(o_full, UNITS * i)
                values(1, 0, i, c)
                norms(0, (1, 2, 3))
                values(1, 1, i, c + 1)
                if not turn.first:
                    wait_alone(ring_full, turn.use[0, "W", 3] + 1)
                for p in range(2):
                    output_weights(p, i, c + 2 + p)
                norms(1, (0,))
                output_weights(2, i, c + 4)
                norms(1, (1, 2, 3))
                output_weights(3, i, c + 5)
                if turn.more:
                    for p in range(2):
                        keys(0, p, i + 1, c + 6 + p)
                norms(2, (0,))
                if turn.more:
                    wait_alone(o_full, UNITS * i + 2)
                    values(0, 0, i + 1, c + 8)
                norms(2, (1, 2, 3))
                if turn.more:
                    inverse_rms(0, i + 1)
                    values(0, 1, i + 1, c + 9)
                    for p in range(2):
                        keys(1, p, i + 1, c + 10 + p)
                    norms(3, (0,))
                    if turn.ahead:
                        wait_alone(ring_full, turn.use[3, "Q", 3] + 1)
                        query_weights(0, i + 2, c + 12)
                    norms(3, (1, 2, 3))
                    inverse_rms(1, i + 1)
                    if turn.ahead:
                        for p in range(1, PIECE):
                            query_weights(p, i + 2, c + 12 + p)

            turns(pool, body)

        @block.scalar
        def _(act):
            def take_queries(tt, use, at):
                act.wait_ge(ring_full, use + 1)
                nc.scalar.activation(q[:, tt, :], bank[:, at, :], ACT.Copy).then_inc(q_out, 1)

            def split_queries(tt, use, at):
                act.wait_ge(ring_full, use + 1)
                nc.scalar.activation(qT_hi[:, :, tt * P:(tt + 1) * P], bank[:, at, :].rearrange("p (g t) -> p g t", g=GRP),
                                     ACT.Copy).then_inc(qt_his, 1)

            def exponentials(n, u, j):
                s = UT * (u % 2) + j
                act.wait_ge(nm_made, n + 1)
                nc.scalar.activation(prob[:, s, :].rearrange("p (a e) -> p a e", a=2),
                                     bank[:, 2 * (j % 2):2 * (j % 2) + 2, 0:HALF], ACT.Exp, bias=nm[:, s:s + 1],
                                     scale=q_rms[:, column(u, j)], accum_out=rsum[:, s:s + 1]).then_inc(exp_made, 1)

            for tt in range(TT):
                take_queries(tt, tt, first_bank(tt))
            for tt in range(2):
                split_queries(tt, TT + tt, first_bank(TT + tt))
            for j in range(UT):
                exponentials(j, 0, j)

            def body(turn):
                i = turn.i
                for s in range(UNITS):
                    for what, a in turn.scalar_order(s):
                        if what == "E":
                            exponentials(TILES * i + UT * (s + 1) + a, (s + 1) % UNITS, a)
                        elif what == "T":
                            act.wait_ge(ring_full, turn.use[s, what, a] + 1)
                            nc.scalar.activation(pT_hi[:, a, :], bank[:, turn.bank[s, what, a], :], ACT.Copy)\
                                .then_inc(pt_his, 1)
                        elif what == "Q":
                            take_queries(a, turn.use[s, what, a], turn.bank[s, what, a])
                        elif what == "QT":
                            split_queries(a, turn.use[s, what, a], turn.bank[s, what, a])
                        elif what == "O":
                            act.wait_ge(o_full, UNITS * i + s + 1)
                            g, rows = 2 * (s % 2), slice(s // 2 * S, (s // 2 + 1) * S)
                            nc.scalar.activation(oT_hi[:, g:g + 2, rows], bank[:, 7, :].rearrange("p (g t) -> p g t", g=2),
                                                 ACT.Copy).then_inc(o_his, 1)

            turns(act, body)

        @block.vector
        def _(dve):
            nc.vector.memset(minus_half[:], -0.5).then_inc(half_set, 1)

            def sum_squares(tt, i, use, at):
                dve.wait_ge(q_out, TT * i + tt + 1)
                for g in range(GRP):
                    w = slice(g * HD, (g + 1) * HD)
                    nc.vector.tensor_tensor_reduce(out=q_sq[:, tt, w], in0=bank[:, at, w], in1=q[:, tt, w],
                                                   scale=1.0, scalar=0.0, op0=ALU.mult, op1=ALU.add,
                                                   accum_out=q_ss[:, tt * GRP + g:tt * GRP + g + 1])\
                        .then_inc(ring_out if g == GRP - 1 else ss_part, 1)
                if tt % 2:
                    dve.wait_ge(ss_part, (GRP - 1) * (TT * i + tt + 1))
                    dve.wait_ge(ring_out, use + 1)
                    nc.vector.tensor_scalar(q_ms[:, columns(tt // 2)], q_ss[:, columns(tt // 2)], 1.0 / HD, RMS_EPS,
                                            ALU.mult, ALU.add).then_inc(ms_made, 1)

            def query_scales(b, i):
                dve.wait_ge(inv_made, 2 * i + b + 1)
                nc.vector.tensor_scalar(q_rms[:, columns(b)], q_inv[:, columns(b)], X_SCALE, None, ALU.mult)\
                    .then_inc(rms_made, 1)
                dve.wait_ge(rms_made, 2 * i + b + 1)

            def split_queries(tt, i, at):
                dve.wait_ge(qt_his, TT * i + tt + 1)
                w = slice(tt * P, (tt + 1) * P)
                nc.vector.tensor_tensor(qT_lo[:, :, w], bank[:, at, :].rearrange("p (g t) -> p g t", g=GRP),
                                        f32(qT_hi[:, :, w]), ALU.subtract).then_inc(ring_out, 1)

            def shift(n, u, j):
                s = UT * (u % 2) + j
                dve.wait_ge(s_full, n + 1)
                nc.vector.reduce_max(mx[:, s:s + 1], bank[:, 2 * (j % 2):2 * (j % 2) + 2, 0:HALF], AX.XY)\
                    .then_inc(mx_made, 1)
                dve.wait_ge(mx_made, n + 1)
                nc.vector.tensor_scalar(nm[:, s:s + 1], mx[:, s:s + 1], q_rms[:, column(u, j)], -1.0,
                                        ALU.mult, ALU.mult).then_inc(nm_made, 1)

            def invert_sum(n, u, j):
                s = UT * (u % 2) + j
                dve.wait_ge(exp_made, n + 1)
                nc.vector.reciprocal(rinv[:, s:s + 1], rsum[:, s:s + 1]).then_inc(rinv_made, 1)

            def add_output(tt, use, at):
                dve.wait_ge(ring_full, use + 1)
                nc.vector.tensor_tensor(x[:, tt, :], bank[:, at, :], x[:, tt, :], ALU.add).then_inc(ring_out, 1)

            for tt in range(TT):
                sum_squares(tt, 0, tt, first_bank(tt))
            for tt in range(2):
                split_queries(tt, 0, first_bank(TT + tt))
            query_scales(0, 0)
            for j in range(UT):
                shift(j, 0, j)
                invert_sum(j, 0, j)

            def body(turn):
                i = turn.i
                for s in range(UNITS):
                    u, n = (s + 1) % UNITS, TILES * i + UT * (s + 1)
                    for what, a in turn.vector_order(s):
                        if what == "M":
                            shift(n + a, u, a)
                        elif what == "I":
                            invert_sum(n + a, u, a)
                        elif what == "T":
                            dve.wait_ge(pt_his, KTL * (UNITS * i + s) + a + 1)
                            nc.vector.tensor_tensor(pT_lo[:, a, :], bank[:, turn.bank[s, what, a], :],
                                                    f32(pT_hi[:, a, :]), ALU.subtract).then_inc(ring_out, 1)
                        elif what == "Q":
                            sum_squares(a, i + 1, turn.use[s, what, a], turn.bank[s, what, a])
                        elif what == "QT":
                            split_queries(a, i if s == 0 else i + 1, turn.bank[s, what, a])
                        elif what == "W":
                            add_output(a, turn.use[s, what, a], turn.bank[s, what, a])
                        elif what == "O":
                            dve.wait_ge(o_his, UNITS * i + s + 1)
                            g, rows = 2 * (s % 2), slice(s // 2 * S, (s // 2 + 1) * S)
                            nc.vector.tensor_tensor(oT_lo[:, g:g + 2, rows],
                                                    bank[:, 7, :].rearrange("p (g t) -> p g t", g=2),
                                                    f32(oT_hi[:, g:g + 2, rows]), ALU.subtract).then_inc(o_out, 1)
                    if s == 0:
                        query_scales(1, i)
                    if s == 2 and turn.more:
                        query_scales(0, i + 1)
                if not turn.more:
                    for r in range(2):
                        add_output(2 + r, turn.end + r, last_banks[r])

            turns(dve, body)

        @block.tensor
        def _(pe):
            def ring_free(use):
                pe.wait_ge(ring_out, use - RING + 1)

            def queries(tt, use, at):
                if not (isinstance(use, int) and use < RING):
                    ring_free(use)
                for m in range(KT):
                    w = slice(tt * P, (tt + 1) * P)
                    last = three_passes(nc, bank[:, at, :], k.x1_hi[:, m, w], k.x1_lo[:, m, w],
                                        wq_hi[:, m, :], wq_lo[:, m, :], m == 0, m == KT - 1)
                last.then_inc(ring_full, 1)

            def transposed_queries(tt, i, use, at):
                pe.wait_ge(q_out, TT * i + tt + 1)
                ring_free(use)
                for g in range(GRP):
                    last = nc.tensor.transpose(bank[:, at, g * P:(g + 1) * P], q[:, tt, g * HD:(g + 1) * HD], ident[:])
                last.then_inc(ring_full, 1)

            def scores(n, u, j, early):
                g, tt = tile_of(u, j)
                b, w = u // 2, slice(tt * P, (tt + 1) * P)
                if not early:
                    pe.wait_ge(exp_made, n - 1)
                for a_hi, k_part, start, stop in ((qT_hi, k_hi, True, False), (qT_hi, k_lo, False, False),
                                                  (qT_lo, k_hi, False, True)):
                    for c in range(2):
                        last = nc.tensor.matmul(bank[:, 2 * (j % 2) + c, 0:HALF], a_hi[:, g, w],
                                                k_part[:, b, c * HALF:(c + 1) * HALF], start=start, stop=stop)
                last.then_inc(s_full, 1)

            def output(tt, i, use, at):
                pe.wait_ge(o_out, UNITS * i + 2 * (tt // 2) + 2)
                w = slice(tt * P, (tt + 1) * P)
                ring_free(use)
                for g in range(GRP):
                    last = three_passes(nc, bank[:, at, :], oT_hi[:, g, w], oT_lo[:, g, w],
                                        wo_hi[:, g, :], wo_lo[:, g, :], g == 0, g == GRP - 1)
                last.then_inc(ring_full, 1)

            pe.wait_ge(wq_split, PIECE)
            for tt in range(TT):
                queries(tt, tt, first_bank(tt))
            for tt in range(2):
                transposed_queries(tt, 0, TT + tt, first_bank(TT + tt))
            pe.wait_ge(ring_out, Turn.BEFORE)
            pe.wait_ge(k_split, 2)
            for j in range(UT):
                scores(j, 0, j, j < 2)

            def body(turn):
                i = turn.i
                for s in range(UNITS):
                    u, b = (s + 1) % UNITS, s // 2
                    for what, a in turn.tensor_order(s):
                        use, at = turn.use.get((s, what, a)), turn.bank.get((s, what, a))
                        if what == "S":
                            if a == 0 and s == 1:
                                pe.wait_ge(k_split, PIECE * i + 4)
                                pe.wait_ge(ring_out, turn.use[0, "QT", 3] + 1)
                            if a == 0 and s == 3:
                                pe.wait_ge(k_split, PIECE * i + 6)
                                pe.wait_ge(ring_out, turn.use[2, "QT", 1] + 1)
                            scores(TILES * i + UT * (s + 1) + a, u, a, False)
                        elif what == "T":
                            if a == 0:
                                pe.wait_ge(prob_made, TILES * i + UT * (s + 1))
                            ring_free(use)
                            for j in range(UT):
                                last = nc.tensor.transpose(bank[:, at, j * P:(j + 1) * P],
                                                           prob[:, UT * (s % 2) + j, a * P:(a + 1) * P], ident[:])
                            last.then_inc(ring_full, 1)
                        elif what == "O":
                            if a == 0:
                                if not (turn.first and s == 0):
                                    pe.wait_ge(o_out, UNITS * i + s)
                                pe.wait_ge(v_split, PIECE * i + 2 * b + 2)
                            pe.wait_ge(ring_out, turn.use[s, "T", a] + 1)
                            w = slice(a * HD, (a + 1) * HD)
                            last = three_passes(nc, bank[:, 7, :], v_hi[:, b, w], v_lo[:, b, w],
                                                pT_hi[:, a, :], pT_lo[:, a, :], a == 0, a == KTL - 1)
                            if a == KTL - 1:
                                last.then_inc(o_full, 1)
                        elif what == "Q":
                            if a == 0:
                                pe.wait_ge(wq_split, PIECE * i + 2 * PIECE)
                            queries(a, use, at)
                        elif what == "QT":
                            transposed_queries(a, i if s == 0 else i + 1, use, at)
                        elif what == "W" and s == 0:
                            output(a, i - 1, use, at)
                        elif what == "W":
                            if a == 0:
                                pe.wait_ge(wo_split, PIECE * i + PIECE)
                            output(a, i, use, at)
                if not turn.more:
                    for r in range(2):
                        output(2 + r, i, turn.end + r, last_banks[r])

            turns(pe, body)


def feed_forward(nc, d, k):
    with ExitStack() as ctx:
        t = Tensors(nc, ctx)
        up = t.sb("up_w", [P, FH // HPT, FM])
        down = t.sb("down_w", [P, FH, FD])
        perm_i = t.sb("perm_i", [1, D], I32)
        perm_f = t.sb("perm_f", [1, D])
        perm_rows_i = t.sb("perm_rows_i", [KT, P], I32)
        perm_rows = t.sb("perm_rows", [KT, P])
        perm_cols = t.sb("perm_cols", [P, KT])
        index_row = t.sb("index_row", [P, D])
        index_col = t.sb("index_col", [P, KT])
        ones = t.sb("ones_row2", [1, P])
        gather = t.sb("gather", [P, KT, D], F32R)
        scatter = t.sb("scatter", [P, KT, D], F32R)
        xT_hi = t.sb("x2T_hi", [P, KT, TOK], F32R)
        xT_lo = t.sb("x2T_lo", [P, KT, TOK], F32R)
        tT = t.sb("tT", [P, KT, TOK])
        hid = t.sb("hid", [P, HPT, TOK])
        yT_hi = t.sb("yT_hi", [P, KT, TOK], F32R)
        yT_lo = t.sb("yT_lo", [P, KT, TOK], F32R)
        stats = t.sb("stats2", [P, TT, 6])
        mv = t.sb("mv2", [P, 2, TT, 2])
        std = t.sb("std2", [P, 2 * TT])
        rstd = t.sb("rstd2", [P, 2 * TT])
        x, bank, ident = k.x, k.bank, k.ident

        perm_in, up_in, down_in, out_stored = t.sem("perm_in"), t.sem("up_in"), t.sem("down_in"), t.sem("out_stored")
        index_made, perm_made, perm_ps, cols_out = t.sem("index_made"), t.sem("perm_made"), t.sem("perm_ps"), t.sem("cols_out")
        gather_made, scatter_made = t.sem("gather_made"), t.sem("scatter_made")
        y_sum, y_stats, y_mv = t.sem("y_sum2"), t.sem("y_stats2"), t.sem("y_mv2")
        std_made, rstd_made, ln_made = t.sem("std_made2"), t.sem("rstd_made2"), t.sem("ln_made2")
        xt_ps, xt_hi, xt_lo = t.sem("x2t_ps"), t.sem("x2t_hi"), t.sem("x2t_lo")
        t_ps, t_out = t.sem("t_ps"), t.sem("t_out")
        h_ps, h_out = t.sem("h_ps"), t.sem("h_out")
        y_ps, y_hi, y_lo, z_ps = t.sem("y_ps2"), t.sem("y_hi2"), t.sem("y_lo2"), t.sem("z_ps")
        block = ctx.enter_context(nc.Block())

        @block.sync
        def _(sp):
            sp.dma_start(perm_i[:], d["perm"].rearrange("(a n) -> a n", a=1)).then_inc(perm_in, 16)
            sp.dma_start(perm_rows_i[:], d["perm"].rearrange("(k p) -> k p", p=P)).then_inc(perm_in, 16)
            sp.dma_start(up[:], d["up"].rearrange("(t q) e m -> (q e) t m", q=HPT)).then_inc(up_in, 16)
            sp.dma_start(down[:], d["down"].rearrange("h m e -> m h e")).then_inc(down_in, 16)
            for i in range(TT):
                sp.wait_ge(ln_made, TT + i + 1)
                sp.dma_start(d["out"].rearrange("b s d -> (b s) d")[i * P:(i + 1) * P, :], x[:, i, :])\
                    .then_inc(out_stored, 16)
            sp.wait_ge(out_stored, 16 * TT)

        @block.gpsimd
        def _(pool):
            nc.gpsimd.memset(ones[:], 1.0).then_inc(index_made, 1)
            nc.gpsimd.iota(index_row[:], [[1, D]], base=0, channel_multiplier=0,
                           allow_small_or_imprecise_dtypes=True).then_inc(index_made, 1)
            nc.gpsimd.iota(index_col[:], [[P, KT]], base=0, channel_multiplier=1,
                           allow_small_or_imprecise_dtypes=True).then_inc(index_made, 1)

        @block.scalar
        def _(act):
            act.wait_ge(perm_ps, 1)
            nc.scalar.activation(perm_cols[:], bank[:, 7, 0:KT], ACT.Copy).then_inc(cols_out, 1)
            for i in range(TT):
                act.wait_ge(y_mv, i + 1)
                nc.scalar.activation(std[:, i:i + 1], mv[:, 0, i, 1:2], ACT.Sqrt, bias=k.ln_eps[:]).then_inc(std_made, 1)
            for i in range(KT):
                act.wait_ge(xt_ps, i + 1)
                nc.scalar.activation(xT_hi[:, i, :], bank[:, i, :], ACT.Copy).then_inc(xt_hi, 1)
            for i in range(KT):
                act.wait_ge(t_ps, i + 1)
                nc.scalar.activation(tT[:, i, :], bank[:, 4 + i, :], ACT.Copy).then_inc(t_out, 1)
            for h in range(FH):
                act.wait_ge(h_ps, h + 1)
                nc.scalar.activation(hid[:, h % HPT, :], bank[:, h % HPT, :], ACT.Gelu).then_inc(h_out, 1)
            for i in range(KT):
                act.wait_ge(y_ps, HPT * (i + 1))
                nc.scalar.activation(yT_hi[:, i, :], bank[:, 4 + i, :], ACT.Copy).then_inc(y_hi, 1)
            for i in range(TT):
                act.wait_ge(y_mv, TT + i + 1)
                nc.scalar.activation(std[:, TT + i:TT + i + 1], mv[:, 1, i, 1:2], ACT.Sqrt, bias=k.ln_eps[:])\
                    .then_inc(std_made, 1)

        @block.vector
        def _(dve):
            def statistics(r, i):
                nc.vector.bn_stats(stats[:, i, :], x[:, i, :]).then_inc(y_stats, 1)
                dve.wait_ge(y_stats, TT * r + i + 1)
                nc.vector.bn_aggr(mv[:, r, i, :], stats[:, i, :]).then_inc(y_mv, 1)

            def normalise(r, i):
                n = TT * r + i
                dve.wait_ge(std_made, n + 1)
                nc.vector.reciprocal(rstd[:, n:n + 1], std[:, n:n + 1]).then_inc(rstd_made, 1)
                dve.wait_ge(rstd_made, n + 1)
                nc.vector.tensor_scalar(x[:, i, :], x[:, i, :], mv[:, r, i, 0:1], rstd[:, n:n + 1],
                                        ALU.subtract, ALU.mult).then_inc(ln_made, 1)

            dve.wait_ge(perm_in, 32)
            nc.vector.tensor_copy(perm_f[:], perm_i[:]).then_inc(perm_made, 1)
            nc.vector.tensor_copy(perm_rows[:], perm_rows_i[:]).then_inc(perm_made, 1)
            for i in range(TT):
                statistics(0, i)
            for i in range(TT):
                normalise(0, i)
            dve.wait_ge(index_made, 3)
            dve.wait_ge(cols_out, 1)
            for i in range(KT):
                nc.vector.tensor_scalar(gather[:, i, :], bank[:, 6, :], index_col[:, i:i + 1], None, ALU.is_equal)\
                    .then_inc(gather_made, 1)
            for i in range(KT):
                dve.wait_ge(xt_hi, i + 1)
                nc.vector.tensor_tensor(xT_lo[:, i, :], bank[:, i, :], f32(xT_hi[:, i, :]), ALU.subtract)\
                    .then_inc(xt_lo, 1)
            for i in range(KT):
                nc.vector.tensor_scalar(scatter[:, i, :], index_row[:], perm_cols[:, i:i + 1], None, ALU.is_equal)\
                    .then_inc(scatter_made, 1)
            for i in range(KT):
                dve.wait_ge(y_hi, i + 1)
                nc.vector.tensor_tensor(yT_lo[:, i, :], bank[:, 4 + i, :], f32(yT_hi[:, i, :]), ALU.subtract)\
                    .then_inc(y_lo, 1)
            for i in range(TT):
                dve.wait_ge(z_ps, i + 1)
                nc.vector.tensor_tensor(x[:, i, :], bank[:, i, :], x[:, i, :], ALU.add).then_inc(y_sum, 1)
                dve.wait_ge(y_sum, i + 1)
                statistics(1, i)
            for i in range(TT):
                normalise(1, i)

        @block.tensor
        def _(pe):
            pe.wait_ge(perm_made, 2)
            pe.wait_ge(index_made, 1)
            nc.tensor.matmul(bank[:, 6, :], ones[:], perm_f[:], start=True, stop=True)
            nc.tensor.transpose(bank[:, 7, 0:KT], perm_rows[:], ident[0:KT, 0:KT]).then_inc(perm_ps, 1)
            pe.wait_ge(ln_made, TT)
            for i in range(KT):
                for j in range(TT):
                    last = nc.tensor.transpose(bank[:, i, j * P:(j + 1) * P], x[:, j, i * P:(i + 1) * P], ident[:])
                last.then_inc(xt_ps, 1)
            pe.wait_ge(gather_made, KT)
            pe.wait_ge(xt_lo, KT)
            for i in range(KT):
                for j in range(KT):
                    w = slice(i * P, (i + 1) * P)
                    nc.tensor.matmul(bank[:, 4 + i, :], gather[:, j, w], xT_hi[:, j, :], start=j == 0, stop=False)
                    last = nc.tensor.matmul(bank[:, 4 + i, :], gather[:, j, w], xT_lo[:, j, :], start=False,
                                            stop=j == KT - 1)
                last.then_inc(t_ps, 1)
            pe.wait_ge(up_in, 16)
            pe.wait_ge(down_in, 16)
            pe.wait_ge(t_out, KT)

            def up_product(h):
                r = FD * (h % HPT)
                if h >= HPT:
                    pe.wait_ge(h_out, h - HPT + 1)
                nc.tensor.matmul(bank[:, h % HPT, :], up[r:r + FD, h // HPT, :], tT[r:r + FD, h // HPT, :],
                                 start=True, stop=True).then_inc(h_ps, 1)

            def down_product(h):
                r = FD * (h % HPT)
                pe.wait_ge(h_out, h + 1)
                nc.tensor.matmul(bank[r:r + FD, 4 + h // HPT, :], down[:, h, :], hid[:, h % HPT, :],
                                 start=True, stop=True).then_inc(y_ps, 1)

            up_product(0)
            up_product(1)
            for h in range(FH):
                if h + 2 < FH:
                    up_product(h + 2)
                down_product(h)
            pe.wait_ge(y_lo, KT)
            pe.wait_ge(scatter_made, KT)
            for j in range(TT):
                w = slice(j * P, (j + 1) * P)
                for i in range(KT):
                    nc.tensor.matmul(bank[:, j, :], yT_hi[:, i, w], scatter[:, i, :], start=i == 0, stop=False)
                    last = nc.tensor.matmul(bank[:, j, :], yT_lo[:, i, w], scatter[:, i, :], start=False,
                                            stop=i == KT - 1)
                last.then_inc(z_ps, 1)


class Kept:
    pass


def build(nc, d):
    with ExitStack() as ctx:
        t = Tensors(nc, ctx)
        k = Kept()
        k.x = t.sb("x_rows", [P, TT, D])
        k.x1_hi = t.sb("x1_hi", [P, KT, TOK], F32R)
        k.x1_lo = t.sb("x1_lo", [P, KT, TOK], F32R)
        k.ident = t.sb("ident", [P, P])
        k.ln_eps = t.sb("ln_eps", [P, 1])
        k.rms_eps = t.sb("rms_eps", [P, 1])
        k.bank = ctx.enter_context(nc.psum_tensor("bank", [P, 8, 512], F32))
        k.kT_dram = nc.dram_tensor("kT_by_head", [KVH, HD, B * KEYS], F32, kind="Internal").ap()
        k.v_dram = nc.dram_tensor("v_by_head", [KVH, P, B * KEYS], F32, kind="Internal").ap()
        self_attention(nc, d, k)
        keys_values(nc, d, k)
        cross_attention(nc, d, k)
        feed_forward(nc, d, k)


_INS = {"x": "x", "ctx": "ctx_4096", "w_attn": "L0_attn_w_attn", "b_attn": "L0_attn_b_attn",
        "w_proj": "L0_attn_w_proj", "b_proj": "L0_attn_b_proj", "Wq": "L0_xattn_Wq", "Wk": "L0_xattn_Wk",
        "Wv": "L0_xattn_Wv", "Wo": "L0_xattn_Wo", "q_norm": "L0_xattn_q_norm_w", "k_norm": "L0_xattn_k_norm_w",
        "up": "L0_ffn_up", "down": "L0_ffn_down", "perm": "L0_ffn_perm"}


def kernel(**inputs):
    import numpy as np
    import concourse.bacc as bacc
    from concourse.bass_utils import run_bass_kernel_spmd

    nc = bacc.Bacc("TRN2", target_bir_lowering=False, num_devices=1)
    arrays, d = {}, {}
    for name, given in _INS.items():
        a = np.ascontiguousarray(inputs[given])
        arrays[f"in_{name}"] = a
        d[name] = nc.dram_tensor(f"in_{name}", a.shape, mybir.dt.from_np(a.dtype), kind="ExternalInput").ap()
    d["out"] = nc.dram_tensor("out", (B, S, D), F32, kind="ExternalOutput").ap()
    build(nc, d)
    return run_bass_kernel_spmd(nc, [arrays], core_ids=[0]).results[0]["out"]
```

```python
from contextlib import ExitStack

import concourse.bass as bass
from concourse import mybir

P = 128
ALU = mybir.AluOpType
ACT = mybir.ActivationFunctionType
AX = mybir.AxisListType
F32 = mybir.dt.float32
F32R = mybir.dt.float32r
I32 = mybir.dt.int32

B, S, D = 2, 256, 512
TOK = B * S
TT = TOK // P
KT = D // P
C = 512
CT = C // P
LN_EPS = 1e-5

SA_HEADS, SA_DIM = 32, 16
SA_SCALE = 1.0 / SA_DIM
SLOPES = [2.0 ** (-(h + 1) / 4) for h in range(SA_HEADS)]
MASKED = -1e36

XH, KVH, HD = 32, 8, 128
GRP = XH // KVH
KEYS = C + S
KTL = KEYS // P
HALF = KEYS // 2
X_SCALE = float(HD) ** -0.5
RMS_EPS = 1e-6

FH, FD, FM = 16, 32, 128
HPT = P // FD


def three_passes(nc, out, a_hi, a_lo, b_hi, b_lo, first, last):
    nc.tensor.matmul(out, a_hi, b_hi, start=first, stop=False)
    nc.tensor.matmul(out, a_hi, b_lo, start=False, stop=False)
    return nc.tensor.matmul(out, a_lo, b_hi, start=False, stop=last)


def f32(ap):
    return ap.bitcast(F32)


class Tensors:

    def __init__(self, nc, ctx):
        self.nc, self.ctx = nc, ctx

    def sb(self, name, shape, dt=F32):
        return self.ctx.enter_context(self.nc.sbuf_tensor(name, shape, dt))

    def sem(self, name):
        return self.ctx.enter_context(self.nc.semaphore(name))


HB = SA_HEADS * B
PER_TILE = P // SA_DIM
LT = S // P
ROWS = B * (CT + LT)
PARTS = 8
LN_ORDER = (0, 2, 1, 3)


def order_of_work():
    order = [("S", 0)]
    q, skipped = 0, set()
    for n in range(HB):
        if n + 1 < HB:
            order.append(("S", n + 1))
        if q not in skipped and (q % PARTS == 2 or q % (2 * PARTS) == PARTS + 4):
            skipped.add(q)
        else:
            order.append(("part", q))
            q += 1
        if n >= 1:
            order.append(("PV", n - 1))
        order.append(("T", n))
    tail = ("PV", "part", "part", "AT0", "AT2", "part", "part", "Y0", "AT1", "part", "LN0", "Y2", "AT3", "part", "LN2",
            "Y1", "part", "XT0", "LN1", "Y3", "part", "XT2", "part", "LN3", "part", "XT1", "XT3")
    for name in tail:
        if name == "part":
            order.append(("part", q))
            q += 1
        elif name == "PV":
            order.append(("PV", HB - 1))
        else:
            order.append((name[:-1], int(name[-1])))
    assert q == B * CT * PARTS
    for q in range(q, ROWS * PARTS + 5):
        order.append(("part", q))
        if q == B * CT * PARTS + 6:
            order.append(("WQ", 0))
        order += [("Q", j) for j in range(TT) if q == ROWS * PARTS + (-1, 2, 4, 4)[j]]
    return order


def vector_order(order):
    order = list(order)
    for i in reversed(range(len(order))):
        ahead = [what for what, _ in order[i + 1:i + 3]]
        if order[i][0] == "part" and "T" in ahead:
            order.insert(i + 1 + ahead.index("T"), order.pop(i))
    return order


def self_attention_and_keys(nc, d, k):
    with ExitStack() as ctx:
        t = Tensors(nc, ctx)
        xT_hi, xT_lo = k.x1_hi, k.x1_lo
        w_raw = k.wq_raw
        w_hi = t.sb("w_hi", [P, 4, KT, D], F32R)
        w_lo = t.sb("w_lo", [P, 4, KT, D], F32R)
        SLOT = (0, 1, 2, 0, 1, 3, 2)
        EARLY = 3 * KT
        qT = t.sb("qT", [P, KT, TOK])
        kT_even = t.sb("kT_even", [P, KT, TOK])
        kT_odd = t.sb("kT_odd", [P, KT, TOK])
        v, att = k.q_sq, k.q
        col_rows = t.sb("col_rows", [2 * KT + 2, P])
        cols = t.sb("cols", [P, 2 * KT + 2])
        nw = t.sb("nw", [P, 1])
        row_bias = t.sb("row_bias", [1, D])
        ones = t.sb("ones_row", [1, P])
        even = t.sb("even", [P, 1])
        odd = t.sb("odd", [P, 1])
        minus_half = k.minus_half
        rel = t.sb("rel", [P, S])
        bias = t.sb("alibi", [P, 2, S])
        s_sb = t.sb("s_self", [P, 2, 3 * P])
        pT = t.sb("pT_self", [P, 2, 3 * P])
        mx = t.sb("mx_self", [P, 2, 2])
        nm = t.sb("nm_self", [P, 2, 2])
        rsum = t.sb("rsum_self", [P, TT, SA_HEADS])
        rinv = t.sb("rinv_self", [P, TT, SA_HEADS])
        stats = t.sb("stats1", [P, TT, 6])
        mv = t.sb("mv1", [P, TT, 2])
        var = t.sb("var1", [P, TT])
        rstd = t.sb("rstd1", [P, TT])
        c_raw = t.sb("c_raw", [P, 2, D])
        cT_hi = t.sb("cT_hi", [P, 2, KT, P], F32R)
        cT_lo = t.sb("cT_lo", [P, 2, KT, P], F32R)
        k_raw = t.sb("k_raw", [P, KVH, HD])
        k_sq = t.sb("k_sq", [P, KVH // 2, HD])
        k_ss = t.sb("k_ss", [P, KVH])
        k_ms = t.sb("k_ms", [P, KVH])
        k_inv = t.sb("k_inv", [P, KVH])
        k_nrm = t.sb("k_nrm", [P, KVH, HD])
        kT_st = t.sb("kT_st", [P, 2, KVH, P])
        v_st = t.sb("v_st", [P, 2, KVH, HD])
        x, bank, ident = k.x, k.bank, k.ident
        GROUP, TRANSPOSED = 5, 7

        bias_in = t.sem("bias_in")
        x_in = [t.sem(f"x_in{j}") for j in range(TT)]
        w_in = [t.sem(f"w_in{i}") for i in range(KT)]
        const, mask = t.sem("const_ready"), t.sem("mask_ready")
        xt_ps, xt_hi, xt_lo = t.sem("xt_ps"), t.sem("xt_hi"), t.sem("xt_lo")
        w_his, w_los, late_los = t.sem("w_his"), t.sem("w_los"), t.sem("late_los")
        col_ps, col_out, nw_made = t.sem("col_ps"), t.sem("col_out"), t.sem("nw_made")
        qk_ps, q_out, k_out = t.sem("qk_ps"), t.sem("q_out"), t.sem("k_out")
        v_ps, v_out = t.sem("v_ps"), t.sem("v_out")
        bias_made = t.sem("alibi_made")
        s_ps, s_half, s_out = t.sem("s_ps_self"), t.sem("s_half_self"), t.sem("s_out_self")
        nm_made, p_made = t.sem("nm_made_self"), t.sem("p_made_self")
        pt_ps, pt_out, o_ps = t.sem("pt_ps_self"), t.sem("pt_out_self"), t.sem("o_ps_self")
        rinv_made, att_out = t.sem("rinv_made_self"), t.sem("att_out")
        at_ps, at_hi, at_lo = t.sem("at_ps_self"), t.sem("at_hi_self"), t.sem("at_lo_self")
        y_ps, y_sum, y_stats, y_mv = t.sem("y_ps1"), t.sem("y_sum1"), t.sem("y_stats1"), t.sem("y_mv1")
        var_made, rstd_made, x1_made = t.sem("var_made1"), t.sem("rstd_made1"), t.sem("x1_made")
        x1t_ps, x1t_hi, x1t_lo = t.sem("x1t_ps"), t.sem("x1t_hi"), t.sem("x1t_lo")
        c_in = [t.sem("c_in0"), t.sem("c_in1")]
        ct_ps, ct_hi, ct_lo = t.sem("ct_ps"), t.sem("ct_hi"), t.sem("ct_lo")
        g_ps = t.sem("group_ps")
        kg_out, ksq_made, kss_made, kms_made = t.sem("kg_out"), t.sem("ksq_made"), t.sem("kss_made"), t.sem("kms_made")
        kinv_made, knrm_made = t.sem("kinv_made"), t.sem("knrm_made")
        vg_out = t.sem("vg_out")
        kt_ps, kt_out = t.sem("kt_ps"), t.sem("kt_out")
        wq_los, q_ps, q_rows_out, ss_part = t.sem("wq_los"), t.sem("q_ps_cross"), t.sem("q_rows_out"), t.sem("ss_part1")
        k_store = [t.sem("k_store0"), t.sem("k_store1")]
        v_store = [t.sem("v_store0"), t.sem("v_store1")]
        block = ctx.enter_context(nc.Block())

        ORDER = order_of_work()
        pairs = [(h, b) for h in range(SA_HEADS) for b in range(B)]
        GH = KVH // 2

        def tokens(j):
            return slice(j * P, (j + 1) * P)

        def split_of(p, i):
            return (w_hi[:, SLOT[p], i, :], w_lo[:, SLOT[p], i, :]) if p < 7 else (k.wq_hi[:, i, :], k.wq_lo[:, i, :])

        @block.sync
        def _(sp):
            def load_weights(p):
                name, g = (("w_attn", 0), ("w_attn", 1), ("w_attn", 2), ("Wk", 0), ("Wk", 1), ("Wv", 0), ("Wv", 1),
                           ("w_proj", 0), ("Wq", 0))[p]
                for i in range(KT):
                    split = KT * (p - 1) + i + 1
                    if p > 0 and split <= EARLY:
                        sp.wait_ge(w_los, split)
                    elif p > 0:
                        sp.wait_ge(late_los, split - EARLY)
                    sp.dma_start(w_raw[:, i, :], d[name][i * P:(i + 1) * P, g * D:(g + 1) * D]).then_inc(w_in[i], 16)

            def load_context(n):
                if n >= 2:
                    sp.wait_ge(ct_ps, n - 1)
                sp.dma_start(c_raw[:, n % 2, :], d["ctx"][n % 2, n // 2 * P:(n // 2 + 1) * P, :]).then_inc(c_in[n % 2], 16)

            for i in range(TT):
                sp.dma_start(x[:, i, :], d["x"].rearrange("b s d -> (b s) d")[tokens(i), :]).then_inc(x_in[i], 16)
            load_weights(0)
            sp.dma_start(col_rows[0:2 * KT, :], d["b_attn"][0:2 * D].rearrange("(m p) -> m p", p=P)).then_inc(bias_in, 16)
            sp.dma_start(col_rows[2 * KT:2 * KT + 1, :], d["q_norm"].rearrange("(a n) -> a n", a=1)).then_inc(bias_in, 16)
            sp.dma_start(col_rows[2 * KT + 1:2 * KT + 2, :], d["k_norm"].rearrange("(a n) -> a n", a=1)).then_inc(bias_in, 16)
            sp.dma_start(row_bias[:], d["b_attn"][2 * D:3 * D].rearrange("(a n) -> a n", a=1)).then_inc(bias_in, 16)
            load_weights(1)
            load_context(0)
            load_context(1)
            for p in range(2, 7):
                load_weights(p)
            sp.wait_ge(v_ps, TT)
            sp.dma_start(row_bias[:], d["b_proj"].rearrange("(a n) -> a n", a=1)).then_inc(bias_in, 16)

            v_view = k.v_dram.rearrange("h p (n e) -> p h n e", e=HD)
            k_view = k.kT_dram.rearrange("h p (n e) -> p h n e", e=P)
            for n in range(ROWS):
                at = n % 2 * KTL + n // 2
                if n + 2 < B * CT:
                    load_context(n + 2)
                if n == 0:
                    load_weights(7)
                if n == 4:
                    load_weights(8)
                sp.wait_ge(vg_out, 2 * n + 2)
                sp.dma_start(v_view[:, :, at, :], v_st[:, n % 2, :, :]).then_inc(v_store[n % 2], 16)
                sp.wait_ge(kt_out, 2 * n + 2)
                sp.dma_start(k_view[:, :, at, :], kT_st[:, n % 2, :, :]).then_inc(k_store[n % 2], 16)
            for b in range(B):
                sp.wait_ge(v_store[b], 16 * (ROWS // 2))
                sp.wait_ge(k_store[b], 16 * (ROWS // 2))
            sp.dma_start(k.k_raw0[:], k.kT_dram[0, :, 0:KEYS]).then_inc(k.k_in[0], 16)

        @block.gpsimd
        def _(pool):
            nc.gpsimd.memset(ident[:], 0.0).then_inc(const, 1)
            nc.gpsimd.iota(rel[:], [[1, S]], base=-P, channel_multiplier=-1,
                           allow_small_or_imprecise_dtypes=True).then_inc(const, 1)
            nc.gpsimd.memset(ones[:], 1.0).then_inc(const, 1)
            pool.wait_ge(const, 3)
            nc.gpsimd.affine_select(out=ident[:], in_=ident[:], compare_op=ALU.not_equal, fill=1.0, base=0,
                                    pattern=[[-1, P]], channel_multiplier=1).then_inc(const, 1)
            nc.gpsimd.affine_select(out=rel[:], in_=rel[:], compare_op=ALU.is_ge, fill=MASKED, base=P,
                                    pattern=[[-1, S]], channel_multiplier=1).then_inc(const, 1)
            pool.wait_ge(const, 5)

            def late_lo(p):
                for i in range(KT):
                    pool.wait_ge(w_his, KT * p + i + 1)
                    hi, lo = split_of(p, i)
                    nc.gpsimd.tensor_tensor(lo, w_raw[:, i, :], f32(hi), ALU.subtract).then_inc(late_los, 1)

            def alibi(h):
                if h >= 2:
                    pool.wait_ge(s_out, 2 * (h - 1))
                nc.gpsimd.tensor_scalar(bias[:, h % 2, :], rel[:], SLOPES[h] / SA_SCALE, 1.0, ALU.mult, ALU.mult)\
                    .then_inc(bias_made, 1)

            alibi(0)
            alibi(1)
            late_lo(3)
            late_lo(4)
            for what, a in ORDER:
                if what == "S" and a % 2 == 1 and a // 2 + 2 < SA_HEADS:
                    alibi(a // 2 + 2)
                    if a in (1, 3, 17):
                        late_lo({1: 5, 3: 6, 17: 7}[a])
                elif what == "part" and a % PARTS == 5 and a // PARTS < ROWS:
                    pool.wait_ge(kms_made, a // PARTS + 1)
                    nc.gpsimd.tensor_tensor(k_inv[:], k_ms[:], minus_half[:, 0:KVH], ALU.pow).then_inc(kinv_made, 1)
                elif what == "Y":
                    done = LN_ORDER.index(a) + 1
                    pool.wait_ge(var_made, done)
                    nc.gpsimd.tensor_tensor(rstd[:, a:a + 1], var[:, a:a + 1], minus_half[:, 0:1], ALU.pow)\
                        .then_inc(rstd_made, 1)

        @block.scalar
        def _(act):
            def weights_hi(p, i):
                act.wait_ge(w_in[i], 16 * (p + 1))
                nc.scalar.activation(split_of(p, i)[0], w_raw[:, i, :], ACT.Copy).then_inc(w_his, 1)

            def context_hi(n):
                act.wait_ge(ct_ps, n + 1)
                nc.scalar.activation(cT_hi[:, n % 2, :, :], bank[:, TRANSPOSED, :].rearrange("p (k t) -> p k t", k=KT),
                                     ACT.Copy).then_inc(ct_hi, 1)

            def exponentials(n):
                h, b = pairs[n]
                act.wait_ge(nm_made, n + 1)
                for qt, (a, e) in enumerate(((0, P), (P, 3 * P))):
                    nc.scalar.activation(s_sb[:, n % 2, a:e], s_sb[:, n % 2, a:e], ACT.Exp,
                                         bias=nm[:, n % 2, qt:qt + 1], scale=SA_SCALE,
                                         accum_out=rsum[:, 2 * b + qt, h:h + 1]).then_inc(p_made, 1)

            def part(n, r):
                if r in (2, 4):
                    g = r // 2 - 1
                    w = slice(GH * g, GH * (g + 1))
                    if n >= 1:
                        act.wait_ge(kt_ps, 2 * n - 1 + g)
                        if n >= 3:
                            act.wait_ge(k_store[(n - 1) % 2], 16 * ((n - 1) // 2))
                        nc.scalar.activation(kT_st[:, (n - 1) % 2, w, :].rearrange("p h e -> p (h e)"),
                                             bank[:, TRANSPOSED, :], ACT.Copy, scale=nw[:]).then_inc(kt_out, 1)
                    if n < ROWS:
                        act.wait_ge(g_ps, 4 * n + g + 1)
                        if n >= 1:
                            act.wait_ge(knrm_made, n)
                        nc.scalar.activation(k_raw[:, w, :].rearrange("p h e -> p (h e)"), bank[:, GROUP + g, :], ACT.Copy)\
                            .then_inc(kg_out, 1)
                        act.wait_ge(kg_out, 2 * n + g + 1)
                        if 2 * n + g >= 1:
                            act.wait_ge(kss_made, 2 * n + g)
                        nc.scalar.activation(k_sq[:], k_raw[:, w, :], ACT.Square).then_inc(ksq_made, 1)
                elif r == 6 and n + 1 < B * CT:
                    context_hi(n + 1)

            for j in range(TT):
                act.wait_ge(xt_ps, j + 1)
                nc.scalar.activation(xT_hi[:, :, tokens(j)], bank[:, j, :].rearrange("p (k t) -> p k t", k=KT), ACT.Copy)\
                    .then_inc(xt_hi, 1)
            for i in range(KT):
                weights_hi(0, i)
            act.wait_ge(col_ps, 1)
            nc.scalar.activation(cols[:], bank[:, 7, 0:2 * KT + 2], ACT.Copy).then_inc(col_out, 1)
            for i in range(KT):
                weights_hi(1, i)
            act.wait_ge(col_out, 1)
            for m in range(KT):
                act.wait_ge(qk_ps, m + 1)
                nc.scalar.activation(qT[:, m, :], bank[:, 4 + m, :], ACT.Identity, bias=cols[:, m:m + 1])\
                    .then_inc(q_out, 1)
                weights_hi(2, m)
            for i in range(KT):
                weights_hi(3, i)
            act.wait_ge(qk_ps, 2 * KT)
            for i in range(KT):
                weights_hi(4, i)
            for i in range(TT):
                act.wait_ge(v_ps, i + 1)
                nc.scalar.activation(v[:, i, :], bank[:, 4 + i, :], ACT.Copy).then_inc(v_out, 1)
            context_hi(0)
            act.wait_ge(nw_made, 1)
            for what, a in ORDER:
                if what == "S":
                    exponentials(a)
                    if a in (1, 3, 17):
                        for i in range(KT):
                            weights_hi({1: 5, 3: 6, 17: 7}[a], i)
                elif what == "part":
                    part(a // PARTS, a % PARTS)
                elif what == "AT":
                    done = LN_ORDER.index(a) + 1
                    act.wait_ge(at_ps, done)
                    nc.scalar.activation(xT_hi[:, :, tokens(a)], bank[:, a, :].rearrange("p (k t) -> p k t", k=KT), ACT.Copy)\
                        .then_inc(at_hi, 1)
                elif what == "XT":
                    done = LN_ORDER.index(a) + 1
                    act.wait_ge(x1t_ps, done)
                    nc.scalar.activation(xT_hi[:, :, tokens(a)], bank[:, a, :].rearrange("p (k t) -> p k t", k=KT), ACT.Copy)\
                        .then_inc(x1t_hi, 1)
                elif what == "WQ":
                    act.wait_ge(y_ps, TT)
                    for i in range(KT):
                        weights_hi(8, i)
                elif what == "Q":
                    act.wait_ge(q_ps, a + 1)
                    nc.scalar.activation(k.q[:, a, :], bank[:, a, :], ACT.Copy).then_inc(q_rows_out, 1)

        @block.vector
        def _(dve):
            nc.vector.memset(even[:], 0.0).then_inc(mask, 1)
            nc.vector.memset(minus_half[:], -0.5).then_inc(mask, 1)
            dve.wait_ge(mask, 2)
            for g in range(P // 32):
                nc.vector.memset(even[32 * g:32 * g + SA_DIM, :], 1.0).then_inc(mask, 1)
            dve.wait_ge(mask, 6)
            nc.vector.tensor_scalar(odd[:], even[:], -1.0, 1.0, ALU.mult, ALU.add).then_inc(mask, 1)

            def early_lo(p, i):
                dve.wait_ge(w_his, KT * p + i + 1)
                nc.vector.tensor_tensor(w_lo[:, SLOT[p], i, :], w_raw[:, i, :], f32(w_hi[:, SLOT[p], i, :]),
                                        ALU.subtract).then_inc(w_los, 1)

            def context_lo(n):
                dve.wait_ge(ct_hi, n + 1)
                nc.vector.tensor_tensor(cT_lo[:, n % 2, :, :], bank[:, TRANSPOSED, :].rearrange("p (k t) -> p k t", k=KT),
                                        f32(cT_hi[:, n % 2, :, :]), ALU.subtract).then_inc(ct_lo, 1)

            def softmax_shift(n):
                h = pairs[n][0]
                dve.wait_ge(s_ps, n + 1)
                dve.wait_ge(bias_made, h + 1)
                for qt, (a, e, rel0) in enumerate(((0, P, P), (P, 3 * P, 0))):
                    nc.vector.tensor_tensor_reduce(out=s_sb[:, n % 2, a:e], in0=bank[:, n % 2, a:e],
                                                   in1=bias[:, h % 2, rel0:S], scale=1.0, scalar=-3e38,
                                                   op0=ALU.add, op1=ALU.max,
                                                   accum_out=mx[:, n % 2, qt:qt + 1])\
                        .then_inc(s_out if qt else s_half, 1)
                dve.wait_ge(s_half, n + 1)
                dve.wait_ge(s_out, n + 1)
                nc.vector.tensor_scalar(nm[:, n % 2, :], mx[:, n % 2, :], -SA_SCALE, None, ALU.mult)\
                    .then_inc(nm_made, 1)

            def take_transposed(n):
                dve.wait_ge(pt_ps, n + 1)
                if n >= 2:
                    dve.wait_ge(o_ps, n - 1)
                nc.vector.tensor_copy(pT[:, n % 2, :], bank[:, 2 + n % 2, 0:3 * P]).then_inc(pt_out, 1)

            def take_attention(m):
                w = slice(PER_TILE * m, PER_TILE * (m + 1))
                dve.wait_ge(p_made, 4 * PER_TILE * (m + 1))
                nc.vector.reciprocal(rinv[:, :, w], rsum[:, :, w]).then_inc(rinv_made, 1)
                dve.wait_ge(rinv_made, m + 1)
                dve.wait_ge(o_ps, 2 * PER_TILE * (m + 1))
                nc.vector.tensor_tensor(att[:, :, m * P:(m + 1) * P].rearrange("p t (h e) -> p t h e", e=SA_DIM),
                                        bank[:, 4, :].rearrange("p (t h e) -> p t h e", t=TT, e=SA_DIM),
                                        rinv[:, :, w].rearrange("p t (h a) -> p t h a", a=1)
                                        .to_broadcast([P, TT, PER_TILE, SA_DIM]), ALU.mult).then_inc(att_out, 1)

            def take_values(n, g):
                dve.wait_ge(g_ps, 4 * n + g + 3)
                if n >= 2:
                    dve.wait_ge(v_store[n % 2], 16 * (n // 2))
                nc.vector.tensor_copy(v_st[:, n % 2, GH * g:GH * (g + 1), :].rearrange("p h e -> p (h e)"),
                                      bank[:, GROUP + g, :]).then_inc(vg_out, 1)

            def part(n, r):
                if r == 0 and n >= 1:
                    take_values(n - 1, 1)
                if n == ROWS:
                    return
                if r in (3, 5):
                    g = r // 2 - 1
                    dve.wait_ge(ksq_made, 2 * n + g + 1)
                    nc.vector.tensor_reduce(k_ss[:, GH * g:GH * (g + 1)], k_sq[:], AX.X, ALU.add).then_inc(kss_made, 1)
                if r == 5:
                    dve.wait_ge(kss_made, 2 * n + 2)
                    nc.vector.tensor_scalar(k_ms[:], k_ss[:], 1.0 / HD, RMS_EPS, ALU.mult, ALU.add).then_inc(kms_made, 1)
                elif r == 6:
                    if n + 1 < B * CT:
                        context_lo(n + 1)
                    take_values(n, 0)
                elif r == 7:
                    dve.wait_ge(kinv_made, n + 1)
                    if n >= 1:
                        dve.wait_ge(kt_ps, 2 * n)
                    nc.vector.tensor_tensor(k_nrm[:], k_raw[:], k_inv[:].rearrange("p (h a) -> p h a", a=1)
                                            .to_broadcast([P, KVH, HD]), ALU.mult).then_inc(knrm_made, 1)

            for j in range(TT):
                dve.wait_ge(xt_hi, j + 1)
                nc.vector.tensor_tensor(xT_lo[:, :, tokens(j)], bank[:, j, :].rearrange("p (k t) -> p k t", k=KT),
                                        f32(xT_hi[:, :, tokens(j)]), ALU.subtract).then_inc(xt_lo, 1)
            for p in range(2):
                for i in range(KT):
                    early_lo(p, i)
            dve.wait_ge(col_out, 1)
            nc.vector.tensor_tensor(nw[:], cols[:, 2 * KT:2 * KT + 1], cols[:, 2 * KT + 1:2 * KT + 2], ALU.mult)\
                .then_inc(nw_made, 1)
            for i in range(KT):
                early_lo(2, i)
            dve.wait_ge(mask, 7)
            for m in range(KT):
                dve.wait_ge(qk_ps, KT + m + 1)
                for dst, keep in ((kT_even, even), (kT_odd, odd)):
                    nc.vector.tensor_scalar(dst[:, m, :], bank[:, 4 + m, :], cols[:, KT + m:KT + m + 1],
                                            keep[:], ALU.add, ALU.mult).then_inc(k_out, 1)
            context_lo(0)
            for what, a in vector_order(ORDER):
                if what == "S":
                    softmax_shift(a)
                elif what == "T":
                    take_transposed(a)
                elif what == "PV" and (a + 1) % (2 * PER_TILE) == 0:
                    take_attention(a // (2 * PER_TILE))
                elif what == "part":
                    part(a // PARTS, a % PARTS)
                elif what == "AT":
                    done = LN_ORDER.index(a) + 1
                    dve.wait_ge(at_hi, done)
                    nc.vector.tensor_tensor(xT_lo[:, :, tokens(a)], bank[:, a, :].rearrange("p (k t) -> p k t", k=KT),
                                            f32(xT_hi[:, :, tokens(a)]), ALU.subtract).then_inc(at_lo, 1)
                elif what == "Y":
                    done = LN_ORDER.index(a) + 1
                    dve.wait_ge(y_ps, done)
                    nc.vector.tensor_tensor(x[:, a, :], bank[:, a, :], x[:, a, :], ALU.add).then_inc(y_sum, 1)
                    dve.wait_ge(y_sum, done)
                    nc.vector.bn_stats(stats[:, a, :], x[:, a, :]).then_inc(y_stats, 1)
                    dve.wait_ge(y_stats, done)
                    nc.vector.bn_aggr(mv[:, a, :], stats[:, a, :]).then_inc(y_mv, 1)
                    dve.wait_ge(y_mv, done)
                    nc.vector.tensor_scalar(var[:, a:a + 1], mv[:, a, 1:2], LN_EPS, None, ALU.add).then_inc(var_made, 1)
                elif what == "LN":
                    dve.wait_ge(rstd_made, LN_ORDER.index(a) + 1)
                    nc.vector.tensor_scalar(x[:, a, :], x[:, a, :], mv[:, a, 0:1], rstd[:, a:a + 1],
                                            ALU.subtract, ALU.mult).then_inc(x1_made, 1)
                elif what == "XT":
                    done = LN_ORDER.index(a) + 1
                    dve.wait_ge(x1t_hi, done)
                    nc.vector.tensor_tensor(xT_lo[:, :, tokens(a)], bank[:, a, :].rearrange("p (k t) -> p k t", k=KT),
                                            f32(xT_hi[:, :, tokens(a)]), ALU.subtract).then_inc(x1t_lo, 1)
                elif what == "WQ":
                    for i in range(KT):
                        dve.wait_ge(w_his, KT * 8 + i + 1)
                        nc.vector.tensor_tensor(k.wq_lo[:, i, :], w_raw[:, i, :], f32(k.wq_hi[:, i, :]), ALU.subtract)\
                            .then_inc(wq_los, 1)
                elif what == "Q" and a < TT - 1:
                    dve.wait_ge(q_rows_out, a + 1)
                    for g in range(GRP):
                        w = slice(g * HD, (g + 1) * HD)
                        nc.vector.tensor_tensor_reduce(out=k.q_sq[:, a, w], in0=bank[:, a, w], in1=k.q[:, a, w],
                                                       scale=1.0, scalar=0.0, op0=ALU.mult, op1=ALU.add,
                                                       accum_out=k.q_ss[:, a * GRP + g:a * GRP + g + 1])\
                            .then_inc(ss_part, 1)

        @block.tensor
        def _(pe):
            pe.wait_ge(const, 5)
            for j in range(TT):
                pe.wait_ge(x_in[j], 16)
                for i in range(KT):
                    last = nc.tensor.transpose(bank[:, j, tokens(i)], x[:, j, i * P:(i + 1) * P], ident[:])
                last.then_inc(xt_ps, 1)
            pe.wait_ge(xt_lo, TT)
            for m in range(2 * KT):
                if m == 1:
                    pe.wait_ge(bias_in, 64)
                    nc.tensor.transpose(bank[:, 7, 0:2 * KT + 2], col_rows[:], ident[0:2 * KT + 2, 0:2 * KT + 2])\
                        .then_inc(col_ps, 1)
                if m == 3:
                    pe.wait_ge(col_out, 1)
                if m >= KT:
                    pe.wait_ge(q_out, m - KT + 1)
                w = tokens(m % KT)
                for i in range(KT):
                    if m % KT == 0:
                        pe.wait_ge(w_los, m + i + 1)
                    last = three_passes(nc, bank[:, 4 + m % KT, :], w_hi[:, m // KT, i, w], w_lo[:, m // KT, i, w],
                                        xT_hi[:, i, :], xT_lo[:, i, :], i == 0, i == KT - 1)
                last.then_inc(qk_ps, 1)
            pe.wait_ge(w_los, 3 * KT)
            for j in range(TT):
                pe.wait_ge(k_out, 2 * (j + 1))
                nc.tensor.matmul(bank[:, 4 + j, :], ones[:], row_bias[:], start=True, stop=False)
                for i in range(KT):
                    last = three_passes(nc, bank[:, 4 + j, :], xT_hi[:, i, tokens(j)], xT_lo[:, i, tokens(j)],
                                        w_hi[:, 2, i, :], w_lo[:, 2, i, :], False, i == KT - 1)
                last.then_inc(v_ps, 1)

            def scores(n):
                h, b = pairs[n]
                m, r = h // PER_TILE, 32 * (h % PER_TILE // 2)
                keys = kT_odd if h % 2 else kT_even
                if n >= 2:
                    pe.wait_ge(s_out, n - 1)
                nc.tensor.matmul(bank[:, n % 2, 0:P], qT[r:r + 32, m, b * S:b * S + P],
                                 keys[r:r + 32, m, b * S:b * S + P], start=True, stop=True)
                nc.tensor.matmul(bank[:, n % 2, P:3 * P], qT[r:r + 32, m, b * S + P:b * S + S],
                                 keys[r:r + 32, m, b * S:b * S + S], start=True, stop=True).then_inc(s_ps, 1)

            def transposes(n):
                pe.wait_ge(p_made, 2 * (n + 1))
                if n >= 2:
                    pe.wait_ge(pt_out, n - 1)
                for j in range(3):
                    last = nc.tensor.transpose(bank[:, 2 + n % 2, tokens(j)], s_sb[:, n % 2, tokens(j)], ident[:])
                last.then_inc(pt_ps, 1)

            def weigh_values(n):
                h, b = pairs[n]
                w = slice(h * SA_DIM, (h + 1) * SA_DIM)
                pe.wait_ge(pt_out, n + 1)
                if n > 0 and n % (2 * PER_TILE) == 0:
                    pe.wait_ge(att_out, n // (2 * PER_TILE))
                for qt, kt, start, stop in ((0, 0, True, True), (1, 0, True, False), (1, 1, False, True)):
                    at = (2 * b + qt) * P + h % PER_TILE * SA_DIM
                    last = nc.tensor.matmul(bank[:, 4, at:at + SA_DIM], pT[:, n % 2, tokens(qt + kt)],
                                            v[:, 2 * b + kt, w], start=start, stop=stop)
                last.then_inc(o_ps, 1)

            def context_transposes(n):
                pe.wait_ge(c_in[n % 2], 16 * (n // 2 + 1))
                if n >= 2:
                    pe.wait_ge(kt_out, 2 * (n - 1))
                for i in range(KT):
                    last = nc.tensor.transpose(bank[:, TRANSPOSED, tokens(i)], c_raw[:, n % 2, tokens(i)], ident[:])
                last.then_inc(ct_ps, 1)

            def key_transposes(n, g):
                if g == 0:
                    pe.wait_ge(knrm_made, n + 1)
                if 2 * n + g >= 1:
                    pe.wait_ge(kt_out, 2 * n + g)
                for h in range(GH):
                    last = nc.tensor.transpose(bank[:, TRANSPOSED, tokens(h)], k_nrm[:, GH * g + h, :], ident[:])
                last.then_inc(kt_ps, 1)

            def part(n, r):
                which, g = r // 4, r // 2 % 2
                if r in (1, 3) and n >= 1:
                    key_transposes(n - 1, r // 2)
                if n == ROWS:
                    return
                if r == 5 and n + 1 < B * CT:
                    context_transposes(n + 1)
                if r % 2 == 0:
                    if which == 1:
                        pe.wait_ge(kg_out, 2 * n + g + 1)
                    elif n >= 1:
                        pe.wait_ge(vg_out, 2 * n - 1 + g)
                    if n == 0:
                        pe.wait_ge(late_los, KT * (r // 2 + 1))
                if n < B * CT:
                    if r == 0:
                        pe.wait_ge(ct_lo, n + 1)
                    rows_hi, rows_lo = cT_hi[:, n % 2, :, :], cT_lo[:, n % 2, :, :]
                else:
                    if r == 0:
                        pe.wait_ge(x1t_lo, n - B * CT + 1)
                    w = tokens(LN_ORDER[n - B * CT])
                    rows_hi, rows_lo = xT_hi[:, :, w], xT_lo[:, :, w]
                slot = SLOT[3 + r // 2]
                for i in range(2 * (r % 2), 2 * (r % 2) + 2):
                    last = three_passes(nc, bank[:, GROUP + g, :], rows_hi[:, i, :], rows_lo[:, i, :],
                                        w_hi[:, slot, i, :], w_lo[:, slot, i, :], i == 0, i == KT - 1)
                if r % 2:
                    last.then_inc(g_ps, 1)

            pe.wait_ge(v_out, TT)
            context_transposes(0)
            for what, a in ORDER:
                if what == "S":
                    scores(a)
                elif what == "T":
                    transposes(a)
                elif what == "PV":
                    weigh_values(a)
                elif what == "part":
                    part(a // PARTS, a % PARTS)
                elif what == "AT":
                    pe.wait_ge(att_out, KT)
                    pe.wait_ge(pt_out, HB)
                    for i in range(KT):
                        last = nc.tensor.transpose(bank[:, a, tokens(i)], att[:, a, i * P:(i + 1) * P], ident[:])
                    last.then_inc(at_ps, 1)
                elif what == "Y":
                    pe.wait_ge(late_los, 5 * KT)
                    pe.wait_ge(bias_in, 80)
                    pe.wait_ge(at_lo, LN_ORDER.index(a) + 1)
                    nc.tensor.matmul(bank[:, a, :], ones[:], row_bias[:], start=True, stop=False)
                    for i in range(KT):
                        last = three_passes(nc, bank[:, a, :], xT_hi[:, i, tokens(a)], xT_lo[:, i, tokens(a)],
                                            k.wq_hi[:, i, :], k.wq_lo[:, i, :], False, i == KT - 1)
                    last.then_inc(y_ps, 1)
                elif what == "XT":
                    pe.wait_ge(x1_made, LN_ORDER.index(a) + 1)
                    for i in range(KT):
                        last = nc.tensor.transpose(bank[:, a, tokens(i)], x[:, a, i * P:(i + 1) * P], ident[:])
                    last.then_inc(x1t_ps, 1)
                elif what == "Q":
                    if a == 0:
                        pe.wait_ge(x1t_lo, TT)
                        pe.wait_ge(wq_los, KT)
                    for i in range(KT):
                        last = three_passes(nc, bank[:, a, :], xT_hi[:, i, tokens(a)], xT_lo[:, i, tokens(a)],
                                            k.wq_hi[:, i, :], k.wq_lo[:, i, :], i == 0, i == KT - 1)
                    last.then_inc(q_ps, 1)


UNITS = 2 * B
UT = 4
TILES = UNITS * UT
PIECE = 4
RING = 3

FILLERS = ((("W", 2), ("QT", 2), ("QT", 3), ("W", 3)),
           (("Q", 0), None, None, ("Q", 1)),
           (("Q", 2), ("QT", 0), ("QT", 1), ("W", 0)),
           (("Q", 3), None, None, ("W", 1)))


LAST_FILLERS = ((("W", 2), ("QT", 2), ("QT", 3), None),
                (("W", 3), None, None, None),
                (None, None, None, ("W", 0)),
                (None, None, None, ("W", 1)))


class Turn:

    BEFORE = 2
    EACH = UNITS * KTL + 2 * TT + TT

    def __init__(self, i, first=False, more=True, ahead=True):
        self.i, self.first, self.more, self.ahead = i, first, more, ahead
        begin, shift = (self.BEFORE, 0) if first else (self.BEFORE - 2 + self.EACH * i, self.BEFORE - 2)
        shift = self.BEFORE if first else shift
        self.use, self.bank = {}, {}
        n = 0
        for s in range(UNITS):
            for what, a in self.tensor_order(s):
                if what in ("T", "Q", "QT", "W"):
                    self.use[s, what, a] = begin + n
                    self.bank[s, what, a] = 4 + (shift + n) % RING
                    n += 1
        self.end = begin + n
        self.pieces = 2 * PIECE + 4 * PIECE * i - (0 if more else PIECE)

    def fillers(self, s):
        kept = []
        for f in (FILLERS if self.more else LAST_FILLERS)[s]:
            from_before = s == 0 and f is not None and f[0] == "W"
            of_next = f is not None and (f[0] == "Q" or s == 2 and f[0] == "QT")
            kept.append(None if from_before and self.first or of_next and not self.more else f)
        return kept

    def scored(self, s):
        return self.more or s < UNITS - 1

    def tensor_order(self, s):
        f = self.fillers(s)
        order = [("T", 0), ("S", 0), ("T", 1), f[0], f[1], ("T", 2), ("O", 0), ("S", 1), ("T", 3), ("O", 1),
                 ("S", 2), ("T", 4), ("O", 2), ("S", 3), ("T", 5), ("O", 3), f[2], f[3], ("O", 4), ("O", 5)]
        if not self.scored(s):
            order.append(order.pop(-3))
        return [e for e in order if e is not None and (e[0] != "S" or self.scored(s))]

    def scalar_order(self, s):
        f = self.fillers(s)
        order = [("T", 0), ("T", 1), ("E", 0), f[0], f[1], ("T", 2), ("T", 3), ("E", 1), ("T", 4), ("E", 2),
                 ("T", 5), ("E", 3), f[2], f[3], ("O", 0)]
        return [e for e in order if e is not None and (e[0] != "E" or self.scored(s))]

    def vector_order(self, s):
        f = self.fillers(s)
        order = [("T", 0), ("M", 0), ("T", 1), ("I", 0), f[0], f[1], ("T", 2), ("M", 1), ("T", 3), ("M", 2), ("I", 1),
                 ("T", 4), ("M", 3), ("I", 2), ("T", 5), ("I", 3), f[2], f[3], ("O", 0)]
        if not self.scored(s):
            order.append(order.pop(-2))
        return [e for e in order if e is not None and (e[0] not in "MI" or self.scored(s))]


assert Turn.EACH % RING == 0


def cross_attention(nc, d, k):
    with ExitStack() as ctx:
        t = Tensors(nc, ctx)
        k_raw = (k.k_raw0, t.sb("xk_raw1", [P, KEYS]))
        v_raw = t.sb("xv_raw", [P, B, KEYS])
        k_hi = t.sb("xk_hi", [P, B, KEYS], F32R)
        k_lo = t.sb("xk_lo", [P, B, KEYS], F32R)
        v_hi = t.sb("xv_hi", [P, B, KEYS], F32R)
        v_lo = t.sb("xv_lo", [P, B, KEYS], F32R)
        wq_raw, wq_hi, wq_lo = k.wq_raw, k.wq_hi, k.wq_lo
        wo_raw = t.sb("wo_raw", [P, GRP, D])
        wo_hi = t.sb("wo_hi", [P, GRP, D], F32R)
        wo_lo = t.sb("wo_lo", [P, GRP, D], F32R)
        q, q_sq, q_ss, q_ms, q_inv, q_rms, minus_half = k.q, k.q_sq, k.q_ss, k.q_ms, k.q_inv, k.q_rms, k.minus_half
        qT_hi = t.sb("qT_hi", [P, GRP, TOK], F32R)
        qT_lo = t.sb("qT_lo", [P, GRP, TOK], F32R)
        prob = t.sb("prob", [P, 2 * UT, KEYS])
        mx = t.sb("x_mx", [P, 2 * UT])
        nm = t.sb("x_nm", [P, 2 * UT])
        rsum = t.sb("x_rsum", [P, 2 * UT])
        rinv = t.sb("x_rinv", [P, 2 * UT])
        pT_hi = t.sb("pT_hi", [P, KTL, UT * P], F32R)
        pT_lo = t.sb("pT_lo", [P, KTL, UT * P], F32R)
        oT_hi = t.sb("oT_hi", [P, GRP, TOK], F32R)
        oT_lo = t.sb("oT_lo", [P, GRP, TOK], F32R)
        x, bank, ident = k.x, k.bank, k.ident

        k_in = k.k_in
        v_in = [t.sem("xv_in0"), t.sem("xv_in1")]
        wq_in, wo_in = t.sem("wq_in"), t.sem("wo_in")
        piece_hi = t.sem("piece_hi")
        k_split, v_split, wq_split, wo_split = t.sem("xk_split"), t.sem("xv_split"), t.sem("wq_split"), t.sem("wo_split")
        ring_full = t.sem("ring_full")
        ring_out = t.sem("ring_out")
        q_out, qt_his = t.sem("xq_out"), t.sem("qt_his")
        ss_part, ms_made = t.sem("ss_part"), t.sem("ms_made")
        first_ss, first_ms = t.sem("first_ss"), t.sem("first_ms")
        first_hi, first_inv, first_rms = t.sem("first_keys_hi"), t.sem("first_inv"), t.sem("first_rms")
        flag, begun = t.sb("flag", [P, 1]), t.sem("begun")
        inv_made, rms_made = t.sem("inv_made"), t.sem("rms_made")
        s_full, mx_made, nm_made = t.sem("s_full"), t.sem("x_mx_made"), t.sem("x_nm_made")
        exp_made, rinv_made, prob_made = t.sem("exp_made"), t.sem("x_rinv_made"), t.sem("prob_made")
        pt_his = t.sem("pt_his")
        o_full, o_his, o_out = t.sem("o_full"), t.sem("o_his"), t.sem("o_out")
        x_stats, x_mv, var_made, rstd_made, x2_made = (t.sem("x_stats"), t.sem("x_mv"), t.sem("x_var"), t.sem("x_rstd"),
                                                       t.sem("x2_made"))
        perm_in, index_made, perm_made, matrix_made = (t.sem("perm_in"), t.sem("index_made"), t.sem("perm_made"),
                                                       t.sem("matrix_made"))
        perm_row_i, perm_row, index_row = wq_raw[:, 0, :].bitcast(I32), wq_raw[:, 1, :], wq_raw[:, 2, :]
        perm_cols_i, perm_cols = wq_raw[:, 3, 0:KT].bitcast(I32), wq_raw[:, 3, KT:2 * KT]
        index_col = wq_raw[:, 3, 2 * KT:3 * KT]
        block = ctx.enter_context(nc.Block())

        def turns(eng, body):
            body(Turn(0, first=True))
            with eng.Fori(1, KVH - 2) as i:
                body(Turn(i))
            body(Turn(KVH - 2, ahead=False))
            body(Turn(KVH - 1, more=False, ahead=False))

        def first_bank(use):
            return 4 + use % RING

        last_use = Turn(KVH - 1, more=False, ahead=False).end
        last_banks = [4 + (last_use + r) % RING for r in range(2)]

        def tile_of(u, j):
            return 2 * (u % 2) + j // 2, 2 * (u // 2) + j % 2

        def column(u, j):
            g, tt = tile_of(u, j)
            return slice(tt * GRP + g, tt * GRP + g + 1)

        def columns(b):
            return slice(2 * b * GRP, 2 * (b + 1) * GRP)

        @block.sync
        def _(sp):
            wq_view = d["Wq"].rearrange("(k p) (h n) -> h p k n", p=P, n=D)
            wo_view = d["Wo"].rearrange("(h g p) n -> h p g n", p=HD, g=GRP)

            def load_keys(b, i):
                sp.dma_start(k_raw[b][:], k.kT_dram[i, :, b * KEYS:(b + 1) * KEYS]).then_inc(k_in[b], 16)

            def load_values(b, i):
                sp.dma_start(v_raw[:, b, :], k.v_dram[i, :, b * KEYS:(b + 1) * KEYS]).then_inc(v_in[b], 16)

            def load_wq(i):
                sp.dma_start(wq_raw[:], wq_view[i, :, :, :]).then_inc(wq_in, 16)

            def load_wo(i):
                sp.dma_start(wo_raw[:], wo_view[i, :, :, :]).then_inc(wo_in, 16)

            load_keys(1, 0)
            for b in range(B):
                load_values(b, 0)
            load_wq(1)
            load_wo(0)
            sp.wait_ge(k_split, 2)
            load_keys(0, 1)
            sp.wait_ge(v_split, 2)
            load_values(0, 1)
            sp.wait_ge(k_split, 4)
            load_keys(1, 1)
            sp.wait_ge(wq_split, PIECE)
            load_wq(2)

            def this_head(i):
                sp.wait_ge(v_split, PIECE * i + 4)
                load_values(1, i + 1)
                sp.wait_ge(wo_split, PIECE * i + PIECE)
                load_wo(i + 1)

            def next_head(i):
                sp.wait_ge(k_split, PIECE * i + 6)
                load_keys(0, i + 2)
                sp.wait_ge(v_split, PIECE * i + 6)
                load_values(0, i + 2)
                sp.wait_ge(k_split, PIECE * i + 8)
                load_keys(1, i + 2)

            with sp.Fori(0, KVH - 3) as i:
                this_head(i)
                next_head(i)
                sp.wait_ge(wq_split, PIECE * i + 2 * PIECE)
                load_wq(i + 3)
            this_head(KVH - 3)
            next_head(KVH - 3)
            this_head(KVH - 2)
            sp.wait_ge(wq_split, PIECE * (KVH - 1))
            sp.dma_start(perm_row_i, d["perm"].rearrange("(a n) -> a n", a=1).to_broadcast([P, D])).then_inc(perm_in, 16)
            sp.dma_start(perm_cols_i, d["perm"].rearrange("(k p) -> p k", p=P), allow_slow_non_contiguous=True)\
                .then_inc(perm_in, 16)

        @block.gpsimd
        def _(pool):
            awaited = pool.alloc_register("awaited")

            def wait_alone(sem, value):
                if not isinstance(value, int):
                    pool.reg_mov(awaited, value)
                    value = awaited
                pool.wait_ge(begun, 1)
                pool.wait_ge(sem, value)

            def split(hi, lo, raw, count, done):
                nc.gpsimd.tensor_scalar(hi, raw, 1.0, 1.0, ALU.mult, ALU.mult).then_inc(piece_hi, 1)
                pool.wait_ge(piece_hi, count + 1)
                nc.gpsimd.tensor_tensor(lo, raw, f32(hi), ALU.subtract).then_inc(done, 1)

            def keys(b, piece, i, count):
                w = slice(piece * HALF, (piece + 1) * HALF)
                wait_alone(k_in[b], 16 * i + 16)
                split(k_hi[:, b, w], k_lo[:, b, w], k_raw[b][:, w], count, k_split)

            def values(b, piece, i, count):
                w = slice(piece * HALF, (piece + 1) * HALF)
                wait_alone(v_in[b], 16 * i + 16)
                split(v_hi[:, b, w], v_lo[:, b, w], v_raw[:, b, w], count, v_split)

            def query_weights(piece, i, count):
                wait_alone(wq_in, 16 * i)
                split(wq_hi[:, piece, :], wq_lo[:, piece, :], wq_raw[:, piece, :], count, wq_split)

            def output_weights(piece, i, count):
                wait_alone(wo_in, 16 * i + 16)
                split(wo_hi[:, piece, :], wo_lo[:, piece, :], wo_raw[:, piece, :], count, wo_split)

            def inverse_rms(b, i):
                pool.wait_ge(ms_made, 2 * i + b - 1)
                nc.gpsimd.tensor_tensor(q_inv[:, columns(b)], q_ms[:, columns(b)], minus_half[:, columns(b)], ALU.pow)\
                    .then_inc(inv_made, 1)

            def norm(n, s):
                wait_alone(rinv_made, n + 1)
                nc.gpsimd.tensor_scalar(prob[:, s, :], prob[:, s, :], rinv[:, s:s + 1], 1.0, ALU.mult, ALU.mult)\
                    .then_inc(prob_made, 1)

            pool.wait_ge(first_ms, 1)
            nc.gpsimd.tensor_tensor(q_inv[:], q_ms[:], minus_half[:], ALU.pow).then_inc(first_inv, 1)
            for p in range(2):
                values(0, p, 0, p)
            norm(0, 0)
            keys(1, 0, 0, 2)
            for j in range(1, UT):
                norm(j, j)
            keys(1, 1, 0, 3)
            for p in range(PIECE):
                query_weights(p, 1, PIECE + p)

            def body(turn):
                i, c = turn.i, turn.pieces

                def norms(s, tiles):
                    for j in tiles:
                        norm(TILES * i + UT * (s + 1) + j, UT * ((s + 1) % 2) + j)

                norms(0, (0,))
                if not turn.first:
                    wait_alone(o_full, UNITS * i)
                values(1, 0, i, c)
                norms(0, (1, 2, 3))
                values(1, 1, i, c + 1)
                if not turn.first:
                    wait_alone(ring_full, turn.use[0 if turn.more else 1, "W", 3] + 1)
                for p in range(2):
                    output_weights(p, i, c + 2 + p)
                norms(1, (0,))
                output_weights(2, i, c + 4)
                norms(1, (1, 2, 3))
                output_weights(3, i, c + 5)
                if turn.more:
                    for p in range(2):
                        keys(0, p, i + 1, c + 6 + p)
                norms(2, (0,))
                if turn.more:
                    wait_alone(o_full, UNITS * i + 2)
                    values(0, 0, i + 1, c + 8)
                norms(2, (1, 2, 3))
                if turn.more:
                    inverse_rms(0, i + 1)
                    values(0, 1, i + 1, c + 9)
                    for p in range(2):
                        keys(1, p, i + 1, c + 10 + p)
                    norms(3, (0,))
                    if turn.ahead:
                        wait_alone(ring_full, turn.use[3, "Q", 3] + 1)
                        query_weights(0, i + 2, c + 12)
                    norms(3, (1, 2, 3))
                    inverse_rms(1, i + 1)
                    if turn.ahead:
                        for p in range(1, PIECE):
                            query_weights(p, i + 2, c + 12 + p)

            turns(pool, body)
            nc.gpsimd.iota(index_row, [[1, D]], base=0, channel_multiplier=0,
                           allow_small_or_imprecise_dtypes=True).then_inc(index_made, 1)
            nc.gpsimd.iota(index_col, [[P, KT]], base=0, channel_multiplier=1,
                           allow_small_or_imprecise_dtypes=True).then_inc(index_made, 1)
            pool.wait_ge(perm_in, 32)
            nc.gpsimd.tensor_copy(perm_row, perm_row_i).then_inc(perm_made, 1)
            nc.gpsimd.tensor_copy(perm_cols, perm_cols_i).then_inc(perm_made, 1)
            pool.wait_ge(index_made, 2)
            pool.wait_ge(perm_made, 2)
            for i in range(KT):
                nc.gpsimd.tensor_scalar(k.gather[:, i, :], perm_row, index_col[:, i:i + 1], None, ALU.is_equal)\
                    .then_inc(matrix_made, 1)
                nc.gpsimd.tensor_scalar(k.scatter[:, i, :], index_row, perm_cols[:, i:i + 1], None, ALU.is_equal)\
                    .then_inc(matrix_made, 1)
            for i in range(TT):
                pool.wait_ge(var_made, i + 1)
                nc.gpsimd.tensor_tensor(k.rstd[:, i:i + 1], k.var[:, i:i + 1], minus_half[:, 0:1], ALU.pow)\
                    .then_inc(rstd_made, 1)

        @block.scalar
        def _(act):
            def take_queries(tt, use, at):
                act.wait_ge(ring_full, use + 1)
                nc.scalar.activation(q[:, tt, :], bank[:, at, :], ACT.Copy).then_inc(q_out, 1)

            def split_queries(tt, use, at):
                act.wait_ge(ring_full, use + 1)
                nc.scalar.activation(qT_hi[:, :, tt * P:(tt + 1) * P], bank[:, at, :].rearrange("p (g t) -> p g t", g=GRP),
                                     ACT.Copy).then_inc(qt_his, 1)

            def exponentials(n, u, j, at):
                s = UT * (u % 2) + j
                act.wait_ge(nm_made, n + 1)
                nc.scalar.activation(prob[:, s, :].rearrange("p (a e) -> p a e", a=2),
                                     bank[:, at:at + 2, 0:HALF], ACT.Exp, bias=nm[:, s:s + 1],
                                     scale=q_rms[:, column(u, j)], accum_out=rsum[:, s:s + 1]).then_inc(exp_made, 1)

            for tt in range(2):
                split_queries(tt, tt, first_bank(tt))
            act.wait_ge(k_in[0], 16)
            for p in range(2):
                w = slice(p * HALF, (p + 1) * HALF)
                nc.scalar.activation(k_hi[:, 0, w], k_raw[0][:, w], ACT.Copy).then_inc(first_hi, 1)
            for j in range(UT):
                exponentials(j, 0, j, 2 * j)

            def body(turn):
                i = turn.i
                for s in range(UNITS):
                    for what, a in turn.scalar_order(s):
                        if what == "E":
                            exponentials(TILES * i + UT * (s + 1) + a, (s + 1) % UNITS, a, 2 * (a % 2))
                        elif what == "T":
                            act.wait_ge(ring_full, turn.use[s, what, a] + 1)
                            nc.scalar.activation(pT_hi[:, a, :], bank[:, turn.bank[s, what, a], :], ACT.Copy)\
                                .then_inc(pt_his, 1)
                        elif what == "Q":
                            take_queries(a, turn.use[s, what, a], turn.bank[s, what, a])
                        elif what == "QT":
                            split_queries(a, turn.use[s, what, a], turn.bank[s, what, a])
                        elif what == "O":
                            act.wait_ge(o_full, UNITS * i + s + 1)
                            g, rows = 2 * (s % 2), slice(s // 2 * S, (s // 2 + 1) * S)
                            nc.scalar.activation(oT_hi[:, g:g + 2, rows], bank[:, 7, :].rearrange("p (g t) -> p g t", g=2),
                                                 ACT.Copy).then_inc(o_his, 1)

            turns(act, body)

        @block.vector
        def _(dve):
            nc.vector.memset(flag[:], 0.0).then_inc(begun, 1)

            def sum_squares(tt, i, use, at):
                dve.wait_ge(q_out, TT * i + tt + 1 - TT)
                for g in range(GRP):
                    w = slice(g * HD, (g + 1) * HD)
                    nc.vector.tensor_tensor_reduce(out=q_sq[:, tt, w], in0=bank[:, at, w], in1=q[:, tt, w],
                                                   scale=1.0, scalar=0.0, op0=ALU.mult, op1=ALU.add,
                                                   accum_out=q_ss[:, tt * GRP + g:tt * GRP + g + 1])\
                        .then_inc(ring_out if g == GRP - 1 else ss_part, 1)
                if tt % 2:
                    dve.wait_ge(ss_part, (GRP - 1) * (TT * i + tt + 1 - TT))
                    dve.wait_ge(ring_out, use + 1)
                    nc.vector.tensor_scalar(q_ms[:, columns(tt // 2)], q_ss[:, columns(tt // 2)], 1.0 / HD, RMS_EPS,
                                            ALU.mult, ALU.add).then_inc(ms_made, 1)

            def query_scales(b, i):
                dve.wait_ge(inv_made, 2 * i + b - 1)
                nc.vector.tensor_scalar(q_rms[:, columns(b)], q_inv[:, columns(b)], X_SCALE, None, ALU.mult)\
                    .then_inc(rms_made, 1)
                dve.wait_ge(rms_made, 2 * i + b - 1)

            def split_queries(tt, i, at):
                dve.wait_ge(qt_his, TT * i + tt + 1)
                w = slice(tt * P, (tt + 1) * P)
                nc.vector.tensor_tensor(qT_lo[:, :, w], bank[:, at, :].rearrange("p (g t) -> p g t", g=GRP),
                                        f32(qT_hi[:, :, w]), ALU.subtract).then_inc(ring_out, 1)

            def shift(n, u, j, at):
                s = UT * (u % 2) + j
                dve.wait_ge(s_full, n + 1)
                nc.vector.reduce_max(mx[:, s:s + 1], bank[:, at:at + 2, 0:HALF], AX.XY)\
                    .then_inc(mx_made, 1)
                dve.wait_ge(mx_made, n + 1)
                nc.vector.tensor_scalar(nm[:, s:s + 1], mx[:, s:s + 1], q_rms[:, column(u, j)], -1.0,
                                        ALU.mult, ALU.mult).then_inc(nm_made, 1)

            def invert_sum(n, u, j):
                s = UT * (u % 2) + j
                dve.wait_ge(exp_made, n + 1)
                nc.vector.reciprocal(rinv[:, s:s + 1], rsum[:, s:s + 1]).then_inc(rinv_made, 1)

            def add_output(tt, use, at):
                dve.wait_ge(ring_full, use + 1)
                nc.vector.tensor_tensor(x[:, tt, :], bank[:, at, :], x[:, tt, :], ALU.add).then_inc(ring_out, 1)

            for g in range(GRP):
                w = slice(g * HD, (g + 1) * HD)
                nc.vector.tensor_tensor_reduce(out=q_sq[:, TT - 1, w], in0=q[:, TT - 1, w], in1=q[:, TT - 1, w],
                                               scale=1.0, scalar=0.0, op0=ALU.mult, op1=ALU.add,
                                               accum_out=q_ss[:, (TT - 1) * GRP + g:(TT - 1) * GRP + g + 1])\
                    .then_inc(first_ss, 1)
            dve.wait_ge(first_ss, GRP)
            nc.vector.tensor_scalar(q_ms[:], q_ss[:], 1.0 / HD, RMS_EPS, ALU.mult, ALU.add).then_inc(first_ms, 1)
            for tt in range(2):
                split_queries(tt, 0, first_bank(tt))
            for p in range(2):
                w = slice(p * HALF, (p + 1) * HALF)
                dve.wait_ge(first_hi, p + 1)
                nc.vector.tensor_tensor(k_lo[:, 0, w], k_raw[0][:, w], f32(k_hi[:, 0, w]), ALU.subtract)\
                    .then_inc(k_split, 1)
            def statistics(i):
                nc.vector.bn_stats(k.stats[:, i, :], x[:, i, :]).then_inc(x_stats, 1)
                dve.wait_ge(x_stats, i + 1)
                nc.vector.bn_aggr(k.mv[:, 0, i, :], k.stats[:, i, :]).then_inc(x_mv, 1)
                dve.wait_ge(x_mv, i + 1)
                nc.vector.tensor_scalar(k.var[:, i:i + 1], k.mv[:, 0, i, 1:2], LN_EPS, None, ALU.add).then_inc(var_made, 1)

            def normalise(i):
                dve.wait_ge(rstd_made, i + 1)
                nc.vector.tensor_scalar(x[:, i, :], x[:, i, :], k.mv[:, 0, i, 0:1], k.rstd[:, i:i + 1],
                                        ALU.subtract, ALU.mult).then_inc(x2_made, 1)

            dve.wait_ge(first_inv, 1)
            nc.vector.tensor_scalar(q_rms[:], q_inv[:], X_SCALE, None, ALU.mult).then_inc(first_rms, 1)
            dve.wait_ge(first_rms, 1)
            for j in range(UT + 1):
                if j < UT:
                    shift(j, 0, j, 2 * j)
                if j > 0:
                    invert_sum(j - 1, 0, j - 1)

            def body(turn):
                i = turn.i
                for s in range(UNITS):
                    u, n = (s + 1) % UNITS, TILES * i + UT * (s + 1)
                    for what, a in turn.vector_order(s):
                        if what == "M":
                            shift(n + a, u, a, 2 * (a % 2))
                        elif what == "I":
                            invert_sum(n + a, u, a)
                        elif what == "T":
                            dve.wait_ge(pt_his, KTL * (UNITS * i + s) + a + 1)
                            nc.vector.tensor_tensor(pT_lo[:, a, :], bank[:, turn.bank[s, what, a], :],
                                                    f32(pT_hi[:, a, :]), ALU.subtract).then_inc(ring_out, 1)
                        elif what == "Q":
                            sum_squares(a, i + 1, turn.use[s, what, a], turn.bank[s, what, a])
                        elif what == "QT":
                            split_queries(a, i if s == 0 else i + 1, turn.bank[s, what, a])
                        elif what == "W":
                            add_output(a, turn.use[s, what, a], turn.bank[s, what, a])
                        elif what == "O":
                            dve.wait_ge(o_his, UNITS * i + s + 1)
                            g, rows = 2 * (s % 2), slice(s // 2 * S, (s // 2 + 1) * S)
                            nc.vector.tensor_tensor(oT_lo[:, g:g + 2, rows],
                                                    bank[:, 7, :].rearrange("p (g t) -> p g t", g=2),
                                                    f32(oT_hi[:, g:g + 2, rows]), ALU.subtract).then_inc(o_out, 1)
                    if s == 0 and not turn.first:
                        query_scales(1, i)
                    if s == 2 and turn.more:
                        query_scales(0, i + 1)
                if not turn.more:
                    dve.wait_ge(ring_out, turn.use[3, "W", 1] + 1)
                    statistics(0)
                    statistics(1)
                    normalise(0)
                    normalise(1)
                    for r in range(2):
                        add_output(2 + r, turn.end + r, last_banks[r])
                        dve.wait_ge(ring_out, turn.end + r + 1)
                        statistics(2 + r)

            turns(dve, body)

        @block.tensor
        def _(pe):
            def ring_free(use):
                pe.wait_ge(ring_out, use - RING + 1)

            def queries(tt, use, at):
                ring_free(use)
                for m in range(KT):
                    w = slice(tt * P, (tt + 1) * P)
                    last = three_passes(nc, bank[:, at, :], k.x1_hi[:, m, w], k.x1_lo[:, m, w],
                                        wq_hi[:, m, :], wq_lo[:, m, :], m == 0, m == KT - 1)
                last.then_inc(ring_full, 1)

            def transposed_queries(tt, i, use, at, first=False):
                if not first:
                    pe.wait_ge(q_out, TT * i + tt + 1 - TT)
                if not (first and use < RING):
                    ring_free(use)
                for g in range(GRP):
                    last = nc.tensor.transpose(bank[:, at, g * P:(g + 1) * P], q[:, tt, g * HD:(g + 1) * HD], ident[:])
                last.then_inc(ring_full, 1)

            def scores(n, u, j, at, early=False):
                g, tt = tile_of(u, j)
                b, w = u // 2, slice(tt * P, (tt + 1) * P)
                if not early:
                    pe.wait_ge(exp_made, n - 1)
                for a_hi, k_part, start, stop in ((qT_hi, k_hi, True, False), (qT_hi, k_lo, False, False),
                                                  (qT_lo, k_hi, False, True)):
                    for c in range(2):
                        last = nc.tensor.matmul(bank[:, at + c, 0:HALF], a_hi[:, g, w],
                                                k_part[:, b, c * HALF:(c + 1) * HALF], start=start, stop=stop)
                last.then_inc(s_full, 1)

            def output(tt, i, use, at):
                pe.wait_ge(o_out, UNITS * i + 2 * (tt // 2) + 2)
                w = slice(tt * P, (tt + 1) * P)
                ring_free(use)
                for g in range(GRP):
                    last = three_passes(nc, bank[:, at, :], oT_hi[:, g, w], oT_lo[:, g, w],
                                        wo_hi[:, g, :], wo_lo[:, g, :], g == 0, g == GRP - 1)
                last.then_inc(ring_full, 1)

            for tt in range(2):
                transposed_queries(tt, 0, tt, first_bank(tt), first=True)
            pe.wait_ge(ring_out, Turn.BEFORE)
            pe.wait_ge(k_split, 2)
            for j in range(UT):
                scores(j, 0, j, 2 * j, early=True)

            def body(turn):
                i = turn.i
                for s in range(UNITS):
                    u, b = (s + 1) % UNITS, s // 2
                    for what, a in turn.tensor_order(s):
                        use, at = turn.use.get((s, what, a)), turn.bank.get((s, what, a))
                        if what == "S":
                            if a == 0 and s == 1:
                                pe.wait_ge(k_split, PIECE * i + 4)
                                pe.wait_ge(ring_out, turn.use[0, "QT", 3] + 1)
                            if a == 0 and s == 3:
                                pe.wait_ge(k_split, PIECE * i + 6)
                                pe.wait_ge(ring_out, turn.use[2, "QT", 1] + 1)
                            scores(TILES * i + UT * (s + 1) + a, u, a, 2 * (a % 2))
                        elif what == "T":
                            if not (turn.first and use < RING):
                                ring_free(use)
                            for j in range(UT):
                                if a == 0 and turn.first and s == 0 and j == 0:
                                    pe.wait_ge(prob_made, UT)
                                elif a == 0:
                                    pe.wait_ge(prob_made, TILES * i + UT * s + j + 1)
                                last = nc.tensor.transpose(bank[:, at, j * P:(j + 1) * P],
                                                           prob[:, UT * (s % 2) + j, a * P:(a + 1) * P], ident[:])
                            last.then_inc(ring_full, 1)
                        elif what == "O":
                            if a == 0:
                                if not (turn.first and s == 0):
                                    pe.wait_ge(o_out, UNITS * i + s)
                                pe.wait_ge(v_split, PIECE * i + 2 * b + 2)
                            pe.wait_ge(ring_out, turn.use[s, "T", a] + 1)
                            w = slice(a * HD, (a + 1) * HD)
                            last = three_passes(nc, bank[:, 7, :], v_hi[:, b, w], v_lo[:, b, w],
                                                pT_hi[:, a, :], pT_lo[:, a, :], a == 0, a == KTL - 1)
                            if a == KTL - 1:
                                last.then_inc(o_full, 1)
                        elif what == "Q":
                            if a == 0:
                                pe.wait_ge(wq_split, PIECE * i + PIECE)
                            queries(a, use, at)
                        elif what == "QT":
                            transposed_queries(a, i if s == 0 else i + 1, use, at, turn.first and s == 0)
                        elif what == "W" and s < 2:
                            output(a, i - 1, use, at)
                        elif what == "W":
                            if a == 0:
                                pe.wait_ge(wo_split, PIECE * i + PIECE)
                            output(a, i, use, at)
                if not turn.more:
                    for r in range(2):
                        output(2 + r, i, turn.end + r, last_banks[r])

            turns(pe, body)


AHEAD = 2
UP_AHEAD = 3


def feed_forward(nc, d, k):
    with ExitStack() as ctx:
        t = Tensors(nc, ctx)
        up = t.sb("up_w", [P, FH // HPT, FM])
        up_hi = t.sb("up_hi", [P, FH // HPT, FM], F32R)
        up_lo = t.sb("up_lo", [P, FH // HPT, FM], F32R)
        down = t.sb("down_w", [P, FH // HPT, HPT, FD])
        down_hi = t.sb("down_hi", [P, FH // HPT, HPT, HPT, FD], F32R)
        down_lo = t.sb("down_lo", [P, FH // HPT, HPT, HPT, FD], F32R)
        xT_hi = t.sb("x2T_hi", [P, KT, TOK], F32R)
        xT_lo = t.sb("x2T_lo", [P, KT, TOK], F32R)
        tT_hi = t.sb("tT_hi", [P, KT, TOK], F32R)
        tT_lo = t.sb("tT_lo", [P, KT, TOK], F32R)
        hid = t.sb("hid", [P, HPT, TOK])
        hid_hi = t.sb("hid_hi", [P, HPT, TOK], F32R)
        hid_lo = t.sb("hid_lo", [P, HPT, TOK], F32R)
        yT_hi = t.sb("yT_hi", [P, KT, TOK], F32R)
        yT_lo = t.sb("yT_lo", [P, KT, TOK], F32R)
        zeros = t.sb("zeros", [P, FH * P // 4])
        x, bank, ident, gather, scatter = k.x, k.bank, k.ident, k.gather, k.scatter

        up_in, down_in, out_stored = t.sem("up_in"), t.sem("down_in"), t.sem("out_stored")
        zero_made, cleared = t.sem("zero_made"), t.sem("cleared")
        up_his, up_los, down_his, down_los = t.sem("up_his"), t.sem("up_los"), t.sem("down_his"), t.sem("down_los")
        y_sum, y_stats, y_mv = t.sem("y_sum2"), t.sem("y_stats2"), t.sem("y_mv2")
        var_made, rstd_made, ln_made = t.sem("var_made2"), t.sem("rstd_made2"), t.sem("ln_made2")
        x2_made = t.sem("x2_rest_made")
        xt_ps, xt_hi, xt_lo = t.sem("x2t_ps"), t.sem("x2t_hi"), t.sem("x2t_lo")
        t_ps, t_hi, t_lo = t.sem("t_ps"), t.sem("t_hi"), t.sem("t_lo")
        h_ps, h_out, h_hi, h_lo = t.sem("h_ps"), t.sem("h_out"), t.sem("h_hi"), t.sem("h_lo")
        y_ps, y_hi, y_lo, z_ps = t.sem("y_ps2"), t.sem("y_hi2"), t.sem("y_lo2"), t.sem("z_ps")
        block = ctx.enter_context(nc.Block())

        def tokens(j):
            return slice(j * P, (j + 1) * P)

        @block.sync
        def _(sp):
            sp.dma_start(up[:], d["up"].rearrange("(t q) e m -> (q e) t m", q=HPT)).then_inc(up_in, 16)
            sp.dma_start(down[:].rearrange("p t q e -> p (t q) e"), d["down"].rearrange("h m e -> m h e"))\
                .then_inc(down_in, 16)
            for i in range(TT):
                sp.wait_ge(ln_made, i + 1)
                sp.dma_start(d["out"].rearrange("b s d -> (b s) d")[tokens(i), :], x[:, i, :])\
                    .then_inc(out_stored, 16)
            sp.wait_ge(out_stored, 16 * TT)

        @block.gpsimd
        def _(pool):
            nc.gpsimd.memset(zeros[:], 0.0).then_inc(zero_made, 1)
            pool.wait_ge(up_in, 16)
            nc.gpsimd.tensor_scalar(up_hi[:], up[:], 1.0, 1.0, ALU.mult, ALU.mult).then_inc(up_his, 1)
            pool.wait_ge(up_his, 1)
            nc.gpsimd.tensor_tensor(up_lo[:], up[:], f32(up_hi[:]), ALU.subtract).then_inc(up_los, 1)
            pool.wait_ge(zero_made, 1)
            for i in range(FH // HPT):
                for blocks in (down_hi, down_lo):
                    nc.gpsimd.tensor_scalar(blocks[:, i, :, :, :].rearrange("p q r e -> p (q r e)"), zeros[:], 1.0, 1.0,
                                            ALU.mult, ALU.mult).then_inc(cleared, 1)
            pool.wait_ge(cleared, 2 * FH // HPT)
            pool.wait_ge(down_in, 16)
            for r in range(HPT):
                nc.gpsimd.tensor_scalar(down_hi[:, :, r, r, :], down[:, :, r, :], 1.0, 1.0, ALU.mult, ALU.mult)\
                    .then_inc(down_his, 1)
            for r in range(HPT):
                pool.wait_ge(down_his, r + 1)
                nc.gpsimd.tensor_tensor(down_lo[:, :, r, r, :], down[:, :, r, :], f32(down_hi[:, :, r, r, :]), ALU.subtract)\
                    .then_inc(down_los, 1)
            for i in range(TT):
                pool.wait_ge(var_made, i + 1)
                nc.gpsimd.tensor_tensor(k.rstd[:, TT + i:TT + i + 1], k.var[:, TT + i:TT + i + 1], k.minus_half[:, 0:1], ALU.pow)\
                    .then_inc(rstd_made, 1)

        @block.scalar
        def _(act):
            for j in range(TT):
                act.wait_ge(xt_ps, j + 1)
                nc.scalar.activation(xT_hi[:, :, tokens(j)], bank[:, j, :].rearrange("p (k t) -> p k t", k=KT), ACT.Copy)\
                    .then_inc(xt_hi, 1)

            def permuted_hi(i):
                act.wait_ge(t_ps, i + 1)
                nc.scalar.activation(tT_hi[:, i, :], bank[:, 4 + i, :], ACT.Copy).then_inc(t_hi, 1)

            def result_hi(i):
                act.wait_ge(y_ps, i + 1)
                nc.scalar.activation(yT_hi[:, i, :], bank[:, 4 + i, :], ACT.Copy).then_inc(y_hi, 1)

            for i in range(AHEAD):
                permuted_hi(i)
            for h in range(FH):
                act.wait_ge(h_ps, h + 1)
                nc.scalar.activation(hid[:, h % HPT, :], bank[:, h % HPT, :], ACT.Gelu).then_inc(h_out, 1)
                act.wait_ge(h_out, h + 1)
                nc.scalar.activation(hid_hi[:, h % HPT, :], hid[:, h % HPT, :], ACT.Copy).then_inc(h_hi, 1)
                if h + AHEAD < KT:
                    permuted_hi(h + AHEAD)
                if h > HPT and h % HPT == 3:
                    result_hi(h // HPT - 1)
            result_hi(KT - 1)

        @block.vector
        def _(dve):
            def statistics(i):
                nc.vector.bn_stats(k.stats[:, i, :], x[:, i, :]).then_inc(y_stats, 1)
                dve.wait_ge(y_stats, i + 1)
                nc.vector.bn_aggr(k.mv[:, 1, i, :], k.stats[:, i, :]).then_inc(y_mv, 1)
                dve.wait_ge(y_mv, i + 1)
                nc.vector.tensor_scalar(k.var[:, TT + i:TT + i + 1], k.mv[:, 1, i, 1:2], LN_EPS, None, ALU.add)\
                    .then_inc(var_made, 1)

            def normalise(i):
                dve.wait_ge(rstd_made, i + 1)
                nc.vector.tensor_scalar(x[:, i, :], x[:, i, :], k.mv[:, 1, i, 0:1], k.rstd[:, TT + i:TT + i + 1],
                                        ALU.subtract, ALU.mult).then_inc(ln_made, 1)

            for i in (2, 3):
                nc.vector.tensor_scalar(x[:, i, :], x[:, i, :], k.mv[:, 0, i, 0:1], k.rstd[:, i:i + 1],
                                        ALU.subtract, ALU.mult).then_inc(x2_made, 1)
            for j in range(TT):
                dve.wait_ge(xt_hi, j + 1)
                nc.vector.tensor_tensor(xT_lo[:, :, tokens(j)], bank[:, j, :].rearrange("p (k t) -> p k t", k=KT),
                                        f32(xT_hi[:, :, tokens(j)]), ALU.subtract).then_inc(xt_lo, 1)

            def permuted_lo(i):
                dve.wait_ge(t_hi, i + 1)
                nc.vector.tensor_tensor(tT_lo[:, i, :], bank[:, 4 + i, :], f32(tT_hi[:, i, :]), ALU.subtract).then_inc(t_lo, 1)

            def result_lo(i):
                dve.wait_ge(y_hi, i + 1)
                nc.vector.tensor_tensor(yT_lo[:, i, :], bank[:, 4 + i, :], f32(yT_hi[:, i, :]), ALU.subtract).then_inc(y_lo, 1)

            for i in range(AHEAD):
                permuted_lo(i)
            for h in range(FH):
                dve.wait_ge(h_hi, h + 1)
                nc.vector.tensor_tensor(hid_lo[:, h % HPT, :], hid[:, h % HPT, :], f32(hid_hi[:, h % HPT, :]), ALU.subtract)\
                    .then_inc(h_lo, 1)
                if h + AHEAD < KT:
                    permuted_lo(h + AHEAD)
                if h > HPT and h % HPT == 3:
                    result_lo(h // HPT - 1)
            result_lo(KT - 1)
            for i in range(TT):
                dve.wait_ge(z_ps, i + 1)
                nc.vector.tensor_tensor(x[:, i, :], bank[:, i, :], x[:, i, :], ALU.add).then_inc(y_sum, 1)
                dve.wait_ge(y_sum, i + 1)
                statistics(i)
                if i > 0:
                    normalise(i - 1)
            normalise(TT - 1)

        @block.tensor
        def _(pe):
            for j in range(TT):
                if j >= 2:
                    pe.wait_ge(x2_made, j - 1)
                for i in range(KT):
                    last = nc.tensor.transpose(bank[:, j, tokens(i)], x[:, j, i * P:(i + 1) * P], ident[:])
                last.then_inc(xt_ps, 1)

            def permute(i, b):
                w = slice(b * S, (b + 1) * S)
                for j in range(KT):
                    nc.tensor.matmul(bank[:, 4 + i, w], gather[:, j, tokens(i)], xT_hi[:, j, w], start=j == 0, stop=False)
                    last = nc.tensor.matmul(bank[:, 4 + i, w], gather[:, j, tokens(i)], xT_lo[:, j, w], start=False,
                                            stop=j == KT - 1)
                if b == B - 1:
                    last.then_inc(t_ps, 1)

            def up_product(h):
                i, r = h // HPT, slice(FD * (h % HPT), FD * (h % HPT + 1))
                pe.wait_ge(t_lo, i + 1)
                if h >= HPT:
                    pe.wait_ge(h_out, h - HPT + 1)
                three_passes(nc, bank[:, h % HPT, :], up_hi[r, i, :], up_lo[r, i, :], tT_hi[r, i, :], tT_lo[r, i, :],
                             True, True).then_inc(h_ps, 1)

            def down_product(h):
                i, r = h // HPT, h % HPT
                if h == 0:
                    pe.wait_ge(down_los, HPT)
                if r == 0:
                    pe.wait_ge(t_lo, i + 1)
                pe.wait_ge(h_lo, h + 1)
                last = three_passes(nc, bank[:, 4 + i, :], down_hi[:, i, r, :, :].rearrange("p q e -> p (q e)"),
                                    down_lo[:, i, r, :, :].rearrange("p q e -> p (q e)"),
                                    hid_hi[:, r, :], hid_lo[:, r, :], r == 0, r == HPT - 1)
                if r == HPT - 1:
                    last.then_inc(y_ps, 1)

            for b in range(B):
                pe.wait_ge(xt_lo, S // P * (b + 1))
                if b == B - 1:
                    pe.wait_ge(up_los, 1)
                for i in range(KT):
                    permute(i, b)
                    if b == B - 1 and i >= AHEAD - 1 and i - AHEAD + 1 < UP_AHEAD:
                        up_product(i - AHEAD + 1)
            for h in range(FH):
                if h + UP_AHEAD < FH:
                    up_product(h + UP_AHEAD)
                down_product(h)
            for j in range(TT):
                w = slice(j * P, (j + 1) * P)
                for i in range(KT):
                    if j == 0:
                        pe.wait_ge(y_lo, i + 1)
                    nc.tensor.matmul(bank[:, j, :], yT_hi[:, i, w], scatter[:, i, :], start=i == 0, stop=False)
                    last = nc.tensor.matmul(bank[:, j, :], yT_lo[:, i, w], scatter[:, i, :], start=False,
                                            stop=i == KT - 1)
                last.then_inc(z_ps, 1)


class Kept:
    pass


def build(nc, d):
    with ExitStack() as ctx:
        t = Tensors(nc, ctx)
        k = Kept()
        k.x = t.sb("x_rows", [P, TT, D])
        k.x1_hi = t.sb("x1_hi", [P, KT, TOK], F32R)
        k.x1_lo = t.sb("x1_lo", [P, KT, TOK], F32R)
        k.wq_raw = t.sb("wq_raw", [P, KT, D])
        k.wq_hi = t.sb("wq_hi", [P, KT, D], F32R)
        k.wq_lo = t.sb("wq_lo", [P, KT, D], F32R)
        k.q = t.sb("q_rows", [P, TT, D])
        k.q_sq = t.sb("q_sq", [P, TT, D])
        k.k_raw0 = t.sb("xk_raw0", [P, KEYS])
        k.k_in = [t.sem("xk_in0"), t.sem("xk_in1")]
        k.q_ss = t.sb("q_ss", [P, TT * GRP])
        k.q_ms = t.sb("q_ms", [P, TT * GRP])
        k.q_inv = t.sb("q_inv", [P, TT * GRP])
        k.q_rms = t.sb("q_rms", [P, TT * GRP])
        k.minus_half = t.sb("minus_half", [P, TT * GRP])
        k.stats = t.sb("stats", [P, TT, 6])
        k.mv = t.sb("mv", [P, 2, TT, 2])
        k.var = t.sb("var", [P, 2 * TT])
        k.rstd = t.sb("rstd", [P, 2 * TT])
        k.gather = k.wq_hi
        k.scatter = k.wq_lo
        k.ident = t.sb("ident", [P, P])
        k.bank = ctx.enter_context(nc.psum_tensor("bank", [P, 8, 512], F32))
        k.kT_dram = nc.dram_tensor("kT_by_head", [KVH, HD, B * KEYS], F32, kind="Internal").ap()
        k.v_dram = nc.dram_tensor("v_by_head", [KVH, P, B * KEYS], F32, kind="Internal").ap()
        self_attention_and_keys(nc, d, k)
        cross_attention(nc, d, k)
        feed_forward(nc, d, k)


_INS = {"x": "x", "ctx": "ctx_4096", "w_attn": "L0_attn_w_attn", "b_attn": "L0_attn_b_attn",
        "w_proj": "L0_attn_w_proj", "b_proj": "L0_attn_b_proj", "Wq": "L0_xattn_Wq", "Wk": "L0_xattn_Wk",
        "Wv": "L0_xattn_Wv", "Wo": "L0_xattn_Wo", "q_norm": "L0_xattn_q_norm_w", "k_norm": "L0_xattn_k_norm_w",
        "up": "L0_ffn_up", "down": "L0_ffn_down", "perm": "L0_ffn_perm"}


def kernel(**inputs):
    import numpy as np
    import concourse.bacc as bacc
    from concourse.bass_utils import run_bass_kernel_spmd

    nc = bacc.Bacc("TRN2", target_bir_lowering=False, num_devices=1)
    arrays, d = {}, {}
    for name, given in _INS.items():
        a = np.ascontiguousarray(inputs[given])
        arrays[f"in_{name}"] = a
        d[name] = nc.dram_tensor(f"in_{name}", a.shape, mybir.dt.from_np(a.dtype), kind="ExternalInput").ap()
    d["out"] = nc.dram_tensor("out", (B, S, D), F32, kind="ExternalOutput").ap()
    build(nc, d)
    return run_bass_kernel_spmd(nc, [arrays], core_ids=[0]).results[0]["out"]
```
